# Optimizing a Trainium2 kernel written in Bass

```python
import numpy as np
import jax
import jax.numpy as jnp

def _softmax(x, axis=-1):
    return jax.nn.softmax(x, axis=axis)

def _gelu(x):
    return jax.nn.gelu(x, approximate=True)

def _silu(x):
    return jax.nn.silu(x)

def _sigmoid(x):
    return jax.nn.sigmoid(x)

def _layernorm(x, axis=-1, eps=1e-05):
    m = jnp.mean(x, axis=axis, keepdims=True)
    v = jnp.var(x, axis=axis, keepdims=True)
    return (x - m) / jnp.sqrt(v + eps)

def _scatter_add(tgt, idx, src, axis=0):
    return tgt.at[idx].add(src)

def _segment_sum(src, seg, n):
    return jax.ops.segment_sum(src, seg, n)
kernel_name = 'mk_flamingo_gated_d2_seqx_r4_698bb6'

def setup_inputs(seed: int=0):
    np.random.seed(seed)
    _w = jnp.asarray

    def _rec_inputs():
        import jax
        import jax.numpy as jnp
        _rk = jax.random.key(seed)
        x = -0.0002928 + 1 * jax.random.normal(jax.random.fold_in(_rk, 1), (128, 128, 256), jnp.float32)
        _lenS = 128 - jax.random.randint(jax.random.fold_in(_rk, 7), (128,), 0, max(1, 128 // 4) + 1, jnp.int32)
        _lenS2 = 128 - jax.random.randint(jax.random.fold_in(_rk, 8), (128,), 0, max(1, 128 // 4) + 1, jnp.int32)
        _ctx_1024P = jax.random.normal(jax.random.fold_in(_rk, 11), (128, 16, 256), jnp.float32)
        _ctx_1024c = jax.random.dirichlet(jax.random.fold_in(_rk, 511), 0.3 * jnp.ones((16,), jnp.float32), (128, 128))
        _ctx_1024t = jnp.einsum('bsk,bkd->bsd', _ctx_1024c, _ctx_1024P)
        _ctx_1024t = _ctx_1024t * jax.lax.rsqrt(jnp.mean(jnp.square(_ctx_1024t)) + 1e-12) * 0.953939
        ctx_1024 = -1.39393e-06 + 0.999914 * (_ctx_1024t + 0.3 * jax.random.normal(jax.random.fold_in(_rk, 611), (128, 128, 256), jnp.float32))
        _validS = jnp.arange(128)[None, :] < _lenS[:, None]
        _validS2 = jnp.arange(128)[None, :] < _lenS2[:, None]
        _causal = jnp.tril(jnp.ones((128, 128), dtype=bool))
        mask_Bx1xSxS2_ik1 = jnp.where(jnp.broadcast_to(_validS2[:, None, None, :], (128, 1, 128, 128)), 1, 0).astype(jnp.int32)
        mask_BxS2_ik0 = jnp.where(jnp.broadcast_to(_validS2[:, :], (128, 128)), 0, 1).astype(jnp.int32)
        _g = jax.random.normal(jax.random.fold_in(_rk, 9001), (2, 2), jnp.float32)
        _g = jnp.sign(_g) * jnp.maximum(jnp.abs(_g), 1.0) + (_g == 0) * 1.0
        g_xattn = _g[0]
        g_ffn = _g[1]
        return (x, ctx_1024, mask_Bx1xSxS2_ik1, mask_BxS2_ik0, g_xattn, g_ffn)
    x, ctx_1024, mask_Bx1xSxS2_ik1, mask_BxS2_ik0, g_xattn, g_ffn = _rec_inputs()

    def _L0_xattn_setup():
        import jax, jax.numpy as jnp
        import numpy as np
        B, N, C, H = (2, 512, 256, 16)
        HD = C // H
        key = jax.random.key(seed)
        kq, kk, kv, km = jax.random.split(key, 4)
        q = jax.random.normal(kq, (B, N, C), dtype=jnp.float32)
        k = jax.random.normal(kk, (B, N, C), dtype=jnp.float32)
        v = jax.random.normal(kv, (B, N, C), dtype=jnp.float32)
        mask = jax.random.randint(km, (B, 1, N, N), 0, 2, dtype=jnp.int32)
        return {'q': q, 'k': k, 'v': v, 'mask': mask}
    _L0_xattn_all = _L0_xattn_setup()
    _L0_xattn_in = {k: v for k, v in _L0_xattn_all.items() if k in ()}
    del _L0_xattn_all

    def _L0_ffn_setup():
        import jax, jax.numpy as jnp
        import numpy as np
        B, T, D, E, H = (8, 512, 256, 8, 64)
        LN_EPS = 1e-05
        key = jax.random.key(seed)
        ks = jax.random.split(key, 4)
        return {'x': jax.random.normal(ks[0], (B, T, D), dtype=jnp.float32), 'Wg': jax.random.normal(ks[1], (E, D), dtype=jnp.float32) * 0.02, 'ln_scale': jnp.ones((E, D), dtype=jnp.float32), 'ln_bias': jnp.zeros((E, D), dtype=jnp.float32), 'W1': jax.random.normal(ks[2], (E, D, H), dtype=jnp.float32) * 0.02, 'b1': jnp.zeros((E, H), dtype=jnp.float32), 'W2': jax.random.normal(ks[3], (E, H, D), dtype=jnp.float32) * 0.02, 'b2': jnp.zeros((E, D), dtype=jnp.float32)}
    _L0_ffn_all = _L0_ffn_setup()
    _L0_ffn_in = {k: v for k, v in _L0_ffn_all.items() if k in ('Wg', 'ln_scale', 'ln_bias', 'W1', 'b1', 'W2', 'b2')}
    del _L0_ffn_all

    def _L1_xattn_setup():
        import jax, jax.numpy as jnp
        import numpy as np
        B, LQ, LK, D = (4, 512, 512, 256)
        H = 16
        HD = D // H

        def _split_heads(x):
            b, l, _ = x.shape
            return x.reshape(b, l, H, HD).transpose(0, 2, 1, 3)
        key = jax.random.key(seed)
        ks = jax.random.split(key, 10)
        s = 0.02
        return {'hidden_states': jax.random.normal(ks[0], (B, LQ, D), jnp.float32), 'context': jax.random.normal(ks[1], (B, LK, D), jnp.float32), 'attention_mask': jax.random.randint(ks[2], (B, LK), 0, 2, jnp.int32), 'q_w': jax.random.normal(ks[3], (D, D), jnp.float32) * s, 'q_b': jnp.zeros((D,), jnp.float32), 'k_w': jax.random.normal(ks[4], (D, D), jnp.float32) * s, 'k_b': jnp.zeros((D,), jnp.float32), 'v_w': jax.random.normal(ks[5], (D, D), jnp.float32) * s, 'v_b': jnp.zeros((D,), jnp.float32)}
    _L1_xattn_all = _L1_xattn_setup()
    _L1_xattn_in = {k: v for k, v in _L1_xattn_all.items() if k in ('q_w', 'q_b', 'k_w', 'k_b', 'v_w', 'v_b')}
    del _L1_xattn_all

    def _L1_ffn_setup():
        import jax, jax.numpy as jnp
        import numpy as np
        D_MODEL = 256
        H_SHARED = 512
        H_ROUTED = 256
        N_EXPERTS = 8
        TOP_K = 2
        key = jax.random.key(seed)
        ks = jax.random.split(key, 8)
        B, T = (2, 512)
        sc_d = 1.0 / np.sqrt(D_MODEL)
        sc_hs = 1.0 / np.sqrt(H_SHARED)
        sc_hr = 1.0 / np.sqrt(H_ROUTED)
        return {'x': jax.random.normal(ks[0], (B, T, D_MODEL), dtype=jnp.float32), 'router_w': jax.random.normal(ks[1], (N_EXPERTS, D_MODEL), dtype=jnp.float32) * sc_d, 'router_bias': jnp.zeros((N_EXPERTS,), dtype=jnp.float32), 'sw1': jax.random.normal(ks[2], (D_MODEL, H_SHARED), dtype=jnp.float32) * sc_d, 'sw3': jax.random.normal(ks[3], (D_MODEL, H_SHARED), dtype=jnp.float32) * sc_d, 'sw2': jax.random.normal(ks[4], (H_SHARED, D_MODEL), dtype=jnp.float32) * sc_hs, 'ew1': jax.random.normal(ks[5], (N_EXPERTS, D_MODEL, H_ROUTED), dtype=jnp.float32) * sc_d, 'ew2': jax.random.normal(ks[6], (N_EXPERTS, H_ROUTED, D_MODEL), dtype=jnp.float32) * sc_hr}
    _L1_ffn_all = _L1_ffn_setup()
    _L1_ffn_in = {k: v for k, v in _L1_ffn_all.items() if k in ('router_w', 'router_bias', 'sw1', 'sw3', 'sw2', 'ew1', 'ew2')}
    del _L1_ffn_all
    return {'x': x, 'ctx_1024': ctx_1024, 'mask_Bx1xSxS2_ik1': mask_Bx1xSxS2_ik1, 'mask_BxS2_ik0': mask_BxS2_ik0, 'g_xattn': g_xattn, 'g_ffn': g_ffn, 'L0_ffn_Wg': _L0_ffn_in['Wg'], 'L0_ffn_ln_scale': _L0_ffn_in['ln_scale'], 'L0_ffn_ln_bias': _L0_ffn_in['ln_bias'], 'L0_ffn_W1': _L0_ffn_in['W1'], 'L0_ffn_b1': _L0_ffn_in['b1'], 'L0_ffn_W2': _L0_ffn_in['W2'], 'L0_ffn_b2': _L0_ffn_in['b2'], 'L1_xattn_q_w': _L1_xattn_in['q_w'], 'L1_xattn_q_b': _L1_xattn_in['q_b'], 'L1_xattn_k_w': _L1_xattn_in['k_w'], 'L1_xattn_k_b': _L1_xattn_in['k_b'], 'L1_xattn_v_w': _L1_xattn_in['v_w'], 'L1_xattn_v_b': _L1_xattn_in['v_b'], 'L1_ffn_router_w': _L1_ffn_in['router_w'], 'L1_ffn_router_bias': _L1_ffn_in['router_bias'], 'L1_ffn_sw1': _L1_ffn_in['sw1'], 'L1_ffn_sw3': _L1_ffn_in['sw3'], 'L1_ffn_sw2': _L1_ffn_in['sw2'], 'L1_ffn_ew1': _L1_ffn_in['ew1'], 'L1_ffn_ew2': _L1_ffn_in['ew2']}

def reference(x, ctx_1024, mask_Bx1xSxS2_ik1, mask_BxS2_ik0, g_xattn, g_ffn, L0_ffn_Wg, L0_ffn_ln_scale, L0_ffn_ln_bias, L0_ffn_W1, L0_ffn_b1, L0_ffn_W2, L0_ffn_b2, L1_xattn_q_w, L1_xattn_q_b, L1_xattn_k_w, L1_xattn_k_b, L1_xattn_v_w, L1_xattn_v_b, L1_ffn_router_w, L1_ffn_router_bias, L1_ffn_sw1, L1_ffn_sw3, L1_ffn_sw2, L1_ffn_ew1, L1_ffn_ew2):
    import jax
    import jax.numpy as jnp

    def _L0_xattn_ref(q, k, v, mask):
        import jax, jax.numpy as jnp
        import numpy as np
        B, N, C, H = (2, 512, 256, 16)
        HD = C // H
        b, n, c = q.shape
        qh = q.reshape(b, n, H, HD).transpose(0, 2, 1, 3)
        kh = k.reshape(b, n, H, HD).transpose(0, 2, 1, 3)
        vh = v.reshape(b, n, H, HD).transpose(0, 2, 1, 3)
        scale = 1.0 / jnp.sqrt(jnp.float32(HD))
        scores = jnp.einsum('bhqd,bhkd->bhqk', qh, kh) * scale
        scores = jnp.where(mask == 0, jnp.float32(-1000000000.0), scores)
        probs = jax.nn.softmax(scores, axis=-1)
        atten = jnp.einsum('bhqk,bhkd->bhqd', probs, vh)
        return atten.transpose(0, 2, 1, 3).reshape(b, n, c)

    def _L0_ffn_ref(x, Wg, ln_scale, ln_bias, W1, b1, W2, b2):
        import jax, jax.numpy as jnp
        import numpy as np
        B, T, D, E, H = (8, 512, 256, 8, 64)
        LN_EPS = 1e-05
        Bs, Ts, Ds = x.shape
        xt = x.reshape(Bs * Ts, Ds)
        logits = xt @ Wg.T
        top1 = jnp.argmax(logits, axis=-1)
        mu = jnp.mean(xt, axis=-1, keepdims=True)
        var = jnp.mean(jnp.square(xt - mu), axis=-1, keepdims=True)
        xhat = (xt - mu) * jax.lax.rsqrt(var + LN_EPS)
        n_experts = Wg.shape[0]

        def body(y, p):
            s_e, b_e, w1, bb1, w2, bb2, eid = p
            h = jax.nn.gelu((xhat * s_e + b_e) @ w1 + bb1, approximate=False)
            out = h @ w2 + bb2
            mask = (top1 == eid)[:, None].astype(out.dtype)
            return (y + mask * out, None)
        y0 = jnp.zeros_like(xt)
        y, _ = jax.lax.scan(body, y0, (ln_scale, ln_bias, W1, b1, W2, b2, jnp.arange(n_experts)))
        return y.reshape(Bs, Ts, Ds)

    def _L1_xattn_ref(hidden_states, context, attention_mask, q_w, q_b, k_w, k_b, v_w, v_b):
        import jax, jax.numpy as jnp
        import numpy as np
        B, LQ, LK, D = (4, 512, 512, 256)
        H = 16
        HD = D // H

        def _split_heads(x):
            b, l, _ = x.shape
            return x.reshape(b, l, H, HD).transpose(0, 2, 1, 3)
        q = _split_heads(hidden_states @ q_w.T + q_b)
        k = _split_heads(context @ k_w.T + k_b)
        v = _split_heads(context @ v_w.T + v_b)
        scores = jnp.einsum('bhqd,bhkd->bhqk', q, k) / jnp.sqrt(jnp.float32(HD))
        mask = (attention_mask > 0)[:, None, None, :]
        scores = jnp.where(mask, -jnp.inf, scores)
        probs = jax.nn.softmax(scores, axis=-1)
        ctx = jnp.einsum('bhqk,bhkd->bhqd', probs, v)
        ctx = ctx.transpose(0, 2, 1, 3).reshape(ctx.shape[0], ctx.shape[2], H * HD)
        return ctx

    def _L1_ffn_ref(x, router_w, router_bias, sw1, sw3, sw2, ew1, ew2):
        import jax, jax.numpy as jnp
        import numpy as np
        D_MODEL = 256
        H_SHARED = 512
        H_ROUTED = 256
        N_EXPERTS = 8
        TOP_K = 2
        B, T, C = x.shape
        xf = x.reshape(-1, C)
        shared_out = jax.nn.silu(xf @ sw1) * (xf @ sw3) @ sw2
        s = jax.nn.sigmoid((xf @ router_w.T).astype(jnp.float32))
        sel_scores = s + router_bias.astype(jnp.float32)
        _, topk_idx = jax.lax.top_k(sel_scores, TOP_K)
        s_sel = jnp.take_along_axis(s, topk_idx, axis=1)
        denom = s_sel.sum(axis=1, keepdims=True)
        gates = jnp.where(denom > 1e-09, s_sel / (denom + 1e-09), 1.0 / TOP_K).astype(x.dtype)
        one_hot = jax.nn.one_hot(topk_idx, N_EXPERTS, dtype=x.dtype)
        comb = jnp.einsum('nke,nk->ne', one_hot, gates)
        h = jax.nn.gelu(jnp.einsum('nd,edh->neh', xf, ew1), approximate=False)
        y = jnp.einsum('neh,ehd->ned', h, ew2)
        routed_out = jnp.einsum('ned,ne->nd', y, comb)
        return (shared_out + routed_out).reshape(B, T, C)
    x = x + jnp.tanh(g_xattn[0]) * _L0_xattn_ref(_layernorm(x, axis=-1), ctx_1024, ctx_1024, mask_Bx1xSxS2_ik1)
    x = x + jnp.tanh(g_ffn[0]) * _L0_ffn_ref(_layernorm(x, axis=-1), L0_ffn_Wg, L0_ffn_ln_scale, L0_ffn_ln_bias, L0_ffn_W1, L0_ffn_b1, L0_ffn_W2, L0_ffn_b2)
    x = x + jnp.tanh(g_xattn[1]) * _L1_xattn_ref(_layernorm(x, axis=-1), ctx_1024, mask_BxS2_ik0, L1_xattn_q_w, L1_xattn_q_b, L1_xattn_k_w, L1_xattn_k_b, L1_xattn_v_w, L1_xattn_v_b)
    x = x + jnp.tanh(g_ffn[1]) * _L1_ffn_ref(_layernorm(x, axis=-1), L1_ffn_router_w, L1_ffn_router_bias, L1_ffn_sw1, L1_ffn_sw3, L1_ffn_sw2, L1_ffn_ew1, L1_ffn_ew2)
    return x

_drawn_inputs = setup_inputs


def setup_inputs(seed=0):
    import zlib

    import numpy as np

    out = dict(_drawn_inputs(seed))
    spreads = {'g_ffn': (-1.0, 0.2),
     'L0_ffn_ln_scale': (1.0, 0.6),
     'L0_ffn_ln_bias': (0.0, 0.767),
     'L0_ffn_b1': (0.0, 0.385),
     'L0_ffn_b2': (0.0, 0.1),
     'L1_xattn_q_b': (0.0, 0.762),
     'L1_xattn_k_b': (0.0, 0.8),
     'L1_xattn_v_b': (0.0, 0.1),
     'L1_ffn_router_bias': (0.0, 0.1)}
    factors = {'L1_xattn_q_w': 3.44, 'L1_xattn_k_w': 3.288}
    for name, (base, spread) in spreads.items():
        noise = np.random.default_rng([zlib.crc32(name.encode()), seed]).standard_normal(out[name].shape)
        drawn = base * np.exp(spread * noise) if base else spread * noise
        out[name] = jnp.asarray(drawn.astype(out[name].dtype))
    for name, factor in factors.items():
        out[name] = (out[name] * factor).astype(out[name].dtype)
    return out
```

```python
from contextlib import ExitStack

import concourse.bass as bass
from concourse import mybir

F32 = mybir.dt.float32
F16 = mybir.dt.float16
BF16 = mybir.dt.bfloat16
I32 = mybir.dt.int32
U32 = mybir.dt.uint32
ALU = mybir.AluOpType
ACT = mybir.ActivationFunctionType
AX = mybir.AxisListType.X

P = 128
D = 256
KT = D // P
SEQS = 4
TOK = SEQS * P
HEADS = 16
HD = D // HEADS
VW = HD + 1
E = 8
HT0 = 4
HTS = 4
HTR = 16
HT = HT0 + HTS + HTR
RING = 3
UNITS = 2 * SEQS

LN_EPS = 1e-5
S_X = 2.0 ** 11
S_W = 2.0 ** 8
S_XW = S_X * S_W
S_WW = S_W * S_W
S_P = 2.0 ** 8
MASKED = 120000.0
OFF_EXPERT = 2.0 ** 15


class Signal:

    def __init__(self, sem, events, step=1):
        self.sem, self.events, self.step, self.turn = sem, list(events), step, 0

    def by(self, event):
        assert self.events[self.turn % len(self.events)] == event, (self.events[self.turn % len(self.events)], event)
        self.turn += 1
        return self.sem

    def at(self, i, event):
        return i * (len(self.events) * self.step) + (self.events.index(event) + 1) * self.step

    def before(self, i):
        return i * (len(self.events) * self.step)


class Chain:

    def __init__(self, eng, sem, per_group, first=0):
        self.eng, self.sem, self.per_group, self.done, self.i = eng, sem, per_group, first, None
        self.first = first

    def link(self, ins):
        ins.then_inc(self.sem, 1)
        self.done += 1
        if self.i is None:
            self.eng.wait_ge(self.sem, self.done)
        else:
            self.eng.wait_ge(self.sem, self.i * self.per_group + self.done)


W_COLS = {}
_at = 0
for _name, _n in (("q_w", KT * D), ("k_w", KT * D), ("v_w", KT * D), ("W1", KT * HT0 * P), ("W2", HT0 * D),
                  ("Wg", KT * E), ("router_w", KT * E), ("sw1", KT * HTS * P), ("sw3", KT * HTS * P),
                  ("sw2", HTS * D), ("ew1", KT * HTR * P), ("ew2", HTR * D)):
    W_COLS[_name] = (_at, _n)
    _at += _n
W_TOTAL = _at
CHUNKS = [("q_w", "k_w", "v_w", "W1", "W2", "Wg", "router_w"), ("sw1", "sw3", "sw2"), ("ew1",), ("ew2",)]
STAGE = 4096
DVE_SETUP, DVE_LINKS = 19, 67
POOL_LINKS = 10


def build(nc, a, out):
    seqs = a["x"].shape[0]
    groups = seqs // SEQS
    assert a["x"].shape == (seqs, P, D) and seqs % SEQS == 0

    with ExitStack() as ctx:
        def sb(name, shape, dt):
            return ctx.enter_context(nc.sbuf_tensor(name, shape, dt))

        def sem(name):
            return ctx.enter_context(nc.semaphore(name))

        def signal(name, events, step=1):
            return Signal(sem(name), events, step)

        WH = sb("WH", [P, W_TOTAL], F16)
        WL = sb("WL", [P, W_TOTAL], F16)
        attn_arena = sb("attn_arena", [P, STAGE], F32)
        hid_arena = sb("hid_arena", [P, 3 * RING * TOK], F32)
        stage = [attn_arena, hid_arena]
        P32 = attn_arena[:, 0:2048].rearrange("p (b n) -> p b n", b=2)
        PH = attn_arena[:, 2048:3072].bitcast(F16).rearrange("p (b n) -> p b n", b=2)
        PL = attn_arena[:, 3072:4096].bitcast(F16).rearrange("p (b n) -> p b n", b=2)
        R = RING * TOK
        h32 = hid_arena[:, 0:R].rearrange("p (b n) -> p b n", b=RING)
        v32 = hid_arena[:, R:2 * R].rearrange("p (b n) -> p b n", b=RING)
        HH = hid_arena[:, 2 * R:2 * R + R // 2].bitcast(F16).rearrange("p (b n) -> p b n", b=RING)
        HL = hid_arena[:, 2 * R + R // 2:3 * R].bitcast(F16).rearrange("p (b n) -> p b n", b=RING)

        x_in = sb("x_in", [P, SEQS, D], F32)
        x = sb("x_res", [P, SEQS, D], F32)
        x_out = sb("x_out", [P, SEQS, D], F32)
        ctx_in = sb("ctx_in", [P, SEQS, D], F32)
        m_in = [sb(f"mask{l}_in", [P, SEQS, P], I32) for l in range(2)]
        off = sb("off", [P, SEQS, P], F32)
        n_off = sb("n_off", [P, 2, SEQS], F32)
        some_on = sb("some_on", [P, 2, SEQS], F32)
        take_off = sb("take_off", [P, 2, SEQS], F32)
        nan_row = sb("nan_row", [P, SEQS], F32)
        maskb = [sb(f"mask_bias{l}", [P, SEQS, P], BF16) for l in range(2)]
        xn = sb("xn", [P, SEQS, D], F32)
        XT = [sb(f"XT_{h}", [P, KT, TOK], F16) for h in "hl"]
        CT = [sb(f"CT_{h}", [P, KT, TOK], F16) for h in "hl"]
        K1 = [sb(f"K1_{h}", [P, KT, TOK], F16) for h in "hl"]
        Q = [sb(f"Q_{h}", [P, KT, 2, TOK], F16) for h in "hl"]
        V = [[sb(f"V{l}_{h}", [P, SEQS * HEADS, VW], F16) for h in "hl"] for l in range(2)]
        stats = sb("stats", [P, SEQS, 6], F32)
        mv = sb("mv", [P, 4, SEQS, 2], F32)
        rstd = sb("rstd", [P, 4, SEQS], F32)
        ptmp = sb("ptmp", [P, 3, SEQS], F32)
        negmax = sb("negmax", [P, 2, 8], BF16)
        mT = sb("mT", [P, 2, P], BF16)
        rden = sb("rden", [P, HEADS], F32)
        att = sb("att", [P, D], F32)
        lg = sb("lg", [P, SEQS, E], F32)
        top8 = sb("top8", [P, SEQS, 8], F32)
        topi = sb("topi", [P, SEQS, 8], U32)
        topf = sb("topf", [P, SEQS, 8], F32)
        oh = sb("oh", [P, SEQS, E], F32)
        oh2 = sb("oh2", [P, SEQS, E], F32)
        sig = sb("sig", [P, SEQS, E], F32)
        den = sb("den", [P, 5, SEQS], F32)
        idle = sb("idle", [P, 1], F32)
        tokens = sb("tokens", [P, SEQS, 32], F16)
        tokT = sb("tokT", [32, TOK], F16)

        id32 = sb("id32", [P, P], F32)
        id16 = sb("id16", [P, P], F16)
        idb = sb("idb", [P, P], BF16)
        pick = sb("pick", [P, 8, P], BF16)
        gate_pick = sb("gate_pick", [16, E, P], F16)
        expert_of = sb("expert_of", [32, E, 64], F16)
        iota8 = sb("iota8", [P, E], F32)
        iota8i = sb("iota8i", [P, E], I32)
        pi = sb("pi", [P, 4], I32)
        pf = sb("pf", [P, 4], F32)
        half = sb("half", [P, 2, 2], F32)
        c_eps = sb("c_eps", [P, SEQS], F32)
        c_mhalf = sb("c_mhalf", [P, SEQS], F32)
        lnP = sb("lnP", [P, 1], F32)
        ones_q = sb("ones_q", [2, TOK], F16)
        ones_kv = sb("ones_kv", [2, TOK], F16)
        gates4 = sb("gates4", [P, 4], F32)
        tg = sb("tg", [P, 4], F32)
        ln_s = sb("ln_s", [P, KT, E], F32)
        ln_b = sb("ln_b", [P, KT, E], F32)
        b1 = sb("b1", [P, HT0], F32)
        b1e = sb("b1e", [P, HT0], F32)
        b2f = sb("b2f", [32, D], F32)
        b2h = sb("b2h", [32, D], F16)
        b2 = sb("b2", [32, D], F16)
        bf = sb("bf", [2, 3, D], F32)
        bh = sb("bh", [2, 3, D], F16)
        qkv_b = sb("qkv_b", [2, 3, D], F16)
        rb = sb("rb", [P, E], F32)

        ps = ctx.enter_context(nc.psum_tensor("ps", [P, 8, 512], F32))
        G_BANKS = 4

        def view_scores(b, n=1):
            return ps[:, b, :].rearrange("p (t e q) -> p t e q", t=KT, e=2)

        O = ps[:, 6, 0:HEADS * VW].rearrange("p (h w) -> p h w", h=HEADS)
        maxT = ps[0:8, 7, 0:64].bitcast(BF16)
        tokTp = ps[0:32, 6, 0:256].bitcast(F16)
        lgp = ps[:, 7, 0:SEQS * E]

        def y(s):
            return ps[:, 4 + s // 2, (s % 2) * D:(s % 2 + 1) * D]

        w_loaded = [sem(f"w_loaded{c}") for c in range(len(CHUNKS))]
        small_loaded = sem("small_loaded")
        consts_made = sem("consts_made")
        const_step = sem("const_step")
        b1_ready = sem("b1_ready")
        w1_scaled = sem("w1_scaled")
        w_high = sem("w_high")
        w_low = sem("w_low")
        tg_ready = sem("tg_ready")
        setup_done = sem("setup_done")
        dve_step = sem("dve_step")
        pool_step = sem("pool_step")

        x_loaded = signal("x_loaded", ["x"], 16)
        ctx_loaded = signal("ctx_loaded", ["ctx"], 16)
        m_loaded = [signal(f"mask{l}_loaded", ["m"], 16) for l in range(2)]
        out_stored = signal("out_stored", ["out"], 16)

        evac = ["v0", "ct0", "ct1", "qa0", "qa1", "xb0", "xb1", "k0", "k1", "va", "vb", "xc0", "xc1", "qc0", "qc1",
                "xd0", "xd1"]
        hi = signal("hi_made", evac)
        lo = signal("lo_made", evac)
        units = [(l, u) for l in range(2) for u in range(UNITS)]
        s_ready = signal("s_ready", units)
        max_done = signal("max_done", units)
        t_ready = signal("t_ready", units)
        mt_ready = signal("mt_ready", units)
        st_ready = signal("st_ready", units)
        exp_done = signal("exp_done", [(l, u, k) for l, u in units for k in range(2)])
        plo_done = signal("plo_done", units)
        av_done = signal("av_done", units)
        resid = signal("resid", [(f, s) for f in "abcd" for s in range(SEQS)])
        stats_ready = signal("stats_ready", "abcd")
        rstd_ready = signal("rstd_ready", "abcd")
        xn_ready = signal("xn_ready", [(f, s) for f in "abcd" for s in range(SEQS)])
        ct_ready = signal("ct_ready", range(KT))
        xt_ready = signal("xt_ready", [(f, t) for f in "abcd" for t in range(KT)])
        masks_made = signal("masks_made", range(2))
        lg_ready = signal("lg_ready", "bd")
        lg_tanh = signal("lg_tanh", "d")
        tok_ready = signal("tok_ready", "bd")
        tokp_ready = signal("tokp_ready", "bd")
        tokT_ready = signal("tokT_ready", "bd")
        proj_ready = signal("proj_ready", ["k0", "k1", "va", "vb", "q0", "q1"])
        g1_ready = signal("g1_ready", range(HT))
        act_done = signal("act_done", range(HT))
        bc_ready = signal("bc_ready", range(E))
        prod_done = signal("prod_done", range(HT0, HT))
        hid_hi = signal("hid_hi", range(HT))
        hid_lo = signal("hid_lo", range(HT))
        g2_done = signal("g2_done", range(HT))

        def w(part, name, t, lo_, n, m=P):
            base, size = W_COLS[name]
            per = {"q_w": D, "k_w": D, "v_w": D, "W1": HT0 * P, "W2": D, "Wg": E, "router_w": E, "sw1": HTS * P,
                   "sw3": HTS * P, "sw2": D, "ew1": HTR * P, "ew2": D}[name]
            c = base + t * per + lo_
            return (WH, WL)[part][0:m, c:c + n]

        PARTS = ((0, 0), (0, 1), (1, 0))

        xg = a["x"].rearrange("(g s) t d -> g t s d", s=SEQS)
        og = out.rearrange("(g s) t d -> g t s d", s=SEQS)
        cg = a["ctx"].rearrange("(g s) t d -> g t s d", s=SEQS)
        m0g = a["mask0"].rearrange("(g s) o q k -> g q (s o) k", s=SEQS)
        m1g = a["mask1"].rearrange("(g s) k -> g s k", s=SEQS)

        block = ctx.enter_context(nc.Block())

        @block.sync
        def _(sp):
            def load(i):
                sp.dma_start(ctx_in[:, :, :], cg[i]).then_inc(ctx_loaded.sem, 16)
                sp.dma_start(x_in[:, :, :], xg[i]).then_inc(x_loaded.sem, 16)
                sp.dma_start(m_in[0][:, :, :], m0g[i]).then_inc(m_loaded[0].sem, 16)
                sp.dma_start(m_in[1][:, :, :], m1g[i].partition_broadcast(P)).then_inc(m_loaded[1].sem, 16)

            smalls = [(ln_s[:, :, :], a["ln_s"].rearrange("(t p) e -> p t e", p=P)),
                      (ln_b[:, :, :], a["ln_b"].rearrange("(t p) e -> p t e", p=P)),
                      (b1[:, :], a["b1"]),
                      (rb[:, :], a["router_b"].partition_broadcast(P)),
                      (b2f[0:8, :], a["b2"]), (b2f[8:16, :], a["b2"])]
            smalls += [(gates4[:, 2 * j:2 * j + 2], a["g"][j].partition_broadcast(P)) for j in range(2)]
            for j, name in enumerate(("q_b", "k_b", "v_b")):
                src = a[name].rearrange("(o d) -> o d", o=1)
                smalls += [(bf[0:1, j, :], src), (bf[1:2, j, :], src)]
            sp.wait_ge(consts_made, 1)
            for dst, src in smalls:
                sp.dma_start(dst, src).then_inc(small_loaded, 16)
            for c, names in enumerate(CHUNKS):
                if c >= 2:
                    sp.wait_ge(w_high, c - 1)
                    sp.wait_ge(w_low, c - 1)
                at = 0
                for name in names:
                    n = W_COLS[name][1]
                    rows = a[name].shape[0] // P
                    src = a[name].rearrange("(t p) n -> p t n", p=P)
                    dst = stage[c % 2][:, at:at + n].rearrange("p (t n) -> p t n", t=rows)
                    sp.dma_start(dst, src).then_inc(w_loaded[c], 16)
                    at += n
                if c == 1:
                    load(0)
            with sp.Fori(0, groups - 1) as i:
                sp.wait_ge(lo.sem, lo.at(i, "v0"))
                sp.wait_ge(ct_ready.sem, ct_ready.at(i, 1))
                sp.wait_ge(masks_made.sem, masks_made.at(i, 1))
                sp.wait_ge(resid.sem, resid.at(i, ("a", SEQS - 1)))
                load(i + 1)
                sp.wait_ge(resid.sem, resid.at(i, ("d", SEQS - 1)))
                sp.dma_start(og[i], x_out[:, :, :]).then_inc(out_stored.sem, 16)
            sp.wait_ge(resid.sem, resid.at(groups - 1, ("d", SEQS - 1)))
            sp.dma_start(og[groups - 1], x_out[:, :, :]).then_inc(out_stored.sem, 16)
            sp.wait_ge(out_stored.sem, out_stored.before(groups + 1))

        @block.gpsimd
        def _(pool):
            pool.memset(b2f[:, :], 0.0).then_inc(consts_made, 1)
            steps = 0
            zeroed = [(id32, 0.0), (id16, 0.0), (idb, 0.0), (pick, 0.0), (gate_pick, 0.0), (expert_of, 0.0)]
            for t, v in zeroed:
                pool.memset(t[tuple(slice(None) for _ in t.shape)], v).then_inc(const_step, 1)
                steps += 1
            for t, v in ((c_eps, LN_EPS), (c_mhalf, -0.5), (ones_q, S_X), (ones_kv, S_W)):
                pool.memset(t[:, :], v).then_inc(consts_made, 1)
            pool.memset(mT[:, :, :], 0.0).then_inc(consts_made, 1)
            pool.memset(x_out[:, 0, 0:1], 0.0).then_inc(out_stored.sem, 16)
            pool.memset(tokens[:, :, :], 0.0).then_inc(consts_made, 1)
            for l in range(2):
                for h in range(2):
                    pool.memset(V[l][h][:, :, HD:VW], (S_W, 0.0)[h]).then_inc(consts_made, 1)
            pool.wait_ge(const_step, steps)
            for t in (id32, id16, idb):
                pool.affine_select(out=t[:, :], in_=t[:, :], compare_op=ALU.not_equal, fill=1.0, base=0,
                                   pattern=[[-1, P]], channel_multiplier=1).then_inc(consts_made, 1)
            pool.affine_select(out=pick[:, :, :], in_=pick[:, :, :], compare_op=ALU.not_equal, fill=1.0, base=0,
                               pattern=[[-1, 8], [0, P]], channel_multiplier=1).then_inc(consts_made, 1)
            pool.affine_select(out=gate_pick[:, :, :], in_=gate_pick[:, :, :], compare_op=ALU.not_equal, fill=1.0,
                               base=0, pattern=[[-1, E], [0, P]], channel_multiplier=1).then_inc(const_step, 1)
            pool.affine_select(out=expert_of[:, :, :], in_=expert_of[:, :, :], compare_op=ALU.not_equal,
                               fill=OFF_EXPERT, base=-16, pattern=[[-1, E], [0, 64]],
                               channel_multiplier=1).then_inc(consts_made, 1)
            pool.wait_ge(const_step, steps + 1)
            pool.affine_select(out=gate_pick[:, :, :], in_=gate_pick[:, :, :], compare_op=ALU.not_equal, fill=1.0,
                               base=-E, pattern=[[-1, E], [0, P]], channel_multiplier=1).then_inc(consts_made, 1)
            pool.iota(iota8i[:, :], pattern=[[1, E]], base=0, channel_multiplier=0).then_inc(consts_made, 1)
            pool.iota(pi[:, 0:1], pattern=[[0, 1]], base=0, channel_multiplier=1).then_inc(consts_made, 1)

            chain = Chain(pool, pool_step, POOL_LINKS)
            with pool.Fori(0, groups) as i:
                chain.i, chain.done = i, 0
                for f, ph in enumerate("abcd"):
                    var, r = mv[:, f, :, 1], rstd[:, f, :]
                    pool.wait_ge(stats_ready.sem, stats_ready.at(i, ph))
                    chain.link(pool.tensor_tensor(ptmp[:, 0, :], var, c_eps[:, :], ALU.add))
                    if ph == "a":
                        chain.link(pool.tensor_tensor(ptmp[:, 1, :], ptmp[:, 0, :], c_mhalf[:, :], ALU.pow))
                        pool.wait_ge(masks_made.sem, masks_made.at(i, 0))
                        pool.tensor_tensor(r, ptmp[:, 1, :], some_on[:, 0, :], ALU.mult)\
                            .then_inc(rstd_ready.by(ph), 1)
                    elif ph == "b":
                        chain.link(pool.tensor_tensor(ptmp[:, 1, :], ptmp[:, 0, :], c_mhalf[:, :], ALU.pow))
                        chain.link(pool.tensor_tensor(ptmp[:, 2, :], ptmp[:, 1, :], var, ALU.mult))
                        chain.link(pool.tensor_tensor(ptmp[:, 0, :], ptmp[:, 2, :], ptmp[:, 1, :], ALU.mult))
                        chain.link(pool.tensor_tensor(ptmp[:, 2, :], ptmp[:, 0, :], c_eps[:, :], ALU.add))
                        chain.link(pool.tensor_tensor(ptmp[:, 0, :], ptmp[:, 2, :], c_mhalf[:, :], ALU.pow))
                        pool.tensor_tensor(r, ptmp[:, 0, :], ptmp[:, 1, :], ALU.mult)\
                            .then_inc(rstd_ready.by(ph), 1)
                    else:
                        pool.tensor_tensor(r, ptmp[:, 0, :], c_mhalf[:, :], ALU.pow)\
                            .then_inc(rstd_ready.by(ph), 1)
                assert chain.done == POOL_LINKS, f"POOL_LINKS {chain.done}"

        N_CONSTS = 1 + 4 + 1 + 1 + 4 + 3 + 1 + 1 + 1 + 2

        @block.tensor
        def _(pe):
            pe.wait_ge(consts_made, N_CONSTS)
            pe.wait_ge(small_loaded, 16 * 14)
            pe.wait_ge(w_loaded[0], 16 * len(CHUNKS[0]))
            at = W_COLS["W1"][0]
            for t in range(HT0):
                for k in range(KT):
                    c = at + k * HT0 * P + t * P
                    mm = pe.matmul(ps[:, 0, t * E:(t + 1) * E], stage[0][:, c:c + P], ln_b[:, k, :],
                                   start=(t == 0 and k == 0), stop=(k == KT - 1), skip_group_check=True)
            mm.then_inc(b1_ready, 1)
            pe.wait_ge(setup_done, 1)

            def turn(i, f):
                for t in range(KT):
                    for s in range(SEQS):
                        if t == 0:
                            pe.wait_ge(xn_ready.sem, xn_ready.at(i, (f, s)))
                        mm = pe.transpose(ps[:, t, s * P:(s + 1) * P], xn[:, s, t * P:(t + 1) * P], id32[:, :])
                    mm.then_inc(xt_ready.by((f, t)), 1)

            def attention(i, l):
                keys = CT if l == 0 else K1
                B = maskb[l]
                for u in range(UNITS + 2):
                    if u < UNITS:
                        s, j = divmod(u, 2)
                        tok = slice(s * P, (s + 1) * P)
                        if u:
                            pe.wait_ge(max_done.sem, max_done.at(i, (l, u - 1)))
                        for b in range(2):
                            pe.matmul(ps[:, 4 + b, :].rearrange("p (n k) -> p n k", n=4), idb[:, :],
                                      B[:, s:s + 1, :].to_broadcast([P, 4, P]), start=True, stop=False,
                                      skip_group_check=True)
                        for t in range(KT):
                            for e in range(2):
                                for b in range(2):
                                    r = slice(32 * (2 * j + b), 32 * (2 * j + b) + 32)
                                    mm = pe.matmul(view_scores(4 + b)[:, t, e, :], Q[0][r, t, e, tok],
                                                   keys[0][r, t, tok], start=False, stop=True,
                                                   skip_group_check=True)
                        mm.then_inc(s_ready.by((l, u)), 1)
                    if 1 <= u <= UNITS:
                        v = u - 1
                        s, j = divmod(v, 2)
                        tok = slice(s * P, (s + 1) * P)
                        pe.wait_ge(mt_ready.sem, mt_ready.at(i, (l, v)))
                        if v >= 2:
                            pe.wait_ge(exp_done.sem, exp_done.at(i, (l, v - 2, 1)))
                        for b in range(2):
                            bank = 2 * j + b
                            pe.matmul(ps[:, bank, :].rearrange("p (n q) -> p n q", n=4), B[:, s, :],
                                      idb[:, :].unsqueeze(1).to_broadcast([P, 4, P]), start=True, stop=False,
                                      skip_group_check=True)
                            for c in range(4):
                                pe.matmul(view_scores(bank)[:, c // 2, c % 2, :], pick[:, 4 * b + c, :],
                                          mT[:, v % 2, :], start=False, stop=False, skip_group_check=True)
                        for t in range(KT):
                            for n, (pk, pq) in enumerate(PARTS):
                                for b in range(2):
                                    r = slice(32 * (2 * j + b), 32 * (2 * j + b) + 32)
                                    mm = pe.matmul(view_scores(2 * j + b)[:, t, :, :], keys[pk][r, t, tok],
                                                   Q[pq][r, t, :, tok], start=False, stop=(n == 2),
                                                   skip_group_check=True)
                        mm.then_inc(st_ready.by((l, v)), 1)
                    if u < UNITS:
                        pe.wait_ge(max_done.sem, max_done.at(i, (l, u)))
                        if u:
                            pe.wait_ge(mt_ready.sem, mt_ready.at(i, (l, u - 1)))
                        pe.transpose(maxT, negmax[:, u % 2, :], idb[:, :]).then_inc(t_ready.by((l, u)), 1)
                    if u >= 2:
                        v = u - 2
                        s, j = divmod(v, 2)
                        pe.wait_ge(plo_done.sem, plo_done.at(i, (l, v)))
                        if j == 0 and s:
                            pe.wait_ge(resid.sem, resid.at(i, ("ac"[l], s - 1)))
                        for b in range(2):
                            for t in range(KT):
                                for e in range(2):
                                    c = b * 4 + t * 2 + e
                                    h = 8 * t + 2 * (2 * j + b) + e
                                    for n, (pp, pv) in enumerate(PARTS):
                                        prob = (PH, PL)[pp][:, v % 2, c * P:(c + 1) * P]
                                        mm = pe.matmul(O[:, h, :], prob, V[l][pv][:, s * HEADS + h, :],
                                                       start=(j == 0 and c == 0 and n == 0), stop=(n == 2),
                                                       skip_group_check=True)
                        mm.then_inc(av_done.by((l, v)), 1)

            def wide(bank, name, m, src, bias=None, ones=None, stop=True):
                out_ = ps[:, bank, :]
                n = 0
                for k in range(KT):
                    for pw, px in PARTS:
                        mm = pe.matmul(out_, w(pw, name, k, m * P, P), src[px][:, k, :], start=(n == 0),
                                       stop=(stop and bias is None and n == 3 * KT - 1), skip_group_check=True)
                        n += 1
                if bias is not None:
                    mm = pe.matmul(out_, bias, ones, start=False, stop=True, skip_group_check=True)
                return mm

            def logits(i, ph, name):
                for s in range(SEQS):
                    n = 0
                    for k in range(KT):
                        for px, pw in PARTS:
                            mm = pe.matmul(lgp[:, s * E:(s + 1) * E], XT[px][:, k, s * P:(s + 1) * P],
                                           w(pw, name, k, 0, E), start=(s == 0 and n == 0),
                                           stop=(n == 3 * KT - 1), skip_group_check=True)
                            n += 1
                mm.then_inc(lg_ready.by(ph), 1)

            def turn_tokens(i, ph):
                pe.wait_ge(tok_ready.sem, tok_ready.at(i, ph))
                for s in range(SEQS):
                    mm = pe.transpose(tokTp[:, s * P:(s + 1) * P], tokens[:, s, :], id16[:, :])
                mm.then_inc(tokp_ready.by(ph), 1)

            def second(i, n, name, t, first, last):
                pe.wait_ge(hid_lo.sem, hid_lo.at(i, n))
                r = n % RING
                for s in range(SEQS):
                    tok = slice(s * P, (s + 1) * P)
                    for m, (ph_, pw) in enumerate(PARTS):
                        mm = pe.matmul(y(s), (HH, HL)[ph_][:, r, tok], w(pw, name, t, 0, D),
                                       start=(first and m == 0 and s % 2 == 0), stop=(last and m == 2),
                                       skip_group_check=True)
                mm.then_inc(g2_done.by(n), 1)

            with pe.Fori(0, groups) as i:
                pe.wait_ge(ctx_loaded.sem, ctx_loaded.at(i, "ctx"))
                for t in range(KT):
                    for s in range(SEQS):
                        mm = pe.transpose(ps[:, 2 + t, s * P:(s + 1) * P], ctx_in[:, s, t * P:(t + 1) * P],
                                          id32[:, :])
                    mm.then_inc(ct_ready.by(t), 1)
                turn(i, "a")
                pe.wait_ge(lo.sem, lo.at(i, "qa1"))
                attention(i, 0)
                turn(i, "b")
                pe.wait_ge(lo.sem, lo.at(i, "xb1"))
                logits(i, "b", "Wg")
                for n in range(HT0):
                    wide(n, "W1", n, XT, stop=False)
                turn_tokens(i, "b")
                pe.wait_ge(tokT_ready.sem, tokT_ready.at(i, "b"))
                for n in range(HT0):
                    pe.matmul(ps[:, n, :], expert_of[:, 2 * n:2 * n + 2, :].rearrange("r e h -> r (e h)"),
                              tokT[:, :], start=False, stop=True, skip_group_check=True)\
                        .then_inc(g1_ready.by(n), 1)
                for n in range(HT0):
                    if n == HT0 - 1:
                        for s in range(SEQS):
                            pe.matmul(y(s), tokT[:, s * P:(s + 1) * P], b2[:, :], start=False, stop=False,
                                      skip_group_check=True)
                    second(i, n, "W2", n, n == 0, n == HT0 - 1)
                for m in range(2):
                    wide(2 + m, "k_w", m, CT, qkv_b[:, 1, m * P:(m + 1) * P], ones_kv[:, :])\
                        .then_inc(proj_ready.by(f"k{m}"), 1)
                pe.wait_ge(resid.sem, resid.at(i, ("b", SEQS - 1)))
                for s in range(SEQS):
                    n = 0
                    for k in range(KT):
                        for pc, pw in PARTS:
                            pe.matmul(y(s), CT[pc][:, k, s * P:(s + 1) * P], w(pw, "v_w", k, 0, D),
                                      start=(n == 0 and s % 2 == 0), stop=False, skip_group_check=True)
                            n += 1
                    mm = pe.matmul(y(s), ones_kv[:, 0:P], qkv_b[:, 2, :], start=False, stop=True,
                                   skip_group_check=True)
                    if s % 2:
                        mm.then_inc(proj_ready.by("v" + "ab"[s // 2]), 1)
                turn(i, "c")
                pe.wait_ge(lo.sem, lo.at(i, "xc1"))
                for m in range(2):
                    wide(6 + m, "q_w", m, XT, qkv_b[:, 0, m * P:(m + 1) * P], ones_q[:, :])\
                        .then_inc(proj_ready.by(f"q{m}"), 1)
                pe.wait_ge(lo.sem, lo.at(i, "qc1"))
                attention(i, 1)
                turn(i, "d")
                pe.wait_ge(lo.sem, lo.at(i, "xd1"))
                logits(i, "d", "router_w")
                for n in range(HT0, HT + 2):
                    if n < HT0 + HTS:
                        p = n - HT0
                        if p >= 2:
                            pe.wait_ge(prod_done.sem, prod_done.at(i, n - 2))
                        wide(2 * (p % 2), "sw1", p, XT)
                        wide(2 * (p % 2) + 1, "sw3", p, XT).then_inc(g1_ready.by(n), 1)
                    elif n < HT:
                        r = n - HT0 - HTS
                        if r == 0:
                            turn_tokens(i, "d")
                            pe.wait_ge(tokT_ready.sem, tokT_ready.at(i, "d"))
                        if r % 2 == 0:
                            e = r // 2
                            if e >= 2:
                                pe.wait_ge(prod_done.sem, prod_done.at(i, n - 3))
                            pe.matmul(ps[:, 7 - e % 2, :], gate_pick[:, e, :], tokT[0:16, :], start=True,
                                      stop=True).then_inc(bc_ready.by(e), 1)
                        if r < G_BANKS:
                            pe.wait_ge(prod_done.sem, prod_done.at(i, HT0 + 2 + r // 2))
                        else:
                            pe.wait_ge(act_done.sem, act_done.at(i, n - G_BANKS))
                        wide(r % G_BANKS, "ew1", r, XT).then_inc(g1_ready.by(n), 1)
                    m = n - 2
                    if HT0 <= m:
                        if m < HT0 + HTS:
                            second(i, m, "sw2", m - HT0, m == HT0, False)
                        else:
                            second(i, m, "ew2", m - HT0 - HTS, False, m == HT - 1)

        @block.scalar
        def _(act):
            act.wait_ge(small_loaded, 16 * 14)
            act.activation(tg[:, :], gates4[:, :], ACT.Tanh).then_inc(tg_ready, 1)
            for c, names in enumerate(CHUNKS):
                n = sum(W_COLS[x_][1] for x_ in names)
                base = W_COLS[names[0]][0]
                act.wait_ge(w_loaded[c], 16 * len(names))
                if c == 0:
                    act.wait_ge(w1_scaled, 1)
                act.activation(WH[:, base:base + n], stage[c % 2][:, 0:n], ACT.Copy, scale=S_W)\
                    .then_inc(w_high, 1)
            act.wait_ge(setup_done, 1)

            def high(ev, pairs, scale, func=ACT.Copy):
                for o_, i_ in pairs:
                    ins = act.activation(o_, i_, func, scale=scale)
                ins.then_inc(hi.by(ev), 1)

            def query_high(ev, l, t, bank):
                for e in range(2):
                    ins = act.activation(Q[0][:, t, e, :], ps[:, bank, :], ACT.Identity,
                                         scale=half[:, l, e:e + 1])
                ins.then_inc(hi.by(ev), 1)

            def attention(i, l):
                scale = 0.25 / (S_XW if l == 0 else S_WW)
                for v in range(UNITS):
                    j = v % 2
                    src = ps[:, 2 * j:2 * j + 2, :].rearrange("p b n -> p (b n)")
                    act.wait_ge(st_ready.sem, st_ready.at(i, (l, v)))
                    if v >= 2:
                        act.wait_ge(plo_done.sem, plo_done.at(i, (l, v - 2)))
                    act.activation(P32[:, j, :], src, ACT.Exp, bias=lnP[:, :], scale=scale)\
                        .then_inc(exp_done.by((l, v, 0)), 1)
                    if v >= 2:
                        act.wait_ge(av_done.sem, av_done.at(i, (l, v - 2)))
                    act.activation(PH[:, j, :], src, ACT.Exp, bias=lnP[:, :], scale=scale)\
                        .then_inc(exp_done.by((l, v, 1)), 1)

            def turned(i, f):
                for t in range(KT):
                    act.wait_ge(xt_ready.sem, xt_ready.at(i, (f, t)))
                    high(f"x{f}{t}", [(XT[0][:, t, :], ps[:, t, :])], S_X)

            def token_rows(i, ph):
                act.wait_ge(tokp_ready.sem, tokp_ready.at(i, ph))
                act.activation(tokT[:, :], tokTp[:, :], ACT.Copy).then_inc(tokT_ready.by(ph), 1)

            def hidden_high(i, n):
                if n >= RING:
                    act.wait_ge(g2_done.sem, g2_done.at(i, n - RING))
                if n < HT0:
                    src, scale = h32, S_W
                    act.wait_ge(act_done.sem, act_done.at(i, n))
                else:
                    src, scale = v32, (0.5 * S_W / (S_XW * S_XW) if n < HT0 + HTS else 1.0)
                    act.wait_ge(prod_done.sem, prod_done.at(i, n))
                act.activation(HH[:, n % RING, :], src[:, n % RING, :], ACT.Copy, scale=scale)\
                    .then_inc(hid_hi.by(n), 1)

            def hidden(i, n):
                act.wait_ge(g1_ready.sem, g1_ready.at(i, n))
                if n >= RING:
                    act.wait_ge(hid_lo.sem, hid_lo.at(i, n - RING))
                dst = h32[:, n % RING, :]
                if n < HT0:
                    ins = act.activation(dst, ps[:, n, :], ACT.Gelu, bias=b1e[:, n:n + 1], scale=1 / S_XW)
                elif n < HT0 + HTS:
                    ins = act.activation(dst, ps[:, 2 * (n % 2), :], ACT.Tanh, scale=0.5 / S_XW)
                else:
                    ins = act.activation(dst, ps[:, n % G_BANKS, :], ACT.Gelu, scale=1 / S_XW)
                ins.then_inc(act_done.by(n), 1)

            with act.Fori(0, groups) as i:
                act.wait_ge(ctx_loaded.sem, ctx_loaded.at(i, "ctx"))
                high("v0", [(V[0][0][:, :, 0:HD], ctx_in[:, :, :].rearrange("p s (h d) -> p (s h) d", d=HD))], S_W)
                for t in range(KT):
                    act.wait_ge(ct_ready.sem, ct_ready.at(i, t))
                    high(f"ct{t}", [(CT[0][:, t, :], ps[:, 2 + t, :])], S_W)
                for t in range(KT):
                    act.wait_ge(xt_ready.sem, xt_ready.at(i, ("a", t)))
                    query_high(f"qa{t}", 0, t, t)
                attention(i, 0)
                turned(i, "b")
                token_rows(i, "b")
                for n in range(HT0 + 1):
                    if n < HT0:
                        hidden(i, n)
                    if n:
                        hidden_high(i, n - 1)
                for m in range(2):
                    act.wait_ge(proj_ready.sem, proj_ready.at(i, f"k{m}"))
                    high(f"k{m}", [(K1[0][:, m, :], ps[:, 2 + m, :])], 1 / S_W)
                for m in range(2):
                    act.wait_ge(proj_ready.sem, proj_ready.at(i, "v" + "ab"[m]))
                    high("v" + "ab"[m], [(V[1][0][:, 32 * m:32 * m + 32, 0:HD],
                                          ps[:, 4 + m, :].rearrange("p (h d) -> p h d", d=HD))], 1 / S_W)
                turned(i, "c")
                for m in range(2):
                    act.wait_ge(proj_ready.sem, proj_ready.at(i, f"q{m}"))
                    query_high(f"qc{m}", 1, m, 6 + m)
                attention(i, 1)
                turned(i, "d")
                act.wait_ge(lg_ready.sem, lg_ready.at(i, "d"))
                act.activation(lg[:, :, :].rearrange("p s e -> p (s e)"), lgp, ACT.Tanh, scale=0.5 / S_XW)\
                    .then_inc(lg_tanh.by("d"), 1)
                for n in range(HT0, HT + 1):
                    if n == HT0 + HTS:
                        token_rows(i, "d")
                    if n < HT:
                        hidden(i, n)
                    if n > HT0:
                        hidden_high(i, n - 1)

        @block.vector
        def _(dve):
            chain = Chain(dve, dve_step, DVE_LINKS)
            link = chain.link
            dve.memset(lnP[:, :], 5.545177444479562)
            dve.wait_ge(consts_made, N_CONSTS)
            link(dve.tensor_copy(iota8[:, :], iota8i[:, :]))
            for c, shift in ((1, 4), (2, 3), (3, 0)):
                link(dve.tensor_scalar(pi[:, c:c + 1], pi[:, 0:1], shift, 1, ALU.logical_shift_right,
                                       ALU.bitwise_and))
            link(dve.tensor_copy(pf[:, :], pi[:, :]))
            for l, sc in enumerate((S_X, 1 / S_X)):
                link(dve.tensor_scalar(half[:, l, 0:1], pf[:, 1:2], -sc, sc, ALU.mult, ALU.add))
                link(dve.tensor_scalar(half[:, l, 1:2], pf[:, 1:2], sc, None, ALU.mult))
            link(dve.tensor_scalar(pf[:, 2:4], pf[:, 2:4], -1.0, None, ALU.mult))
            dve.wait_ge(small_loaded, 16 * 14)
            for f_, h_, o_, col, rows in ((b2f[:, :], b2h[:, :], b2[:, :], 2, 32),
                                          (bf[:, :, :].rearrange("p a d -> p (a d)"),
                                           bh[:, :, :].rearrange("p a d -> p (a d)"),
                                           qkv_b[:, :, :].rearrange("p a d -> p (a d)"), 3, 2)):
                link(dve.tensor_scalar(f_, f_, S_W, None, ALU.mult))
                link(dve.tensor_copy(h_, f_))
                link(dve.scalar_tensor_tensor(out=o_, in0=h_, scalar=pf[0:rows, col:col + 1], in1=f_,
                                              op0=ALU.mult, op1=ALU.add))
            dve.wait_ge(tg_ready, 1)
            for c in (1, 3):
                link(dve.tensor_scalar(tg[:, c:c + 1], tg[:, c:c + 1], 1 / S_WW, None, ALU.mult))
            dve.wait_ge(b1_ready, 1)
            for t in range(HT0):
                for h_ in range(2):
                    r = slice(64 * h_, 64 * h_ + 64)
                    ins = dve.tensor_tensor(b1e[r, t:t + 1], ps[r, 0, t * E + 2 * t + h_:t * E + 2 * t + h_ + 1],
                                            b1[r, t:t + 1], ALU.add)
                    if h_ and t == HT0 - 1:
                        link(ins)
            at = W_COLS["W1"][0]
            w1v = stage[0][:, at:at + KT * HT0 * P].rearrange("p (t e h) -> p t e h", t=KT, e=E)
            for t in range(KT):
                ins = dve.tensor_tensor(w1v[:, t, :, :], w1v[:, t, :, :],
                                        ln_s[:, t, :].unsqueeze(2).to_broadcast([P, E, 64]), ALU.mult)
            ins.then_inc(w1_scaled, 1)
            dve.wait_ge(w1_scaled, 1)
            for c, names in enumerate(CHUNKS):
                n = sum(W_COLS[x_][1] for x_ in names)
                base = W_COLS[names[0]][0]
                dve.wait_ge(w_high, c + 1)
                ins = dve.scalar_tensor_tensor(out=WL[:, base:base + n], in0=stage[c % 2][:, 0:n], scalar=S_W,
                                               in1=WH[:, base:base + n], op0=ALU.mult, op1=ALU.subtract)
                ins.then_inc(w_low, 1)
            dve.wait_ge(w_low, len(CHUNKS))
            setup = chain.done
            assert setup == DVE_SETUP, f"DVE_SETUP {setup}"
            dve.memset(idle[:, :], 0.0).then_inc(setup_done, 1)

            def low(ev, o_, src, scale, h_):
                dve.wait_ge(hi.sem, hi.at(chain.i, ev))
                dve.scalar_tensor_tensor(out=o_, in0=src, scalar=scale, in1=h_, op0=ALU.mult,
                                         op1=ALU.subtract).then_inc(lo.by(ev), 1)

            def query_low(ev, l, t, bank):
                dve.wait_ge(hi.sem, hi.at(chain.i, ev))
                for e in range(2):
                    ins = dve.scalar_tensor_tensor(out=Q[1][:, t, e, :], in0=ps[:, bank, :],
                                                   scalar=half[:, l, e:e + 1], in1=Q[0][:, t, e, :],
                                                   op0=ALU.mult, op1=ALU.subtract)
                ins.then_inc(lo.by(ev), 1)

            def carry_wait():
                dve.memset(idle[:, :], 0.0)

            def measure(i, f, seqs, src):
                for s in seqs:
                    ins = dve.bn_stats(stats[:, s, :], src[:, s, :])
                link(ins)

            def aggregate(i, f, seqs):
                for s in seqs:
                    ins = dve.bn_aggr(mv[:, f, s, :], stats[:, s, :])
                    if s == SEQS - 1:
                        ins.then_inc(stats_ready.by("abcd"[f]), 1)

            def normalise(i, f, src):
                ph = "abcd"[f]
                dve.wait_ge(rstd_ready.sem, rstd_ready.at(i, ph))
                for s in range(SEQS):
                    dve.tensor_scalar(xn[:, s, :], src[:, s, :], mv[:, f, s, 0:1], rstd[:, f, s:s + 1],
                                      ALU.subtract, ALU.mult).then_inc(xn_ready.by((ph, s)), 1)

            def masks(i, l):
                dve.wait_ge(m_loaded[l].sem, m_loaded[l].at(i, "m"))
                link(dve.tensor_scalar(off[:, :, :], m_in[l][:, :, :], 0.0, None,
                                       (ALU.is_equal, ALU.is_gt)[l]))
                link(dve.tensor_reduce(n_off[:, l, :], off[:, :, :], AX, ALU.add))
                link(dve.tensor_scalar(some_on[:, l, :], n_off[:, l, :], P - 0.5, None, ALU.is_lt))
                link(dve.tensor_scalar(take_off[:, l, :], some_on[:, l, :],
                                       -MASKED * (S_XW, S_WW)[l], None, ALU.mult))
                ins = dve.tensor_tensor(maskb[l][:, :, :], off[:, :, :],
                                        take_off[:, l, :].unsqueeze(2).to_broadcast([P, SEQS, P]), ALU.mult)
                if l == 0:
                    ins.then_inc(masks_made.by(0), 1)
                else:
                    link(dve.reciprocal(nan_row[:, :], some_on[:, 1, :]))
                    dve.tensor_tensor(nan_row[:, :], nan_row[:, :], some_on[:, 1, :], ALU.mult)\
                        .then_inc(masks_made.by(1), 1)
                dve.wait_ge(masks_made.sem, masks_made.at(i, l))

            def finish_sequence(i, l, s):
                ph = "ac"[l]
                src = (x_in, x)[l]
                dve.wait_ge(av_done.sem, av_done.at(i, (l, 2 * s + 1)))
                link(dve.reciprocal(rden[:, :], O[:, :, HD]))
                if l == 1:
                    link(dve.tensor_scalar(rden[:, :], rden[:, :], nan_row[:, s:s + 1], None, ALU.mult))
                link(dve.tensor_tensor(att[:, :].rearrange("p (h d) -> p h d", d=HD), O[:, :, 0:HD],
                                       rden[:, :].unsqueeze(2).to_broadcast([P, HEADS, HD]), ALU.mult))
                dve.scalar_tensor_tensor(out=x[:, s, :], in0=att[:, :], scalar=tg[:, 2 * l:2 * l + 1],
                                         in1=src[:, s, :], op0=ALU.mult, op1=ALU.add)\
                    .then_inc(resid.by((ph, s)), 1)
                dve.wait_ge(resid.sem, resid.at(i, (ph, s)))
                measure(i, 2 * l + 1, [s], x)

            def attention(i, l):
                for u in range(UNITS + 3):
                    if u < UNITS:
                        dve.wait_ge(s_ready.sem, s_ready.at(i, (l, u)))
                        dve.tensor_reduce(negmax[:, u % 2, :],
                                          ps[:, 4:6, :].rearrange("p b (c k) -> p (b c) k", c=4), AX, ALU.max,
                                          negate=True).then_inc(max_done.by((l, u)), 1)
                    if u >= 4 and u % 2 == 0:
                        finish_sequence(i, l, u // 2 - 2)
                    if u < UNITS:
                        dve.wait_ge(t_ready.sem, t_ready.at(i, (l, u)))
                        dve.tensor_copy(mT[0:8, u % 2, :], maxT).then_inc(mt_ready.by((l, u)), 1)
                    if 1 <= u <= UNITS:
                        v = u - 1
                        if v >= 2:
                            dve.wait_ge(av_done.sem, av_done.at(i, (l, v - 2)))
                        dve.wait_ge(exp_done.sem, exp_done.at(i, (l, v, 1)))
                        dve.tensor_tensor(PL[:, v % 2, :], P32[:, v % 2, :], PH[:, v % 2, :], ALU.subtract)\
                            .then_inc(plo_done.by((l, v)), 1)
                    if u >= 4 and u % 2 == 0:
                        if u > UNITS:
                            carry_wait()
                        aggregate(i, 2 * l + 1, [u // 2 - 2])

            def choose(values):
                carry_wait()
                for s in range(SEQS):
                    ins = dve.max(top8[:, s, :], values[:, s, :])
                link(ins)
                carry_wait()
                for s in range(SEQS):
                    ins = dve.max_index(topi[:, s, :], top8[:, s, :], values[:, s, :])
                link(ins)
                link(dve.tensor_copy(topf[:, :, :], topi[:, :, :]))

            def one_hot(dst, k):
                return dve.tensor_tensor(dst[:, :, :], iota8[:, :].unsqueeze(1).to_broadcast([P, SEQS, E]),
                                         topf[:, :, k:k + 1].to_broadcast([P, SEQS, E]), ALU.is_equal)

            def top1_rows(i):
                dve.wait_ge(lg_ready.sem, lg_ready.at(i, "b"))
                link(dve.tensor_copy(lg[:, :, :].rearrange("p s e -> p (s e)"), lgp))
                choose(lg)
                link(one_hot(oh, 0))
                dve.tensor_scalar(tokens[:, :, 0:8], oh[:, :, :], S_W, None, ALU.mult)
                dve.tensor_scalar(tokens[:, :, 8:16], oh[:, :, :], S_W, None, ALU.mult)
                dve.tensor_scalar(tokens[:, :, 16:24], oh[:, :, :], 1.0, OFF_EXPERT, ALU.subtract, ALU.mult)\
                    .then_inc(tok_ready.by("b"), 1)

            def gate_rows(i):
                dve.wait_ge(lg_tanh.sem, lg_tanh.at(i, "d"))
                link(dve.tensor_scalar(sig[:, :, :], lg[:, :, :], 0.5, 0.5, ALU.mult, ALU.add))
                link(dve.tensor_tensor(oh2[:, :, :], sig[:, :, :],
                                       rb[:, :].unsqueeze(1).to_broadcast([P, SEQS, E]), ALU.add))
                choose(oh2)
                link(one_hot(oh, 0))
                link(one_hot(oh2, 1))
                link(dve.tensor_tensor(oh[:, :, :], oh[:, :, :], oh2[:, :, :], ALU.add))
                link(dve.tensor_tensor(sig[:, :, :], sig[:, :, :], oh[:, :, :], ALU.mult))
                link(dve.tensor_reduce(den[:, 0, :], sig[:, :, :], AX, ALU.add))
                link(dve.tensor_scalar(den[:, 1, :], den[:, 0, :], 1e-9, None, ALU.add))
                link(dve.reciprocal(den[:, 2, :], den[:, 1, :]))
                link(dve.tensor_scalar(den[:, 3, :], den[:, 0, :], 1e-9, None, ALU.is_gt))
                link(dve.tensor_tensor(den[:, 2, :], den[:, 2, :], den[:, 3, :], ALU.mult))
                link(dve.tensor_scalar(den[:, 4, :], den[:, 3, :], -0.5, 0.5, ALU.mult, ALU.add))
                link(dve.tensor_tensor(sig[:, :, :], sig[:, :, :],
                                       den[:, 2, :].unsqueeze(2).to_broadcast([P, SEQS, E]), ALU.mult))
                link(dve.tensor_tensor(oh[:, :, :], oh[:, :, :],
                                       den[:, 4, :].unsqueeze(2).to_broadcast([P, SEQS, E]), ALU.mult))
                link(dve.tensor_tensor(sig[:, :, :], sig[:, :, :], oh[:, :, :], ALU.add))
                link(dve.tensor_scalar(tokens[:, :, 0:8], sig[:, :, :], S_W, None, ALU.mult))
                dve.scalar_tensor_tensor(out=tokens[:, :, 8:16], in0=sig[:, :, :], scalar=S_W,
                                         in1=tokens[:, :, 0:8], op0=ALU.mult, op1=ALU.subtract)\
                    .then_inc(tok_ready.by("d"), 1)

            def hidden_low(i, n):
                dve.wait_ge(hid_hi.sem, hid_hi.at(i, n))
                r = n % RING
                src, scale = (h32, S_W) if n < HT0 else (v32, 0.5 * S_W / (S_XW * S_XW) if n < HT0 + HTS else 1.0)
                dve.scalar_tensor_tensor(out=HL[:, r, :], in0=src[:, r, :], scalar=scale, in1=HH[:, r, :],
                                         op0=ALU.mult, op1=ALU.subtract).then_inc(hid_lo.by(n), 1)

            def hidden_product(i, n):
                dve.wait_ge(act_done.sem, act_done.at(i, n))
                r = n % RING
                if n < HT0 + HTS:
                    a_, b_ = ps[:, 2 * (n % 2), :], ps[:, 2 * (n % 2) + 1, :]
                    link(dve.scalar_tensor_tensor(out=v32[:, r, :], in0=h32[:, r, :], scalar=1.0, in1=a_,
                                                  op0=ALU.add, op1=ALU.mult))
                    dve.tensor_tensor(v32[:, r, :], v32[:, r, :], b_, ALU.mult).then_inc(prod_done.by(n), 1)
                else:
                    e = (n - HT0 - HTS) // 2
                    if n % 2 == 0:
                        dve.wait_ge(bc_ready.sem, bc_ready.at(i, e))
                    dve.tensor_tensor(v32[:, r, :], h32[:, r, :], ps[:, 7 - e % 2, :], ALU.mult)\
                        .then_inc(prod_done.by(n), 1)

            with dve.Fori(0, groups) as i:
                chain.i, chain.done = i, setup
                dve.wait_ge(x_loaded.sem, x_loaded.at(i, "x"))
                measure(i, 0, range(SEQS), x_in)
                carry_wait()
                aggregate(i, 0, range(SEQS))
                masks(i, 0)
                low("v0", V[0][1][:, :, 0:HD], ctx_in[:, :, :].rearrange("p s (h d) -> p (s h) d", d=HD), S_W,
                    V[0][0][:, :, 0:HD])
                normalise(i, 0, x_in)
                masks(i, 1)
                for t in range(KT):
                    low(f"ct{t}", CT[1][:, t, :], ps[:, 2 + t, :], S_W, CT[0][:, t, :])
                for t in range(KT):
                    query_low(f"qa{t}", 0, t, t)
                attention(i, 0)

                normalise(i, 1, x)
                for t in range(KT):
                    low(f"xb{t}", XT[1][:, t, :], ps[:, t, :], S_X, XT[0][:, t, :])
                top1_rows(i)
                for n in range(HT0):
                    hidden_low(i, n)
                dve.wait_ge(g2_done.sem, g2_done.at(i, HT0 - 1))
                for s in range(SEQS):
                    dve.scalar_tensor_tensor(out=x[:, s, :], in0=y(s), scalar=tg[:, 1:2], in1=x[:, s, :],
                                             op0=ALU.mult, op1=ALU.add).then_inc(resid.by(("b", s)), 1)
                dve.wait_ge(resid.sem, resid.at(i, ("b", SEQS - 1)))
                measure(i, 2, range(SEQS), x)
                carry_wait()
                aggregate(i, 2, range(SEQS))

                for m in range(2):
                    low(f"k{m}", K1[1][:, m, :], ps[:, 2 + m, :], 1 / S_W, K1[0][:, m, :])
                normalise(i, 2, x)
                for m in range(2):
                    low("v" + "ab"[m], V[1][1][:, 32 * m:32 * m + 32, 0:HD],
                        ps[:, 4 + m, :].rearrange("p (h d) -> p h d", d=HD), 1 / S_W,
                        V[1][0][:, 32 * m:32 * m + 32, 0:HD])
                for t in range(KT):
                    low(f"xc{t}", XT[1][:, t, :], ps[:, t, :], S_X, XT[0][:, t, :])
                for m in range(2):
                    query_low(f"qc{m}", 1, m, 6 + m)
                attention(i, 1)

                normalise(i, 3, x)
                for t in range(KT):
                    low(f"xd{t}", XT[1][:, t, :], ps[:, t, :], S_X, XT[0][:, t, :])
                gate_rows(i)
                for n in range(HT0, HT + 1):
                    if n < HT:
                        hidden_product(i, n)
                    if n > HT0:
                        hidden_low(i, n - 1)
                dve.wait_ge(g2_done.sem, g2_done.at(i, HT - 1))
                dve.wait_ge(out_stored.sem, out_stored.before(i + 1))
                for s in range(SEQS):
                    dve.scalar_tensor_tensor(out=x_out[:, s, :], in0=y(s), scalar=tg[:, 3:4], in1=x[:, s, :],
                                             op0=ALU.mult, op1=ALU.add).then_inc(resid.by(("d", s)), 1)
                assert chain.done - setup == DVE_LINKS, f"DVE_LINKS {chain.done - setup}"


_RENAMED = {"x": "x", "ctx": "ctx_1024", "mask0": "mask_Bx1xSxS2_ik1", "mask1": "mask_BxS2_ik0"}


def kernel(**inputs):
    import numpy as np
    import concourse.bacc as bacc
    from concourse.bass_utils import run_bass_kernel_spmd

    v = {k: np.asarray(t) for k, t in inputs.items()}
    arrays = {
        "x": v["x"], "ctx": v["ctx_1024"], "mask0": v["mask_Bx1xSxS2_ik1"], "mask1": v["mask_BxS2_ik0"],
        "g": np.stack([np.stack([v["g_xattn"][l], v["g_ffn"][l]]) for l in range(2)]),
        "Wg": v["L0_ffn_Wg"].T, "ln_s": v["L0_ffn_ln_scale"].T, "ln_b": v["L0_ffn_ln_bias"].T,
        "W1": v["L0_ffn_W1"].transpose(1, 0, 2).reshape(D, HT0 * P),
        "b1": v["L0_ffn_b1"].reshape(HT0, P).T,
        "W2": v["L0_ffn_W2"].reshape(HT0 * P, D), "b2": v["L0_ffn_b2"],
        "q_w": v["L1_xattn_q_w"].T, "k_w": v["L1_xattn_k_w"].T, "v_w": v["L1_xattn_v_w"].T,
        "q_b": v["L1_xattn_q_b"], "k_b": v["L1_xattn_k_b"], "v_b": v["L1_xattn_v_b"],
        "router_w": v["L1_ffn_router_w"].T, "router_b": v["L1_ffn_router_bias"],
        "sw1": v["L1_ffn_sw1"], "sw3": v["L1_ffn_sw3"], "sw2": v["L1_ffn_sw2"],
        "ew1": v["L1_ffn_ew1"].transpose(1, 0, 2).reshape(D, HTR * P),
        "ew2": v["L1_ffn_ew2"].reshape(HTR * P, D),
    }
    nc = bacc.Bacc("TRN2", target_bir_lowering=False, num_devices=1)
    feeds, aps = {}, {}
    for name, t in arrays.items():
        t = np.ascontiguousarray(t)
        feeds[f"in_{name}"] = t
        aps[name] = nc.dram_tensor(f"in_{name}", t.shape, mybir.dt.from_np(t.dtype), kind="ExternalInput").ap()
    out = nc.dram_tensor("out", v["x"].shape, F32, kind="ExternalOutput").ap()
    build(nc, aps, out)
    r = run_bass_kernel_spmd(nc, [feeds], core_ids=[0])
    return r.results[0]["out"]
```

```python
from contextlib import ExitStack

import concourse.bass as bass
from concourse import mybir

F32 = mybir.dt.float32
F16 = mybir.dt.float16
BF16 = mybir.dt.bfloat16
I32 = mybir.dt.int32
U32 = mybir.dt.uint32
ALU = mybir.AluOpType
ACT = mybir.ActivationFunctionType
AX = mybir.AxisListType.X

P = 128
D = 256
KT = D // P
SEQS = 4
TOK = SEQS * P
HEADS = 16
HD = D // HEADS
VW = HD + 1
E = 8
HT0 = 4
HTS = 4
HTR = 16
HTD = HTS + HTR
UNITS = 4 * SEQS
PL_LAG, AV_LAG = 3, 4
STEPS = HTS + E
START = {0: {4: 0, 7: 1, 10: 2, 13: 3, 16: 4}, 1: {3: 7, 6: 8, 9: 9, 12: 10, 15: 11}}
IN_BETWEEN = (5, 6)
START[1][-3] = 6
GATES_AT = (4, 10, 13)

LN_EPS = 1e-5
S_X = 2.0 ** 11
S_W = 2.0 ** 8
S_XW = S_X * S_W
S_WW = S_W * S_W
S_P = 2.0 ** 8
MASKED = 120000.0
OFF_EXPERT = 2.0 ** 15


class Signal:

    def __init__(self, sem, events, step=1):
        self.sem, self.events, self.step, self.turn = sem, list(events), step, 0

    def by(self, event):
        assert self.events[self.turn % len(self.events)] == event, (self.events[self.turn % len(self.events)], event)
        self.turn += 1
        return self.sem

    def at(self, i, event):
        return i * (len(self.events) * self.step) + (self.events.index(event) + 1) * self.step

    def before(self, i):
        return i * (len(self.events) * self.step)


class Chain:

    def __init__(self, eng, sem, per_group, setup=0):
        self.eng, self.sem, self.per_group, self.setup = eng, sem, per_group, setup
        self.i, self.done = None, 0

    def group(self, i):
        assert self.i is None or self.done == self.setup + self.per_group, (self.done - self.setup, self.per_group)
        self.i, self.done = i, self.setup

    def link(self, ins):
        ins.then_inc(self.sem, 1)
        self.done += 1
        if self.i is None:
            self.eng.wait_ge(self.sem, self.done)
        else:
            self.eng.wait_ge(self.sem, self.i * self.per_group + self.done)


W_COLS = {}
_at = 0
for _name, _n in (("q_w", KT * D), ("k_w", KT * D), ("v_w", KT * D), ("W1", KT * HT0 * P), ("W2", HT0 * D),
                  ("Wg", KT * E), ("router_w", KT * E), ("sw1", KT * HTS * P), ("sw3", KT * HTS * P),
                  ("sw2", HTS * D), ("ew1", KT * HTR * P), ("ew2", HTR * D)):
    W_COLS[_name] = (_at, _n)
    _at += _n
W_TOTAL = _at
CHUNKS = [("q_w", "k_w", "v_w", "W1", "W2", "Wg", "router_w"), ("sw1", "sw3", "sw2"), ("ew1",), ("ew2",)]
STAGE = 4096
DVE_SETUP, DVE_LINKS, DVE_PREP_LINKS, DVE_ROUTER_LINKS = 19, 34, 5, 18
POOL_LINKS, POOL_PREP_LINKS = 4, 2


def build(nc, a, out):
    seqs = a["x"].shape[0]
    groups = seqs // SEQS
    assert a["x"].shape == (seqs, P, D) and seqs % SEQS == 0

    with ExitStack() as ctx:
        def sb(name, shape, dt):
            return ctx.enter_context(nc.sbuf_tensor(name, shape, dt))

        def sem(name):
            return ctx.enter_context(nc.semaphore(name))

        def signal(name, events, step=1):
            return Signal(sem(name), events, step)

        WH = sb("WH", [P, W_TOTAL], F16)
        WL = sb("WL", [P, W_TOTAL], F16)
        attn_arena = sb("attn_arena", [P, STAGE], F32)
        hid_arena = sb("hid_arena", [P, STAGE], F32)
        stage = [attn_arena, hid_arena]
        P32 = attn_arena[:, 0:2048].rearrange("p (b n) -> p b n", b=4)
        PH = attn_arena[:, 2048:3072].bitcast(F16).rearrange("p (b n) -> p b n", b=4)
        PL = attn_arena[:, 3072:4096].bitcast(F16).rearrange("p (b n) -> p b n", b=4)
        h32 = hid_arena[:, 0:1024].rearrange("p (b n) -> p b n", b=2)
        v32 = hid_arena[:, 1024:2048].rearrange("p (b n) -> p b n", b=2)
        HH = hid_arena[:, 2048:3072].bitcast(F16).rearrange("p (b n) -> p b n", b=4)
        HL = hid_arena[:, 3072:4096].bitcast(F16).rearrange("p (b n) -> p b n", b=4)

        x_in = sb("x_in", [P, SEQS, D], F32)
        x = sb("x_res", [P, SEQS, D], F32)
        x_ffn = sb("x_ffn", [P, SEQS, D], F32)
        x_out = sb("x_out", [P, SEQS, D], F32)
        ctx_in = sb("ctx_in", [P, SEQS, D], F32)
        m_in = [sb(f"mask{l}_in", [P, SEQS, P], I32) for l in range(2)]
        mk_in = sb("mask1_keys_in", [P, SEQS], I32)
        key_bias = sb("key_bias", [P, SEQS], F32)
        off = sb("off", [P, SEQS, P], F32)
        n_off = sb("n_off", [P, 2, SEQS], F32)
        some_on = sb("some_on", [P, 2, SEQS], F32)
        take_off = sb("take_off", [P, 2, SEQS], F32)
        nan_row = sb("nan_row", [P, SEQS], F32)
        maskb = [sb(f"mask_bias{l}", [P, SEQS, P], BF16) for l in range(2)]
        xn = sb("xn", [P, SEQS, D], F32)
        XT = [sb(f"XT_{h}", [P, KT, TOK], F16) for h in "hl"]
        XD = [sb(f"XD_{h}", [P, KT, TOK], F16) for h in "hl"]
        CT = [sb(f"CT_{h}", [P, KT, TOK], F16) for h in "hl"]
        K1 = [sb(f"K1_{h}", [P, KT, TOK], F16) for h in "hl"]
        Q = [[sb(f"Q{l}_{h}", [P, KT, 2, TOK], F16) for h in "hl"] for l in range(2)]
        V = [[sb(f"V{l}_{h}", [P, SEQS * HEADS, VW], F16) for h in "hl"] for l in range(2)]
        stats = [sb(f"stats{h}", [P, SEQS, 6], F32) for h in range(2)]
        mv = sb("mv", [P, 4, SEQS, 2], F32)
        rstd = sb("rstd", [P, 4, SEQS], F32)
        ptmp = [sb(f"ptmp{f}", [P, 3, SEQS], F32) for f in range(4)]
        negmax = sb("negmax", [P, 2, 4], BF16)
        mT = sb("mT", [P, 2, P], BF16)
        rden = sb("rden", [P, HEADS], F32)
        att = sb("att", [P, D], F32)
        lg = sb("lg", [P, SEQS, E], F32)
        top8 = sb("top8", [P, SEQS, 8], F32)
        topi = sb("topi", [P, SEQS, 8], U32)
        topf = sb("topf", [P, SEQS, 8], F32)
        oh = sb("oh", [P, SEQS, E], F32)
        oh2 = sb("oh2", [P, SEQS, E], F32)
        sig = sb("sig", [P, SEQS, E], F32)
        gates = sb("gates", [P, SEQS, E], F32)
        den = sb("den", [P, 5, SEQS], F32)
        idle = sb("idle", [P, 1], F32)
        tokens = sb("tokens", [P, SEQS, 32], F16)
        tokT = sb("tokT", [32, TOK], F16)

        id32 = sb("id32", [P, P], F32)
        id16 = sb("id16", [P, P], F16)
        idb = sb("idb", [P, P], BF16)
        pick = sb("pick", [P, 4, P], BF16)
        expert_of = sb("expert_of", [32, E, 64], F16)
        iota8 = sb("iota8", [P, E], F32)
        iota8i = sb("iota8i", [P, E], I32)
        pi = sb("pi", [P, 4], I32)
        pf = sb("pf", [P, 4], F32)
        half = sb("half", [P, 2, 2], F32)
        c_eps = sb("c_eps", [P, SEQS], F32)
        c_1eps = sb("c_1eps", [P, SEQS], F32)
        c_eps2 = sb("c_eps2", [P, SEQS], F32)
        c_mhalf = sb("c_mhalf", [P, SEQS], F32)
        lnP = sb("lnP", [P, 1], F32)
        ones_q = sb("ones_q", [2, TOK], F16)
        ones_kv = sb("ones_kv", [2, TOK], F16)
        gates4 = sb("gates4", [P, 4], F32)
        tg = sb("tg", [P, 4], F32)
        ln_s = sb("ln_s", [P, KT, E], F32)
        ln_b = sb("ln_b", [P, KT, E], F32)
        b1 = sb("b1", [P, HT0], F32)
        b1e = sb("b1e", [P, HT0], F32)
        b2f = sb("b2f", [32, D], F32)
        b2h = sb("b2h", [32, D], F16)
        b2 = sb("b2", [32, D], F16)
        bf = sb("bf", [2, 3, D], F32)
        bh = sb("bh", [2, 3, D], F16)
        qkv_b = sb("qkv_b", [2, 3, D], F16)
        rb = sb("rb", [P, E], F32)

        ps = ctx.enter_context(nc.psum_tensor("ps", [P, 8, 512], F32))
        ST, SQ, OB = (0, 1), 2, 3
        Y = 4
        G = 6
        G0 = (7, 2, 3, 6)

        def by_heads(b):
            return ps[:, b, :].rearrange("p (t e q) -> p t e q", t=KT, e=2)

        O = ps[:, OB, 0:HEADS * VW].rearrange("p (h w) -> p h w", h=HEADS)
        maxT = ps[0:4, SQ, 0:64].bitcast(BF16)

        def token_bank(b):
            return ps[0:32, b, 0:256].bitcast(F16)

        def lgp(b):
            return ps[:, b, 0:SEQS * E]

        def y(s, first):
            return ps[:, first + s // 2, (s % 2) * D:(s % 2 + 1) * D]

        def slices(j):
            return [j] if j < HTS else [2 * j - HTS, 2 * j - HTS + 1]

        def step_at(l, u, after):
            return START[l].get(u - after)

        w_loaded = [sem(f"w_loaded{c}") for c in range(len(CHUNKS))]
        small_loaded = sem("small_loaded")
        consts_made = sem("consts_made")
        const_step = sem("const_step")
        b1_ready = sem("b1_ready")
        w1_scaled = sem("w1_scaled")
        w_high = sem("w_high")
        w_low = sem("w_low")
        tg_ready = sem("tg_ready")
        setup_done = sem("setup_done")
        dve_step = sem("dve_step")
        pool_step = sem("pool_step")
        dve_prep_step = sem("dve_prep_step")
        dve_router_step = sem("dve_router_step")
        pool_prep_step = sem("pool_prep_step")

        x_loaded = signal("x_loaded", ["x"], 16)
        ctx_loaded = signal("ctx_loaded", ["ctx"], 16)
        m_loaded = [signal(f"mask{l}_loaded", ["m"], 16) for l in range(2)]
        mk_loaded = signal("mask1_keys_loaded", ["m"], 16)
        out_stored = signal("out_stored", ["out"], 16)

        evac = {"v0": 1, "ct": KT, "qa": KT, "xb": KT, "k": KT, "v1": 2, "xc": KT, "qc": KT, "xd": KT}
        hi = {n_: signal(f"high_{n_}", range(c)) for n_, c in evac.items()}
        lo = {n_: signal(f"low_{n_}", range(c)) for n_, c in evac.items()}
        units = [(l, u) for l in range(2) for u in range(UNITS)]
        s_ready = signal("s_ready", units)
        max_done = signal("max_done", units)
        t_ready = signal("t_ready", units)
        mt_ready = signal("mt_ready", units)
        st_ready = signal("st_ready", units)
        exp_done = signal("exp_done", [(l, u, k) for l, u in units for k in range(2)])
        plo_done = signal("plo_done", units)
        av_done = signal("av_done", units)
        o_read = signal("o_read", [(l, s) for l in range(2) for s in range(SEQS)])
        resid = signal("resid", [(f, s) for f in "abc" for s in range(SEQS)])
        x_kept = signal("x_kept", range(1))
        x_moved = signal("x_moved", range(1))
        stats_ready = {f: signal(f"stats_ready_{f}", range(1)) for f in "abcd"}
        rstd_ready = {f: signal(f"rstd_ready_{f}", range(1)) for f in "abcd"}
        xn_ready = {f: signal(f"xn_ready_{f}", range(SEQS)) for f in "abcd"}
        xt_ready = {f: signal(f"xt_ready_{f}", range(KT)) for f in "abcd"}
        ct_ready = signal("ct_ready", range(KT))
        masks_made = [signal(f"masks{l}_made", range(1)) for l in range(2)]
        lg_ready = {f: signal(f"logits_ready_{f}", range(1)) for f in "bd"}
        lg_tanh = signal("lg_tanh", range(1))
        gates_ready = signal("gates_ready", range(1))
        tok_ready = signal("tok_ready", range(1))
        tokp_ready = signal("tokp_ready", range(1))
        tokT_ready = signal("tokT_ready", range(1))
        proj_ready = signal("proj_ready", ["k0", "k1", "v0", "v1", "q0", "q1"])
        e_g1, e_act, e_hi, e_lo = (signal("ffn0_" + n_, range(HT0)) for n_ in ("g1", "act", "hi", "lo"))
        e_sums = signal("ffn0_sums", range(2))
        g1, acted, hid_hi, hid_lo, g2 = (signal("ffn1_" + n_, range(HTD))
                                         for n_ in ("g1", "act", "hi", "lo", "g2"))
        silu_half = signal("silu_half", range(HTS))
        prod = signal("swiglu_product", range(HTS))
        summed = signal("summed", range(1 + E))

        def w(part, name, t, lo_, n, m=P):
            base, size = W_COLS[name]
            per = {"q_w": D, "k_w": D, "v_w": D, "W1": HT0 * P, "W2": D, "Wg": E, "router_w": E, "sw1": HTS * P,
                   "sw3": HTS * P, "sw2": D, "ew1": HTR * P, "ew2": D}[name]
            c = base + t * per + lo_
            return (WH, WL)[part][0:m, c:c + n]

        PARTS = ((0, 0), (0, 1), (1, 0))

        xg = a["x"].rearrange("(g s) t d -> g t s d", s=SEQS)
        og = out.rearrange("(g s) t d -> g t s d", s=SEQS)
        cg = a["ctx"].rearrange("(g s) t d -> g t s d", s=SEQS)
        m0g = a["mask0"].rearrange("(g s) o q k -> g q (s o) k", s=SEQS)
        m1g = a["mask1"].rearrange("(g s) k -> g s k", s=SEQS)
        mkg = a["mask1_keys"].rearrange("k (g s) -> g k s", s=SEQS)

        block = ctx.enter_context(nc.Block())

        @block.sync
        def _(sp):
            def load(i):
                sp.dma_start(ctx_in[:, :, :], cg[i]).then_inc(ctx_loaded.sem, 16)
                sp.dma_start(x_in[:, :, :], xg[i]).then_inc(x_loaded.sem, 16)
                sp.dma_start(m_in[0][:, :, :], m0g[i]).then_inc(m_loaded[0].sem, 16)
                sp.dma_start(m_in[1][:, :, :], m1g[i].partition_broadcast(P)).then_inc(m_loaded[1].sem, 16)
                sp.dma_start(mk_in[:, :], mkg[i]).then_inc(mk_loaded.sem, 16)

            smalls = [(ln_s[:, :, :], a["ln_s"].rearrange("(t p) e -> p t e", p=P)),
                      (ln_b[:, :, :], a["ln_b"].rearrange("(t p) e -> p t e", p=P)),
                      (b1[:, :], a["b1"]),
                      (rb[:, :], a["router_b"].partition_broadcast(P)),
                      (b2f[0:8, :], a["b2"]), (b2f[8:16, :], a["b2"])]
            smalls += [(gates4[:, 2 * j:2 * j + 2], a["g"][j].partition_broadcast(P)) for j in range(2)]
            for j, name in enumerate(("q_b", "k_b", "v_b")):
                src = a[name].rearrange("(o d) -> o d", o=1)
                smalls += [(bf[0:1, j, :], src), (bf[1:2, j, :], src)]
            sp.wait_ge(consts_made, 1)
            for dst, src in smalls:
                sp.dma_start(dst, src).then_inc(small_loaded, 16)
            for c, names in enumerate(CHUNKS):
                if c >= 2:
                    sp.wait_ge(w_high, c - 1)
                    sp.wait_ge(w_low, c - 1)
                at = 0
                for name in names:
                    n = W_COLS[name][1]
                    rows = a[name].shape[0] // P
                    src = a[name].rearrange("(t p) n -> p t n", p=P)
                    dst = stage[c % 2][:, at:at + n].rearrange("p (t n) -> p t n", t=rows)
                    sp.dma_start(dst, src).then_inc(w_loaded[c], 16)
                    at += n
                if c == 1:
                    load(0)

            def body(i):
                sp.wait_ge(lo["v0"].sem, lo["v0"].at(i, 0))
                sp.wait_ge(ct_ready.sem, ct_ready.at(i, KT - 1))
                sp.dma_start(ctx_in[:, :, :], cg[i + 1]).then_inc(ctx_loaded.sem, 16)
                sp.wait_ge(xn_ready["a"].sem, xn_ready["a"].at(i, SEQS - 1))
                sp.wait_ge(x_moved.sem, x_moved.at(i, 0))
                sp.dma_start(x_in[:, :, :], xg[i + 1]).then_inc(x_loaded.sem, 16)
                sp.wait_ge(masks_made[0].sem, masks_made[0].at(i, 0))
                sp.dma_start(m_in[0][:, :, :], m0g[i + 1]).then_inc(m_loaded[0].sem, 16)
                sp.wait_ge(masks_made[1].sem, masks_made[1].at(i, 0))
                sp.dma_start(m_in[1][:, :, :], m1g[i + 1].partition_broadcast(P)).then_inc(m_loaded[1].sem, 16)
                sp.dma_start(mk_in[:, :], mkg[i + 1]).then_inc(mk_loaded.sem, 16)

            def store(i):
                sp.wait_ge(summed.sem, summed.at(i, E))
                sp.dma_start(og[i], x_out[:, :, :]).then_inc(out_stored.sem, 16)

            body(0)
            with sp.Fori(1, groups - 1) as i:
                body(i)
                store(i - 1)
            store(groups - 2)
            store(groups - 1)
            sp.wait_ge(out_stored.sem, out_stored.before(groups + 1))

        @block.gpsimd
        def _(pool):
            pool.memset(b2f[:, :], 0.0).then_inc(consts_made, 1)
            steps = 0
            zeroed = [(id32, 0.0), (id16, 0.0), (idb, 0.0), (pick, 0.0), (expert_of, 0.0)]
            for t, v in zeroed:
                pool.memset(t[tuple(slice(None) for _ in t.shape)], v).then_inc(const_step, 1)
                steps += 1
            for t, v in ((c_eps, LN_EPS), (c_1eps, 1.0 + LN_EPS), (c_eps2, LN_EPS * LN_EPS), (c_mhalf, -0.5), (ones_q, S_X), (ones_kv, S_W)):
                pool.memset(t[:, :], v).then_inc(consts_made, 1)
            pool.memset(mT[:, :, :], 0.0).then_inc(consts_made, 1)
            pool.memset(x_out[:, 0, 0:1], 0.0).then_inc(out_stored.sem, 16)
            pool.memset(tokens[:, :, :], 0.0).then_inc(consts_made, 1)
            for l in range(2):
                for h in range(2):
                    pool.memset(V[l][h][:, :, HD:VW], (S_W, 0.0)[h]).then_inc(consts_made, 1)
            pool.wait_ge(const_step, steps)
            for t in (id32, id16, idb):
                pool.affine_select(out=t[:, :], in_=t[:, :], compare_op=ALU.not_equal, fill=1.0, base=0,
                                   pattern=[[-1, P]], channel_multiplier=1).then_inc(consts_made, 1)
            pool.affine_select(out=pick[:, :, :], in_=pick[:, :, :], compare_op=ALU.not_equal, fill=1.0, base=0,
                               pattern=[[-1, 4], [0, P]], channel_multiplier=1).then_inc(consts_made, 1)
            pool.affine_select(out=expert_of[:, :, :], in_=expert_of[:, :, :], compare_op=ALU.not_equal,
                               fill=OFF_EXPERT, base=-16, pattern=[[-1, E], [0, 64]],
                               channel_multiplier=1).then_inc(consts_made, 1)
            pool.iota(iota8i[:, :], pattern=[[1, E]], base=0, channel_multiplier=0).then_inc(consts_made, 1)
            pool.iota(pi[:, 0:1], pattern=[[0, 1]], base=0, channel_multiplier=1).then_inc(consts_made, 1)

            chain = Chain(pool, pool_step, POOL_LINKS)
            prep = Chain(pool, pool_prep_step, POOL_PREP_LINKS)

            def inverse_std(i, ph):
                f = "abcd".index(ph)
                link = (prep if ph == "a" else chain).link
                var, r, q = mv[:, f, :, 1], rstd[:, f, :], ptmp[f]
                pool.wait_ge(stats_ready[ph].sem, stats_ready[ph].at(i, 0))
                if ph == "a":
                    link(pool.tensor_tensor(q[:, 0, :], var, c_eps[:, :], ALU.add))
                    link(pool.tensor_tensor(q[:, 1, :], q[:, 0, :], c_mhalf[:, :], ALU.pow))
                    pool.wait_ge(masks_made[0].sem, masks_made[0].at(i, 0))
                    pool.tensor_tensor(r, q[:, 1, :], some_on[:, 0, :], ALU.mult).then_inc(rstd_ready[ph].by(0), 1)
                elif ph == "b":
                    link(pool.tensor_tensor(q[:, 0, :], var, c_1eps[:, :], ALU.mult))
                    link(pool.tensor_tensor(q[:, 1, :], q[:, 0, :], c_eps2[:, :], ALU.add))
                    pool.tensor_tensor(r, q[:, 1, :], c_mhalf[:, :], ALU.pow).then_inc(rstd_ready[ph].by(0), 1)
                else:
                    link(pool.tensor_tensor(q[:, 0, :], var, c_eps[:, :], ALU.add))
                    pool.tensor_tensor(r, q[:, 0, :], c_mhalf[:, :], ALU.pow).then_inc(rstd_ready[ph].by(0), 1)

            def carry_wait(f):
                pool.tensor_tensor(ptmp[f][:, 2, :], c_eps[:, :], c_eps[:, :], ALU.add)

            def group(i, following, fill):
                chain.group(i)
                inverse_std(i, "b")
                if following:
                    prep.group(i + 1)
                    inverse_std(i + 1, "a")
                inverse_std(i, "c")
                inverse_std(i, "d")
                if fill:
                    pool.wait_ge(summed.sem, summed.at(i - 1, 0))
                    carry_wait(0)
                pool.tensor_copy(x_ffn[:, :, :], x[:, :, :]).then_inc(x_kept.by(0), 1)
                if following:
                    pool.wait_ge(xn_ready["d"].sem, xn_ready["d"].at(i, SEQS - 1))
                    carry_wait(2)
                    pool.wait_ge(x_kept.sem, x_kept.at(i, 0))
                    carry_wait(3)
                    pool.tensor_copy(x[:, :, :], x_in[:, :, :]).then_inc(x_moved.by(0), 1)

            pool.wait_ge(x_loaded.sem, 16)
            pool.tensor_copy(x[:, :, :], x_in[:, :, :]).then_inc(x_moved.by(0), 1)
            prep.group(0)
            inverse_std(0, "a")
            group(0, True, False)
            with pool.Fori(1, groups - 1) as i:
                group(i, True, True)
            group(groups - 1, False, True)

        N_CONSTS = 1 + 6 + 1 + 1 + 4 + 3 + 1 + 1 + 2

        @block.tensor
        def _(pe):
            pe.wait_ge(consts_made, N_CONSTS)
            pe.wait_ge(small_loaded, 16 * 14)
            pe.wait_ge(w_loaded[0], 16 * len(CHUNKS[0]))
            at = W_COLS["W1"][0]
            for t in range(HT0):
                for k in range(KT):
                    c = at + k * HT0 * P + t * P
                    mm = pe.matmul(ps[:, 0, t * E:(t + 1) * E], stage[0][:, c:c + P], ln_b[:, k, :],
                                   start=(t == 0 and k == 0), stop=(k == KT - 1), skip_group_check=True)
            mm.then_inc(b1_ready, 1)
            pe.wait_ge(setup_done, 1)

            def turn(i, f, first):
                for t in range(KT):
                    for s in range(SEQS):
                        if t == 0:
                            pe.wait_ge(xn_ready[f].sem, xn_ready[f].at(i, s))
                        mm = pe.transpose(ps[:, first + t, s * P:(s + 1) * P], xn[:, s, t * P:(t + 1) * P],
                                          id32[:, :])
                    mm.then_inc(xt_ready[f].by(t), 1)

            def scores(i, l, u):
                s, j = divmod(u, 4)
                tok = slice(s * P, (s + 1) * P)
                r = slice(32 * j, 32 * j + 32)
                if u:
                    pe.wait_ge(mt_ready.sem, mt_ready.at(i, (l, u - 1)))
                pe.matmul(ps[:, SQ, :].rearrange("p (n k) -> p n k", n=4), idb[:, :],
                          maskb[l][:, s:s + 1, :].to_broadcast([P, 4, P]), start=True, stop=False,
                          skip_group_check=True)
                for t in range(KT):
                    for e in range(2):
                        mm = pe.matmul(by_heads(SQ)[:, t, e, :], Q[l][0][r, t, e, tok],
                                       (CT, K1)[l][0][r, t, tok], start=False, stop=True, skip_group_check=True)
                mm.then_inc(s_ready.by((l, u)), 1)

            def turn_maxima(i, l, u):
                pe.wait_ge(max_done.sem, max_done.at(i, (l, u)))
                pe.transpose(maxT, negmax[:, u % 2, :], idb[:, :]).then_inc(t_ready.by((l, u)), 1)

            def attention(i, l, following, fill):
                keys = CT if l == 0 else K1
                B = maskb[l]
                qh, ql = Q[l]
                for u in range(1 - l, UNITS + AV_LAG):
                    if u < UNITS:
                        scores(i, l, u)
                    if 1 <= u <= UNITS:
                        v = u - 1
                        s, j = divmod(v, 4)
                        tok = slice(s * P, (s + 1) * P)
                        r = slice(32 * j, 32 * j + 32)
                        bank = ST[v % 2]
                        pe.wait_ge(mt_ready.sem, mt_ready.at(i, (l, v)))
                        if v >= 2:
                            pe.wait_ge(exp_done.sem, exp_done.at(i, (l, v - 2, 1)))
                        if l == 0:
                            pe.matmul(ps[:, bank, :].rearrange("p (n q) -> p n q", n=4), B[:, s, :],
                                      idb[:, :].unsqueeze(1).to_broadcast([P, 4, P]), start=True, stop=False,
                                      skip_group_check=True)
                        for c in range(4):
                            pe.matmul(by_heads(bank)[:, c // 2, c % 2, :], pick[:, c, :], mT[:, v % 2, :],
                                      start=(l == 1 and c == 0), stop=False, skip_group_check=True)
                        for t in range(KT):
                            for n, (pk, pq) in enumerate(PARTS):
                                mm = pe.matmul(by_heads(bank)[:, t, :, :], keys[pk][r, t, tok],
                                               (qh, ql)[pq][r, t, :, tok],
                                               start=False, stop=(n == 2), skip_group_check=True)
                        mm.then_inc(st_ready.by((l, v)), 1)
                    beside_maxima(i, l, u, following, fill)
                    if u < UNITS:
                        turn_maxima(i, l, u)
                    if u >= AV_LAG:
                        v = u - AV_LAG
                        s, j = divmod(v, 4)
                        if l == 0 and v == 0:
                            pe.wait_ge(lo["v0"].sem, lo["v0"].at(i, 0))
                        pe.wait_ge(plo_done.sem, plo_done.at(i, (l, v)))
                        if j == 0 and s:
                            pe.wait_ge(o_read.sem, o_read.at(i, (l, s - 1)))
                        elif j == 0 and l == 0 and fill:
                            pe.wait_ge(o_read.sem, o_read.at(i - 1, (1, SEQS - 1)))
                        for t in range(KT):
                            for e in range(2):
                                c = t * 2 + e
                                h = 8 * t + 2 * j + e
                                for n, (pp, pv) in enumerate(PARTS):
                                    mm = pe.matmul(O[:, h, :], (PH, PL)[pp][:, v % 4, c * P:(c + 1) * P],
                                                   V[l][pv][:, s * HEADS + h, :],
                                                   start=(j == 0 and c == 0 and n == 0), stop=(n == 2),
                                                   skip_group_check=True)
                        mm.then_inc(av_done.by((l, v)), 1)
                    if fill:
                        for half_ in range(2):
                            j = step_at(l, u, 5 + half_)
                            if j is not None and half_ < len(slices(j)):
                                step_second(i - 1, j, half_)

            def beside_maxima(i, l, u, following, fill):
                if fill:
                    if l == 0 and u == 1:
                        turn(i - 1, "d", G)
                    if l == 0 and u == 3:
                        pe.wait_ge(lo["xd"].sem, lo["xd"].at(i - 1, KT - 1))
                        logits(i - 1, "d", "router_w", XD, G)
                    if following and l == 1 and u == 3:
                        pe.wait_ge(lo["ct"].sem, lo["ct"].at(i + 1, KT - 1))
                    for half_ in range(2):
                        j = step_at(l, u, half_)
                        if j is not None:
                            step_first(i - 1, j, half_)
                if following and l == 1 and u < KT:
                    turn_context(i + 1, u)

            def wide(bank, name, m, src, bias=None, ones=None, stop=True):
                out_ = ps[:, bank, :]
                n = 0
                for k in range(KT):
                    for pw, px in PARTS:
                        mm = pe.matmul(out_, w(pw, name, k, m * P, P), src[px][:, k, :], start=(n == 0),
                                       stop=(stop and bias is None and n == 3 * KT - 1), skip_group_check=True)
                        n += 1
                if bias is not None:
                    mm = pe.matmul(out_, bias, ones, start=False, stop=True, skip_group_check=True)
                return mm

            def logits(i, ph, name, src, bank):
                for s in range(SEQS):
                    n = 0
                    for k in range(KT):
                        for px, pw in PARTS:
                            mm = pe.matmul(lgp(bank)[:, s * E:(s + 1) * E], src[px][:, k, s * P:(s + 1) * P],
                                           w(pw, name, k, 0, E), start=(s == 0 and n == 0),
                                           stop=(n == 3 * KT - 1), skip_group_check=True)
                            n += 1
                mm.then_inc(lg_ready[ph].by(0), 1)

            def turn_tokens(i, bank):
                pe.wait_ge(tok_ready.sem, tok_ready.at(i, 0))
                for s in range(SEQS):
                    mm = pe.transpose(token_bank(bank)[:, s * P:(s + 1) * P], tokens[:, s, :], id16[:, :])
                mm.then_inc(tokp_ready.by(0), 1)

            def second(parts, slot, sums, name, t, first, last, banks=None):
                for s in range(SEQS):
                    tok = slice(s * P, (s + 1) * P)
                    for m, (ph_, pw) in enumerate(PARTS):
                        mm = pe.matmul(y(s, sums), parts[ph_][:, slot, tok], w(pw, name, t, 0, D),
                                       start=(first and m == 0 and s % 2 == 0), stop=(last and m == 2),
                                       skip_group_check=True)
                    if banks and s % 2:
                        mm.then_inc(banks.by(s // 2), 1)
                return mm

            def step_first(g, j, half_):
                n = slices(j)[0] if j < HTS else slices(j)[half_]
                if j < HTS:
                    if j:
                        pe.wait_ge(prod.sem, prod.at(g, j - 1))
                    elif half_ == 0:
                        pe.wait_ge(lg_tanh.sem, lg_tanh.at(g, 0))
                    mm = wide(G + half_, ("sw1", "sw3")[half_], n, XD)
                    if half_ == 0:
                        return
                else:
                    if n < HTS + 2:
                        pe.wait_ge(prod.sem, prod.at(g, HTS - 1))
                    else:
                        pe.wait_ge(acted.sem, acted.at(g, n - 2))
                    mm = wide(G + n % 2, "ew1", n - HTS, XD)
                mm.then_inc(g1.by(n), 1)

            def step_second(g, j, half_):
                n = slices(j)[half_]
                if n >= HTS and n % 2 == 0:
                    pe.wait_ge(summed.sem, summed.at(g, j - HTS))
                pe.wait_ge(hid_lo.sem, hid_lo.at(g, n))
                name, t = ("sw2", n) if n < HTS else ("ew2", n - HTS)
                first = n == 0 or (n >= HTS and n % 2 == 0)
                last = n == HTS - 1 or (n >= HTS and n % 2 == 1)
                second((HH, HL), n % 4, Y, name, t, first, last).then_inc(g2.by(n), 1)

            def turn_context(i, t):
                if t == 0:
                    pe.wait_ge(ctx_loaded.sem, ctx_loaded.at(i, "ctx"))
                for s in range(SEQS):
                    mm = pe.transpose(ps[:, G + t, s * P:(s + 1) * P], ctx_in[:, s, t * P:(t + 1) * P], id32[:, :])
                mm.then_inc(ct_ready.by(t), 1)

            def group(i, following, fill):
                attention(i, 0, following, fill)
                if fill:
                    pe.wait_ge(acted.sem, acted.at(i - 1, slices(4)[-1]))

                def keys(m):
                    wide(6 + m, "k_w", m, CT, qkv_b[:, 1, m * P:(m + 1) * P], ones_kv[:, :])\
                        .then_inc(proj_ready.by(f"k{m}"), 1)

                keys(0)
                turn(i, "b", 0)
                keys(1)
                pe.wait_ge(lo["xb"].sem, lo["xb"].at(i, KT - 1))
                logits(i, "b", "Wg", XT, 6)
                pe.wait_ge(lo["k"].sem, lo["k"].at(i, 1))
                wide(G0[0], "W1", 0, XT, stop=False)
                wide(G0[1], "W1", 1, XT, stop=False)
                turn_tokens(i, 6)
                wide(G0[2], "W1", 2, XT, stop=False)
                if following:
                    turn(i + 1, "a", 0)
                pe.wait_ge(tokT_ready.sem, tokT_ready.at(i, 0))
                wide(G0[3], "W1", 3, XT, stop=False)
                for n in range(HT0):
                    pe.matmul(ps[:, G0[n], :], expert_of[:, 2 * n:2 * n + 2, :].rearrange("r e h -> r (e h)"),
                              tokT[:, :], start=False, stop=True, skip_group_check=True)\
                        .then_inc(e_g1.by(n), 1)
                if fill:
                    for half_ in range(2):
                        step_second(i - 1, 4, half_)
                if following:
                    pe.wait_ge(lo["qa"].sem, lo["qa"].at(i + 1, KT - 1))
                for n in range(HT0):
                    if n == HT0 - 1:
                        for s in range(SEQS):
                            pe.matmul(y(s, 0), tokT[:, s * P:(s + 1) * P], b2[:, :], start=False, stop=False,
                                      skip_group_check=True)
                    pe.wait_ge(e_lo.sem, e_lo.at(i, n))
                    second((PH, PL), n, 0, "W2", n, n == 0, n == HT0 - 1, e_sums if n == HT0 - 1 else None)
                if fill:
                    for half_ in range(2):
                        step_first(i - 1, IN_BETWEEN[0], half_)
                for s in range(SEQS):
                    n = 0
                    for k in range(KT):
                        for pc, pw in PARTS:
                            pe.matmul(y(s, 2), CT[pc][:, k, s * P:(s + 1) * P], w(pw, "v_w", k, 0, D),
                                      start=(n == 0 and s % 2 == 0), stop=False, skip_group_check=True)
                            n += 1
                    mm = pe.matmul(y(s, 2), ones_kv[:, 0:P], qkv_b[:, 2, :], start=False, stop=True,
                                   skip_group_check=True)
                    if s % 2:
                        mm.then_inc(proj_ready.by(f"v{s // 2}"), 1)
                turn(i, "c", 0)
                if fill:
                    for half_ in range(2):
                        step_first(i - 1, IN_BETWEEN[1], half_)
                pe.wait_ge(lo["xc"].sem, lo["xc"].at(i, KT - 1))
                pe.wait_ge(lo["v1"].sem, lo["v1"].at(i, 1))
                for m in range(2):
                    wide(2 + m, "q_w", m, XT, qkv_b[:, 0, m * P:(m + 1) * P], ones_q[:, :])\
                        .then_inc(proj_ready.by(f"q{m}"), 1)
                if fill:
                    for half_ in range(2):
                        step_second(i - 1, IN_BETWEEN[0], half_)
                    pe.wait_ge(acted.sem, acted.at(i - 1, slices(IN_BETWEEN[1])[-1]))
                pe.wait_ge(lo["qc"].sem, lo["qc"].at(i, KT - 1))
                attention(i, 1, following, fill)
                if following:
                    first_scores(i + 1)
                if fill:
                    step_second(i - 1, STEPS - 1, 0)
                if following:
                    turn_maxima(i + 1, 0, 0)
                if fill:
                    step_second(i - 1, STEPS - 1, 1)

            def first_scores(i):
                pe.wait_ge(lo["qa"].sem, lo["qa"].at(i, KT - 1))
                pe.wait_ge(lo["ct"].sem, lo["ct"].at(i, KT - 1))
                scores(i, 0, 0)

            for t in range(KT):
                turn_context(0, t)
            turn(0, "a", 0)
            first_scores(0)
            turn_maxima(0, 0, 0)
            group(0, True, False)
            with pe.Fori(1, groups - 1) as i:
                group(i, True, True)
            group(groups - 1, False, True)
            turn(groups - 1, "d", G)
            pe.wait_ge(lo["xd"].sem, lo["xd"].at(groups - 1, KT - 1))
            logits(groups - 1, "d", "router_w", XD, G)
            for j in range(STEPS + 1):
                for half_ in range(2):
                    if j < STEPS:
                        step_first(groups - 1, j, half_)
                    if j and half_ < len(slices(j - 1)):
                        step_second(groups - 1, j - 1, half_)

        @block.scalar
        def _(act):
            act.wait_ge(small_loaded, 16 * 14)
            act.activation(tg[:, :], gates4[:, :], ACT.Tanh).then_inc(tg_ready, 1)
            for c, names in enumerate(CHUNKS):
                n = sum(W_COLS[x_][1] for x_ in names)
                base = W_COLS[names[0]][0]
                act.wait_ge(w_loaded[c], 16 * len(names))
                if c == 0:
                    act.wait_ge(w1_scaled, 1)
                act.activation(WH[:, base:base + n], stage[c % 2][:, 0:n], ACT.Copy, scale=S_W)\
                    .then_inc(w_high, 1)
            act.wait_ge(setup_done, 1)

            def high(name, t, o_, i_, scale):
                act.activation(o_, i_, ACT.Copy, scale=scale).then_inc(hi[name].by(t), 1)

            def query_high(name, l, t, bank):
                for e in range(2):
                    ins = act.activation(Q[l][0][:, t, e, :], ps[:, bank, :], ACT.Identity,
                                         scale=half[:, l, e:e + 1])
                ins.then_inc(hi[name].by(t), 1)

            def attention(i, l, following, fill):
                scale = 0.25 / (S_XW if l == 0 else S_WW)
                for v in range(UNITS + 2):
                    if v < UNITS:
                        src = ps[:, ST[v % 2], :]
                        bias = lnP[:, :] if l == 0 else key_bias[:, v // 4:v // 4 + 1]
                        act.wait_ge(st_ready.sem, st_ready.at(i, (l, v)))
                        if v >= 4:
                            act.wait_ge(av_done.sem, av_done.at(i, (l, v - 4)))
                        elif l == 0 and fill:
                            act.wait_ge(av_done.sem, av_done.at(i - 1, (1, v + UNITS - 4)))
                        act.activation(P32[:, v % 4, :], src, ACT.Exp, bias=bias, scale=scale)\
                            .then_inc(exp_done.by((l, v, 0)), 1)
                        act.activation(PH[:, v % 4, :], src, ACT.Exp, bias=bias, scale=scale)\
                            .then_inc(exp_done.by((l, v, 1)), 1)
                    if fill:
                        if l == 0 and v == 0:
                            turned(i - 1, "d", XD, G)
                        if l == 0 and v == 2:
                            router_tanh(i - 1)
                        j = step_at(l, v, 0)
                        if j is not None:
                            step_activation(i - 1, j)
                        j = step_at(l, v, 2)
                        if j is not None and j < HTS:
                            shared_high(i - 1, j)
                    if following and l == 1:
                        if v == 0:
                            context_high(i + 1)
                        if v == 2:
                            high("v0", 0, V[0][0][:, :, 0:HD],
                                 ctx_in[:, :, :].rearrange("p s (h d) -> p (s h) d", d=HD), S_W)

            def step_activation(g, j):
                for n in slices(j):
                    act.wait_ge(g1.sem, g1.at(g, n))
                    if n >= 2:
                        act.wait_ge(hid_lo.sem, hid_lo.at(g, n - 2))
                    func, scale = (ACT.Tanh, 0.5 / S_XW) if n < HTS else (ACT.Gelu, 1 / S_XW)
                    bank = G if n < HTS else G + n % 2
                    act.activation(h32[:, n % 2, :], ps[:, bank, :], func, scale=scale).then_inc(acted.by(n), 1)
                if j >= HTS:
                    for n in slices(j):
                        act.wait_ge(acted.sem, acted.at(g, n))
                        act.wait_ge(g2.sem, g2.at(g, n - 4))
                        act.activation(HH[:, n % 4, :], h32[:, n % 2, :], ACT.Copy, scale=S_W)\
                            .then_inc(hid_hi.by(n), 1)

            def shared_high(g, j):
                act.wait_ge(prod.sem, prod.at(g, j))
                act.activation(HH[:, j % 4, :], v32[:, j % 2, :], ACT.Copy, scale=0.5 * S_W / (S_XW * S_XW))\
                    .then_inc(hid_hi.by(j), 1)

            def turned(i, f, dst, first):
                for t in range(KT):
                    act.wait_ge(xt_ready[f].sem, xt_ready[f].at(i, t))
                    high("x" + f, t, dst[0][:, t, :], ps[:, first + t, :], S_X)

            def router_tanh(i):
                act.wait_ge(lg_ready["d"].sem, lg_ready["d"].at(i, 0))
                act.activation(lg[:, :, :].rearrange("p s e -> p (s e)"), lgp(G), ACT.Tanh, scale=0.5 / S_XW)\
                    .then_inc(lg_tanh.by(0), 1)

            def context_high(i):
                for t in range(KT):
                    act.wait_ge(ct_ready.sem, ct_ready.at(i, t))
                    high("ct", t, CT[0][:, t, :], ps[:, G + t, :], S_W)

            def prepare_queries(i):
                for t in range(KT):
                    act.wait_ge(xt_ready["a"].sem, xt_ready["a"].at(i, t))
                    query_high("qa", 0, t, t)

            def group(i, following, fill):
                attention(i, 0, following, fill)
                def key_high(m):
                    act.wait_ge(proj_ready.sem, proj_ready.at(i, f"k{m}"))
                    high("k", m, K1[0][:, m, :], ps[:, 6 + m, :], 1 / S_W)

                key_high(0)
                turned(i, "b", XT, 0)
                key_high(1)
                act.wait_ge(tokp_ready.sem, tokp_ready.at(i, 0))
                act.activation(tokT[:, :], token_bank(6), ACT.Copy).then_inc(tokT_ready.by(0), 1)
                if following:
                    prepare_queries(i + 1)
                for n in range(HT0 + 1):
                    if n < HT0:
                        act.wait_ge(e_g1.sem, e_g1.at(i, n))
                        act.activation(P32[:, n, :], ps[:, G0[n], :], ACT.Gelu, bias=b1e[:, n:n + 1],
                                       scale=1 / S_XW).then_inc(e_act.by(n), 1)
                    if n:
                        act.wait_ge(e_act.sem, e_act.at(i, n - 1))
                        act.activation(PH[:, n - 1, :], P32[:, n - 1, :], ACT.Copy, scale=S_W)\
                            .then_inc(e_hi.by(n - 1), 1)
                if fill:
                    step_activation(i - 1, IN_BETWEEN[0])
                for m in range(2):
                    act.wait_ge(proj_ready.sem, proj_ready.at(i, f"v{m}"))
                    high("v1", m, V[1][0][:, 32 * m:32 * m + 32, 0:HD],
                         ps[:, 2 + m, :].rearrange("p (h d) -> p h d", d=HD), 1 / S_W)
                turned(i, "c", XT, 0)
                for m in range(2):
                    act.wait_ge(proj_ready.sem, proj_ready.at(i, f"q{m}"))
                    query_high("qc", 1, m, 2 + m)
                if fill:
                    step_activation(i - 1, IN_BETWEEN[1])
                attention(i, 1, following, fill)

            act.wait_ge(ctx_loaded.sem, ctx_loaded.at(0, "ctx"))
            high("v0", 0, V[0][0][:, :, 0:HD], ctx_in[:, :, :].rearrange("p s (h d) -> p (s h) d", d=HD), S_W)
            context_high(0)
            prepare_queries(0)
            group(0, True, False)
            with act.Fori(1, groups - 1) as i:
                group(i, True, True)
            group(groups - 1, False, True)
            turned(groups - 1, "d", XD, G)
            router_tanh(groups - 1)
            for j in range(STEPS):
                step_activation(groups - 1, j)
                if j < HTS:
                    shared_high(groups - 1, j)

        @block.vector
        def _(dve):
            chain = Chain(dve, dve_step, DVE_LINKS, DVE_SETUP)
            prep = Chain(dve, dve_prep_step, DVE_PREP_LINKS)
            router = Chain(dve, dve_router_step, DVE_ROUTER_LINKS)
            link = chain.link
            dve.memset(lnP[:, :], 5.545177444479562)
            dve.wait_ge(consts_made, N_CONSTS)
            link(dve.tensor_copy(iota8[:, :], iota8i[:, :]))
            for c, shift in ((1, 4), (2, 3), (3, 0)):
                link(dve.tensor_scalar(pi[:, c:c + 1], pi[:, 0:1], shift, 1, ALU.logical_shift_right,
                                       ALU.bitwise_and))
            link(dve.tensor_copy(pf[:, :], pi[:, :]))
            for l, sc in enumerate((S_X, 1 / S_X)):
                link(dve.tensor_scalar(half[:, l, 0:1], pf[:, 1:2], -sc, sc, ALU.mult, ALU.add))
                link(dve.tensor_scalar(half[:, l, 1:2], pf[:, 1:2], sc, None, ALU.mult))
            link(dve.tensor_scalar(pf[:, 2:4], pf[:, 2:4], -1.0, None, ALU.mult))
            dve.wait_ge(small_loaded, 16 * 14)
            for f_, h_, o_, col, rows in ((b2f[:, :], b2h[:, :], b2[:, :], 2, 32),
                                          (bf[:, :, :].rearrange("p a d -> p (a d)"),
                                           bh[:, :, :].rearrange("p a d -> p (a d)"),
                                           qkv_b[:, :, :].rearrange("p a d -> p (a d)"), 3, 2)):
                link(dve.tensor_scalar(f_, f_, S_W, None, ALU.mult))
                link(dve.tensor_copy(h_, f_))
                link(dve.scalar_tensor_tensor(out=o_, in0=h_, scalar=pf[0:rows, col:col + 1], in1=f_,
                                              op0=ALU.mult, op1=ALU.add))
            dve.wait_ge(tg_ready, 1)
            for c in (1, 3):
                link(dve.tensor_scalar(tg[:, c:c + 1], tg[:, c:c + 1], 1 / S_WW, None, ALU.mult))
            dve.wait_ge(b1_ready, 1)
            for t in range(HT0):
                for h_ in range(2):
                    r = slice(64 * h_, 64 * h_ + 64)
                    ins = dve.tensor_tensor(b1e[r, t:t + 1], ps[r, 0, t * E + 2 * t + h_:t * E + 2 * t + h_ + 1],
                                            b1[r, t:t + 1], ALU.add)
                    if h_ and t == HT0 - 1:
                        link(ins)
            at = W_COLS["W1"][0]
            w1v = stage[0][:, at:at + KT * HT0 * P].rearrange("p (t e h) -> p t e h", t=KT, e=E)
            for t in range(KT):
                ins = dve.tensor_tensor(w1v[:, t, :, :], w1v[:, t, :, :],
                                        ln_s[:, t, :].unsqueeze(2).to_broadcast([P, E, 64]), ALU.mult)
            ins.then_inc(w1_scaled, 1)
            dve.wait_ge(w1_scaled, 1)
            for c, names in enumerate(CHUNKS):
                n = sum(W_COLS[x_][1] for x_ in names)
                base = W_COLS[names[0]][0]
                dve.wait_ge(w_high, c + 1)
                ins = dve.scalar_tensor_tensor(out=WL[:, base:base + n], in0=stage[c % 2][:, 0:n], scalar=S_W,
                                               in1=WH[:, base:base + n], op0=ALU.mult, op1=ALU.subtract)
                ins.then_inc(w_low, 1)
            dve.wait_ge(w_low, len(CHUNKS))
            assert chain.done == DVE_SETUP, f"DVE_SETUP {chain.done}"
            dve.memset(idle[:, :], 0.0).then_inc(setup_done, 1)

            def low(i, name, t, o_, src, scale, h_):
                dve.wait_ge(hi[name].sem, hi[name].at(i, t))
                dve.scalar_tensor_tensor(out=o_, in0=src, scalar=scale, in1=h_, op0=ALU.mult,
                                         op1=ALU.subtract).then_inc(lo[name].by(t), 1)

            def query_low(i, name, l, t, bank):
                dve.wait_ge(hi[name].sem, hi[name].at(i, t))
                for e in range(2):
                    ins = dve.scalar_tensor_tensor(out=Q[l][1][:, t, e, :], in0=ps[:, bank, :],
                                                   scalar=half[:, l, e:e + 1], in1=Q[l][0][:, t, e, :],
                                                   op0=ALU.mult, op1=ALU.subtract)
                ins.then_inc(lo[name].by(t), 1)

            def carry_wait():
                dve.memset(idle[:, :], 0.0)

            def measure(i, f, seqs, src):
                for s in seqs:
                    ins = dve.bn_stats(stats[f % 2][:, s, :], src[:, s, :])
                (prep if f == 0 else chain).link(ins)

            def aggregate(i, f, seqs):
                for s in seqs:
                    ins = dve.bn_aggr(mv[:, f, s, :], stats[f % 2][:, s, :])
                    if s == SEQS - 1:
                        ins.then_inc(stats_ready["abcd"[f]].by(0), 1)

            def normalise(i, f, src):
                ph = "abcd"[f]
                dve.wait_ge(rstd_ready[ph].sem, rstd_ready[ph].at(i, 0))
                for s in range(SEQS):
                    dve.tensor_scalar(xn[:, s, :], src[:, s, :], mv[:, f, s, 0:1], rstd[:, f, s:s + 1],
                                      ALU.subtract, ALU.mult).then_inc(xn_ready[ph].by(s), 1)

            def masks(i, l):
                link = (prep, chain)[l].link
                dve.wait_ge(m_loaded[l].sem, m_loaded[l].at(i, "m"))
                link(dve.tensor_scalar(off[:, :, :], m_in[l][:, :, :], 0.0, None,
                                       (ALU.is_equal, ALU.is_gt)[l]))
                link(dve.tensor_reduce(n_off[:, l, :], off[:, :, :], AX, ALU.add))
                link(dve.tensor_scalar(some_on[:, l, :], n_off[:, l, :], P - 0.5, None, ALU.is_lt))
                link(dve.tensor_scalar(take_off[:, l, :], some_on[:, l, :],
                                       -MASKED * (S_XW, S_WW)[l], None, ALU.mult))
                ins = dve.tensor_tensor(maskb[l][:, :, :], off[:, :, :],
                                        take_off[:, l, :].unsqueeze(2).to_broadcast([P, SEQS, P]), ALU.mult)
                if l == 0:
                    ins.then_inc(masks_made[0].by(0), 1)
                else:
                    dve.wait_ge(mk_loaded.sem, mk_loaded.at(i, "m"))
                    link(dve.tensor_scalar(key_bias[:, :], mk_in[:, :], 0.0, -0.25 * MASKED, ALU.is_gt, ALU.mult))
                    link(dve.tensor_scalar(key_bias[:, :], key_bias[:, :], lnP[:, 0:1], None, ALU.add))
                    link(dve.reciprocal(nan_row[:, :], some_on[:, 1, :]))
                    dve.tensor_tensor(nan_row[:, :], nan_row[:, :], some_on[:, 1, :], ALU.mult)\
                        .then_inc(masks_made[1].by(0), 1)

            def finish_sequence(i, l, s):
                ph = "ac"[l]
                dve.wait_ge(av_done.sem, av_done.at(i, (l, 4 * s + 3)))
                link(dve.reciprocal(rden[:, :], O[:, :, HD]))
                if l == 1:
                    link(dve.tensor_scalar(rden[:, :], rden[:, :], nan_row[:, s:s + 1], None, ALU.mult))
                dve.tensor_tensor(att[:, :].rearrange("p (h d) -> p h d", d=HD), O[:, :, 0:HD],
                                  rden[:, :].unsqueeze(2).to_broadcast([P, HEADS, HD]), ALU.mult)\
                    .then_inc(o_read.by((l, s)), 1)
                if l == 0 and s == 0:
                    dve.wait_ge(x_moved.sem, x_moved.at(i, 0))
                dve.wait_ge(o_read.sem, o_read.at(i, (l, s)))
                dve.scalar_tensor_tensor(out=x[:, s, :], in0=att[:, :], scalar=tg[:, 2 * l:2 * l + 1],
                                         in1=x[:, s, :], op0=ALU.mult, op1=ALU.add)\
                    .then_inc(resid.by((ph, s)), 1)
                dve.wait_ge(resid.sem, resid.at(i, (ph, s)))
                measure(i, 2 * l + 1, [s], x)
                carry_wait()
                aggregate(i, 2 * l + 1, [s])

            def maxima(i, l, u):
                dve.wait_ge(s_ready.sem, s_ready.at(i, (l, u)))
                dve.tensor_reduce(negmax[:, u % 2, :], ps[:, SQ, :].rearrange("p (c k) -> p c k", c=4), AX,
                                  ALU.max, negate=True).then_inc(max_done.by((l, u)), 1)

            def copy_maxima(i, l, u):
                dve.wait_ge(t_ready.sem, t_ready.at(i, (l, u)))
                dve.tensor_copy(mT[0:4, u % 2, :], maxT).then_inc(mt_ready.by((l, u)), 1)

            def attention(i, l, following, fill):
                for u in range(1 - l, UNITS + AV_LAG):
                    if u < UNITS:
                        maxima(i, l, u)
                    if fill:
                        beside_turning(i - 1, l, u)
                    if following and l == 1 and u == 2:
                        context_low(i + 1)
                    if u < UNITS:
                        copy_maxima(i, l, u)
                    j = step_at(l, u, 2)
                    if fill and j is not None and j < HTS:
                        swiglu_product(i - 1, j)
                    if PL_LAG <= u < UNITS + PL_LAG:
                        v = u - PL_LAG
                        dve.wait_ge(exp_done.sem, exp_done.at(i, (l, v, 1)))
                        dve.tensor_tensor(PL[:, v % 4, :], P32[:, v % 4, :], PH[:, v % 4, :], ALU.subtract)\
                            .then_inc(plo_done.by((l, v)), 1)
                    done, last = divmod(u + 1 - AV_LAG, 4)
                    if done and last == 0:
                        finish_sequence(i, l, done - 1)
                    if fill:
                        if l == 0 and u in GATES_AT:
                            gate_rows(i - 1, GATES_AT.index(u))
                        if l == 1 and u == 0:
                            add_sums(i - 1, 1 + IN_BETWEEN[0] - HTS)
                    if l == 0 and following and u == 17:
                        dve.wait_ge(x_loaded.sem, x_loaded.at(i + 1, "x"))
                        measure(i + 1, 0, range(SEQS), x_in)
                        carry_wait()
                        aggregate(i + 1, 0, range(SEQS))
                    if l == 1 and following and u == 5:
                        low(i + 1, "v0", 0, V[0][1][:, :, 0:HD],
                            ctx_in[:, :, :].rearrange("p s (h d) -> p (s h) d", d=HD), S_W, V[0][0][:, :, 0:HD])

            def beside_turning(g, l, u):
                if l == 0 and u == 2:
                    turned_low(g, "d", XD, G)
                j = step_at(l, u, 3)
                if j is not None and j >= HTS and u:
                    step_low(g, j)
                j = step_at(l, u, 4)
                if j is not None and (j < HTS or u == 1):
                    step_low(g, j)
                j = step_at(l, u, 7)
                if j is not None and j >= HTS:
                    add_sums(g, 1 + j - HTS)

            def swiglu_product(g, n):
                dve.wait_ge(acted.sem, acted.at(g, n))
                dve.scalar_tensor_tensor(out=v32[:, n % 2, :], in0=h32[:, n % 2, :], scalar=1.0,
                                         in1=ps[:, G, :], op0=ALU.add, op1=ALU.mult)\
                    .then_inc(silu_half.by(n), 1)
                dve.wait_ge(silu_half.sem, silu_half.at(g, n))
                dve.tensor_tensor(v32[:, n % 2, :], v32[:, n % 2, :], ps[:, G + 1, :], ALU.mult)\
                    .then_inc(prod.by(n), 1)

            def step_low(g, j):
                for n in slices(j):
                    dve.wait_ge(hid_hi.sem, hid_hi.at(g, n))
                    src_, scale = (v32, 0.5 * S_W / (S_XW * S_XW)) if n < HTS else (h32, S_W)
                    dve.scalar_tensor_tensor(out=HL[:, n % 4, :], in0=src_[:, n % 2, :], scalar=scale,
                                             in1=HH[:, n % 4, :], op0=ALU.mult, op1=ALU.subtract)\
                        .then_inc(hid_lo.by(n), 1)

            def add_sums(g, k):
                dve.wait_ge(g2.sem, g2.at(g, HTS - 1 if k == 0 else HTS + 2 * k - 1))
                if k == 0:
                    dve.wait_ge(x_kept.sem, x_kept.at(g, 0))
                    dve.wait_ge(out_stored.sem, out_stored.before(g + 1))
                else:
                    dve.wait_ge(summed.sem, summed.at(g, k - 1))
                    if k == 1:
                        dve.wait_ge(gates_ready.sem, gates_ready.at(g, 0))
                for s in range(SEQS):
                    ins = dve.scalar_tensor_tensor(
                        out=x_out[:, s, :], in0=y(s, Y), scalar=gates[:, s, k - 1:k] if k else tg[:, 3:4],
                        in1=(x_out if k else x_ffn)[:, s, :], op0=ALU.mult, op1=ALU.add)
                ins.then_inc(summed.by(k), 1)

            def choose(values, link):
                carry_wait()
                for s in range(SEQS):
                    ins = dve.max(top8[:, s, :], values[:, s, :])
                link(ins)
                carry_wait()
                for s in range(SEQS):
                    ins = dve.max_index(topi[:, s, :], top8[:, s, :], values[:, s, :])
                link(ins)
                link(dve.tensor_copy(topf[:, :, :], topi[:, :, :]))

            def one_hot(dst, k):
                return dve.tensor_tensor(dst[:, :, :], iota8[:, :].unsqueeze(1).to_broadcast([P, SEQS, E]),
                                         topf[:, :, k:k + 1].to_broadcast([P, SEQS, E]), ALU.is_equal)

            def top1_rows(i):
                dve.wait_ge(lg_ready["b"].sem, lg_ready["b"].at(i, 0))
                link(dve.tensor_copy(lg[:, :, :].rearrange("p s e -> p (s e)"), lgp(6)))
                choose(lg, link)
                link(one_hot(oh, 0))
                dve.tensor_scalar(tokens[:, :, 0:8], oh[:, :, :], S_W, None, ALU.mult)
                dve.tensor_scalar(tokens[:, :, 8:16], oh[:, :, :], S_W, None, ALU.mult)
                dve.tensor_scalar(tokens[:, :, 16:24], oh[:, :, :], 1.0, OFF_EXPERT, ALU.subtract, ALU.mult)\
                    .then_inc(tok_ready.by(0), 1)

            def gate_rows(i, part):
                link = router.link
                if part == 0:
                    router.group(i)
                    dve.wait_ge(lg_tanh.sem, lg_tanh.at(i, 0))
                    link(dve.tensor_scalar(sig[:, :, :], lg[:, :, :], 0.5, 0.5, ALU.mult, ALU.add))
                    link(dve.tensor_tensor(oh2[:, :, :], sig[:, :, :],
                                           rb[:, :].unsqueeze(1).to_broadcast([P, SEQS, E]), ALU.add))
                    choose(oh2, link)
                elif part == 1:
                    link(one_hot(oh, 0))
                    link(one_hot(oh2, 1))
                    link(dve.tensor_tensor(oh[:, :, :], oh[:, :, :], oh2[:, :, :], ALU.add))
                    link(dve.tensor_tensor(sig[:, :, :], sig[:, :, :], oh[:, :, :], ALU.mult))
                    link(dve.tensor_reduce(den[:, 0, :], sig[:, :, :], AX, ALU.add))
                    link(dve.tensor_scalar(den[:, 1, :], den[:, 0, :], 1e-9, None, ALU.add))
                    link(dve.reciprocal(den[:, 2, :], den[:, 1, :]))
                else:
                    link(dve.tensor_scalar(den[:, 3, :], den[:, 0, :], 1e-9, None, ALU.is_gt))
                    link(dve.tensor_tensor(den[:, 2, :], den[:, 2, :], den[:, 3, :], ALU.mult))
                    link(dve.tensor_scalar(den[:, 4, :], den[:, 3, :], -0.5, 0.5, ALU.mult, ALU.add))
                    link(dve.tensor_tensor(sig[:, :, :], sig[:, :, :],
                                           den[:, 2, :].unsqueeze(2).to_broadcast([P, SEQS, E]), ALU.mult))
                    link(dve.tensor_tensor(oh[:, :, :], oh[:, :, :],
                                           den[:, 4, :].unsqueeze(2).to_broadcast([P, SEQS, E]), ALU.mult))
                    link(dve.tensor_tensor(sig[:, :, :], sig[:, :, :], oh[:, :, :], ALU.add))
                    dve.tensor_scalar(gates[:, :, :], sig[:, :, :], tg[:, 3:4], None, ALU.mult)\
                        .then_inc(gates_ready.by(0), 1)

            def turned_low(i, f, dst, first):
                for t in range(KT):
                    low(i, "x" + f, t, dst[1][:, t, :], ps[:, first + t, :], S_X, dst[0][:, t, :])

            def context_low(i):
                for t in range(KT):
                    low(i, "ct", t, CT[1][:, t, :], ps[:, G + t, :], S_W, CT[0][:, t, :])

            def group(i, following, fill):
                chain.group(i)
                if following:
                    prep.group(i + 1)
                attention(i, 0, following, fill)
                if fill:
                    add_sums(i - 1, 0)
                normalise(i, 1, x)
                if following:
                    masks(i + 1, 0)
                low(i, "k", 0, K1[1][:, 0, :], ps[:, 6, :], 1 / S_W, K1[0][:, 0, :])
                turned_low(i, "b", XT, 0)
                low(i, "k", 1, K1[1][:, 1, :], ps[:, 7, :], 1 / S_W, K1[0][:, 1, :])
                top1_rows(i)
                if following:
                    normalise(i + 1, 0, x_in)
                masks(i, 1)
                if following:
                    for t in range(KT):
                        query_low(i + 1, "qa", 0, t, t)
                for n in range(HT0):
                    dve.wait_ge(e_hi.sem, e_hi.at(i, n))
                    dve.scalar_tensor_tensor(out=PL[:, n, :], in0=P32[:, n, :], scalar=S_W, in1=PH[:, n, :],
                                             op0=ALU.mult, op1=ALU.subtract).then_inc(e_lo.by(n), 1)
                if fill:
                    add_sums(i - 1, 1)
                for m in range(2):
                    dve.wait_ge(e_sums.sem, e_sums.at(i, m))
                    both = range(2 * m, 2 * m + 2)
                    for s in both:
                        dve.scalar_tensor_tensor(out=x[:, s, :], in0=y(s, 0), scalar=tg[:, 1:2], in1=x[:, s, :],
                                                 op0=ALU.mult, op1=ALU.add).then_inc(resid.by(("b", s)), 1)
                    dve.wait_ge(resid.sem, resid.at(i, ("b", both[-1])))
                    measure(i, 2, both, x)
                carry_wait()
                aggregate(i, 2, range(SEQS))
                normalise(i, 2, x)
                if fill:
                    step_low(i - 1, IN_BETWEEN[0])
                for m in range(2):
                    low(i, "v1", m, V[1][1][:, 32 * m:32 * m + 32, 0:HD],
                        ps[:, 2 + m, :].rearrange("p (h d) -> p h d", d=HD), 1 / S_W,
                        V[1][0][:, 32 * m:32 * m + 32, 0:HD])
                turned_low(i, "c", XT, 0)
                for m in range(2):
                    query_low(i, "qc", 1, m, 2 + m)
                attention(i, 1, following, fill)
                if following:
                    maxima(i + 1, 0, 0)
                    copy_maxima(i + 1, 0, 0)
                    normalise(i, 3, x)
                if fill:
                    add_sums(i - 1, E)

            prep.group(0)
            dve.wait_ge(x_loaded.sem, x_loaded.at(0, "x"))
            measure(0, 0, range(SEQS), x_in)
            carry_wait()
            aggregate(0, 0, range(SEQS))
            masks(0, 0)
            low(0, "v0", 0, V[0][1][:, :, 0:HD], ctx_in[:, :, :].rearrange("p s (h d) -> p (s h) d", d=HD), S_W,
                V[0][0][:, :, 0:HD])
            normalise(0, 0, x_in)
            context_low(0)
            for t in range(KT):
                query_low(0, "qa", 0, t, t)
            maxima(0, 0, 0)
            copy_maxima(0, 0, 0)
            group(0, True, False)
            with dve.Fori(1, groups - 1) as i:
                group(i, True, True)
            group(groups - 1, False, True)
            normalise(groups - 1, 3, x)
            turned_low(groups - 1, "d", XD, G)
            for part in range(3):
                gate_rows(groups - 1, part)
            for j in range(STEPS):
                if j < HTS:
                    swiglu_product(groups - 1, j)
                step_low(groups - 1, j)
                if j >= HTS - 1:
                    add_sums(groups - 1, j - HTS + 1)


def kernel(**inputs):
    import numpy as np
    import concourse.bacc as bacc
    from concourse.bass_utils import run_bass_kernel_spmd

    v = {k: np.asarray(t) for k, t in inputs.items()}
    arrays = {
        "x": v["x"], "ctx": v["ctx_1024"], "mask0": v["mask_Bx1xSxS2_ik1"], "mask1": v["mask_BxS2_ik0"],
        "mask1_keys": v["mask_BxS2_ik0"].T,
        "g": np.stack([np.stack([v["g_xattn"][l], v["g_ffn"][l]]) for l in range(2)]),
        "Wg": v["L0_ffn_Wg"].T, "ln_s": v["L0_ffn_ln_scale"].T, "ln_b": v["L0_ffn_ln_bias"].T,
        "W1": v["L0_ffn_W1"].transpose(1, 0, 2).reshape(D, HT0 * P),
        "b1": v["L0_ffn_b1"].reshape(HT0, P).T,
        "W2": v["L0_ffn_W2"].reshape(HT0 * P, D), "b2": v["L0_ffn_b2"],
        "q_w": v["L1_xattn_q_w"].T, "k_w": v["L1_xattn_k_w"].T, "v_w": v["L1_xattn_v_w"].T,
        "q_b": v["L1_xattn_q_b"], "k_b": v["L1_xattn_k_b"], "v_b": v["L1_xattn_v_b"],
        "router_w": v["L1_ffn_router_w"].T, "router_b": v["L1_ffn_router_bias"],
        "sw1": v["L1_ffn_sw1"], "sw3": v["L1_ffn_sw3"], "sw2": v["L1_ffn_sw2"],
        "ew1": v["L1_ffn_ew1"].transpose(1, 0, 2).reshape(D, HTR * P),
        "ew2": v["L1_ffn_ew2"].reshape(HTR * P, D),
    }
    nc = bacc.Bacc("TRN2", target_bir_lowering=False, num_devices=1)
    feeds, aps = {}, {}
    for name, t in arrays.items():
        t = np.ascontiguousarray(t)
        feeds[f"in_{name}"] = t
        aps[name] = nc.dram_tensor(f"in_{name}", t.shape, mybir.dt.from_np(t.dtype), kind="ExternalInput").ap()
    out = nc.dram_tensor("out", v["x"].shape, F32, kind="ExternalOutput").ap()
    build(nc, aps, out)
    r = run_bass_kernel_spmd(nc, [feeds], core_ids=[0])
    return r.results[0]["out"]
```

```python
from contextlib import ExitStack

import concourse.bass as bass
from concourse import mybir

F32 = mybir.dt.float32
F16 = mybir.dt.float16
BF16 = mybir.dt.bfloat16
I32 = mybir.dt.int32
U32 = mybir.dt.uint32
ALU = mybir.AluOpType
ACT = mybir.ActivationFunctionType
AX = mybir.AxisListType.X

P = 128
D = 256
KT = D // P
SEQS = 4
TOK = SEQS * P
HEADS = 16
HD = D // HEADS
VW = HD + 1
E = 8
HT0 = 4
HTS = 4
HTR = 16
HTD = HTS + HTR
UNITS = 4 * SEQS
PL_LAG, AV_LAG = 3, 4
STEPS = HTS + E
START = {0: {3: 0, 6: 1, 9: 2, 12: 3, 15: 4}, 1: {3: 7, 6: 8, 9: 9, 12: 10, 15: 11}}
IN_BETWEEN = (5, 6)
START[1][-3] = 6
GATES_AT = (6, 9)

LN_EPS = 1e-5
S_X = 2.0 ** 11
S_W = 2.0 ** 8
S_XW = S_X * S_W
S_WW = S_W * S_W
S_P = 2.0 ** 8
MASKED = 120000.0
OFF_EXPERT = 2.0 ** 15


class Signal:

    def __init__(self, sem, events, step=1):
        self.sem, self.events, self.step, self.turn = sem, list(events), step, 0

    def by(self, event):
        assert self.events[self.turn % len(self.events)] == event, (self.events[self.turn % len(self.events)], event)
        self.turn += 1
        return self.sem

    def at(self, i, event):
        return i * (len(self.events) * self.step) + (self.events.index(event) + 1) * self.step

    def before(self, i):
        return i * (len(self.events) * self.step)


class Chain:

    def __init__(self, eng, sem, per_group, setup=0):
        self.eng, self.sem, self.per_group, self.setup = eng, sem, per_group, setup
        self.i, self.done = None, 0

    def group(self, i):
        assert self.i is None or self.done == self.setup + self.per_group, (self.done - self.setup, self.per_group)
        self.i, self.done = i, self.setup

    def link(self, ins):
        ins.then_inc(self.sem, 1)
        self.done += 1
        if self.i is None:
            self.eng.wait_ge(self.sem, self.done)
        else:
            self.eng.wait_ge(self.sem, self.i * self.per_group + self.done)


W_COLS = {}
_at = 0
for _name, _n in (("q_w", KT * D), ("k_w", KT * D), ("v_w", KT * D), ("W1", KT * HT0 * P), ("W2", HT0 * D),
                  ("Wg", KT * E), ("router_w", KT * E), ("sw1", KT * HTS * P), ("sw3", KT * HTS * P),
                  ("sw2", HTS * D), ("ew1", KT * HTR * P), ("ew2", HTR * D)):
    W_COLS[_name] = (_at, _n)
    _at += _n
W_TOTAL = _at
CHUNKS = [("q_w", "k_w", "v_w", "W1", "W2", "Wg", "router_w"), ("sw1", "sw3", "sw2"), ("ew1",), ("ew2",)]
STAGE = 4096
DVE_SETUP, DVE_LINKS, DVE_PREP_LINKS, DVE_ROUTER_LINKS = 19, 33, 4, 18
POOL_LINKS, POOL_PREP_LINKS = 4, 2


def build(nc, a, out):
    seqs = a["x"].shape[0]
    groups = seqs // SEQS
    assert a["x"].shape == (seqs, P, D) and seqs % SEQS == 0

    with ExitStack() as ctx:
        def sb(name, shape, dt):
            return ctx.enter_context(nc.sbuf_tensor(name, shape, dt))

        def sem(name):
            return ctx.enter_context(nc.semaphore(name))

        def signal(name, events, step=1):
            return Signal(sem(name), events, step)

        WH = sb("WH", [P, W_TOTAL], F16)
        WL = sb("WL", [P, W_TOTAL], F16)
        attn_arena = sb("attn_arena", [P, STAGE], F32)
        hid_arena = sb("hid_arena", [P, STAGE], F32)
        stage = [attn_arena, hid_arena]
        P32 = attn_arena[:, 0:2048].rearrange("p (b n) -> p b n", b=4)
        PH = attn_arena[:, 2048:3072].bitcast(F16).rearrange("p (b n) -> p b n", b=4)
        PL = attn_arena[:, 3072:4096].bitcast(F16).rearrange("p (b n) -> p b n", b=4)
        h32 = hid_arena[:, 0:1024].rearrange("p (b n) -> p b n", b=2)
        v32 = hid_arena[:, 1024:2048].rearrange("p (b n) -> p b n", b=2)
        HH = hid_arena[:, 2048:3072].bitcast(F16).rearrange("p (b n) -> p b n", b=4)
        HL = hid_arena[:, 3072:4096].bitcast(F16).rearrange("p (b n) -> p b n", b=4)

        x_in = sb("x_in", [P, SEQS, D], F32)
        x = sb("x_res", [P, SEQS, D], F32)
        x_ffn = sb("x_ffn", [P, SEQS, D], F32)
        x_out = sb("x_out", [P, SEQS, D], F32)
        ctx_in = sb("ctx_in", [P, SEQS, D], F32)
        m_in = [sb(f"mask{l}_in", [P, SEQS, P], I32) for l in range(2)]
        mk_in = sb("mask1_keys_in", [P, SEQS], I32)
        key_bias = sb("key_bias", [P, SEQS], F32)
        off = [sb(f"off{l}", [P, SEQS, P], F32) for l in range(2)]
        n_off = sb("n_off", [P, 2, SEQS], F32)
        some_on = sb("some_on", [P, 2, SEQS], F32)
        take_off = sb("take_off", [P, 2, SEQS], F32)
        nan_row = sb("nan_row", [P, SEQS], F32)
        maskb = [sb(f"mask_bias{l}", [P, SEQS, P], BF16) for l in range(2)]
        xn = sb("xn", [P, SEQS, D], F32)
        xn_a = sb("xn_first", [P, SEQS, D], F32)
        XT = [sb(f"XT_{h}", [P, KT, TOK], F16) for h in "hl"]
        XD = [sb(f"XD_{h}", [P, KT, TOK], F16) for h in "hl"]
        CT = [sb(f"CT_{h}", [P, KT, TOK], F16) for h in "hl"]
        K1 = [sb(f"K1_{h}", [P, KT, TOK], F16) for h in "hl"]
        Q = [[sb(f"Q{l}_{h}", [P, KT, 2, TOK], F16) for h in "hl"] for l in range(2)]
        V = [[sb(f"V{l}_{h}", [P, SEQS * HEADS, VW], F16) for h in "hl"] for l in range(2)]
        stats = [sb(f"stats{h}", [P, SEQS, 6], F32) for h in range(2)]
        mv = sb("mv", [P, 4, SEQS, 2], F32)
        rstd = sb("rstd", [P, 4, SEQS], F32)
        ptmp = [sb(f"ptmp{f}", [P, 3, SEQS], F32) for f in range(4)]
        negmax = sb("negmax", [P, 2, 4], BF16)
        mT = sb("mT", [P, 2, P], BF16)
        rden = sb("rden", [P, HEADS], F32)
        att = sb("att", [P, D], F32)
        lg = sb("lg", [P, SEQS, E], F32)
        top8 = sb("top8", [P, SEQS, 8], F32)
        topi = sb("topi", [P, SEQS, 8], U32)
        topf = sb("topf", [P, SEQS, 8], F32)
        oh = sb("oh", [P, SEQS, E], F32)
        oh2 = sb("oh2", [P, SEQS, E], F32)
        sig = sb("sig", [P, SEQS, E], F32)
        gates = sb("gates", [P, SEQS, E], F32)
        den = sb("den", [P, 5, SEQS], F32)
        idle = sb("idle", [P, 1], F32)
        tokens = sb("tokens", [P, SEQS, 32], F16)
        tokT = sb("tokT", [32, TOK], F16)

        id32 = sb("id32", [P, P], F32)
        id16 = sb("id16", [P, P], F16)
        idb = sb("idb", [P, P], BF16)
        pick = sb("pick", [P, 4, P], BF16)
        expert_of = sb("expert_of", [32, E, 64], F16)
        iota8 = sb("iota8", [P, E], F32)
        iota8i = sb("iota8i", [P, E], I32)
        pi = sb("pi", [P, 4], I32)
        pf = sb("pf", [P, 4], F32)
        half = sb("half", [P, 2, 2], F32)
        c_eps = sb("c_eps", [P, SEQS], F32)
        c_1eps = sb("c_1eps", [P, SEQS], F32)
        c_eps2 = sb("c_eps2", [P, SEQS], F32)
        c_mhalf = sb("c_mhalf", [P, SEQS], F32)
        lnP = sb("lnP", [P, 1], F32)
        ones_q = sb("ones_q", [2, TOK], F16)
        ones_kv = sb("ones_kv", [2, TOK], F16)
        gates4 = sb("gates4", [P, 4], F32)
        tg = sb("tg", [P, 4], F32)
        ln_s = sb("ln_s", [P, KT, E], F32)
        ln_b = sb("ln_b", [P, KT, E], F32)
        b1 = sb("b1", [P, HT0], F32)
        b1e = sb("b1e", [P, HT0], F32)
        b2f = sb("b2f", [32, D], F32)
        b2h = sb("b2h", [32, D], F16)
        b2 = sb("b2", [32, D], F16)
        bf = sb("bf", [2, 3, D], F32)
        bh = sb("bh", [2, 3, D], F16)
        qkv_b = sb("qkv_b", [2, 3, D], F16)
        rb = sb("rb", [P, E], F32)

        ps = ctx.enter_context(nc.psum_tensor("ps", [P, 8, 512], F32))
        ST, SQ, OB = (0, 1), 2, 3
        Y = 4
        G = 6
        G0 = (7, 2, 3, 6)

        def by_heads(b):
            return ps[:, b, :].rearrange("p (t e q) -> p t e q", t=KT, e=2)

        O = ps[:, OB, 0:HEADS * VW].rearrange("p (h w) -> p h w", h=HEADS)
        maxT = ps[0:4, SQ, 0:64].bitcast(BF16)

        def token_bank(b):
            return ps[0:32, b, 0:256].bitcast(F16)

        def lgp(b):
            return ps[:, b, 0:SEQS * E]

        def y(s, first):
            return ps[:, first + s // 2, (s % 2) * D:(s % 2 + 1) * D]

        def slices(j):
            return [j] if j < HTS else [2 * j - HTS, 2 * j - HTS + 1]

        def ends_sums(n):
            return n == HTS - 1 or (n >= HTS and n % 2 == 1)

        def multiplied(g, n):
            if ends_sums(n):
                return y_ready.sem, y_ready.at(g, (0 if n < HTS else 1 + (n - HTS) // 2, 1))
            return g2.sem, g2.at(g, n)

        def step_at(l, u, after):
            return START[l].get(u - after)

        w_loaded = [sem(f"w_loaded{c}") for c in range(len(CHUNKS))]
        small_loaded = sem("small_loaded")
        consts_made = sem("consts_made")
        const_step = sem("const_step")
        b1_ready = sem("b1_ready")
        w1_scaled = sem("w1_scaled")
        w_high = sem("w_high")
        w_low = sem("w_low")
        tg_ready = sem("tg_ready")
        setup_done = sem("setup_done")
        dve_step = sem("dve_step")
        pool_step = sem("pool_step")
        dve_prep_step = sem("dve_prep_step")
        dve_router_step = sem("dve_router_step")
        pool_prep_step = sem("pool_prep_step")

        x_loaded = signal("x_loaded", ["x"], 16)
        ctx_loaded = signal("ctx_loaded", ["ctx"], 16)
        m_loaded = [signal(f"mask{l}_loaded", ["m"], 16) for l in range(2)]
        mk_loaded = signal("mask1_keys_loaded", ["m"], 16)
        out_stored = signal("out_stored", ["out"], 16)

        evac = {"v0": 1, "ct": KT, "qa": KT, "xb": KT, "k": KT, "v1": 2, "xc": KT, "qc": KT, "xd": KT}
        hi = {n_: signal(f"high_{n_}", range(c)) for n_, c in evac.items()}
        lo = {n_: signal(f"low_{n_}", range(c)) for n_, c in evac.items()}
        units = [(l, u) for l in range(2) for u in range(UNITS)]
        s_ready = signal("s_ready", units)
        max_done = signal("max_done", units)
        t_ready = signal("t_ready", units)
        mt_ready = signal("mt_ready", units)
        st_ready = signal("st_ready", units)
        exp_done = signal("exp_done", [(l, u, k) for l, u in units for k in range(2)])
        plo_done = signal("plo_done", units)
        av_done = signal("av_done", units)
        o_read = signal("o_read", [(l, s) for l in range(2) for s in range(SEQS)])
        resid = signal("resid", [(f, s) for f in "abc" for s in range(SEQS)])
        x_kept = signal("x_kept", range(1))
        x_moved = signal("x_moved", range(1))
        stats_ready = {f: signal(f"stats_ready_{f}", range(1)) for f in "abcd"}
        rstd_ready = {f: signal(f"rstd_ready_{f}", range(1)) for f in "abcd"}
        xn_ready = {f: signal(f"xn_ready_{f}", range(SEQS)) for f in "abcd"}
        xt_ready = {f: signal(f"xt_ready_{f}", range(KT)) for f in "abcd"}
        ct_ready = signal("ct_ready", range(KT))
        rows_made = [signal(f"rows{l}_made", range(1)) for l in range(2)]
        masks_made = [signal(f"masks{l}_made", range(1)) for l in range(2)]
        lg_ready = {f: signal(f"logits_ready_{f}", range(1)) for f in "bd"}
        lg_tanh = signal("lg_tanh", range(1))
        gates_ready = signal("gates_ready", range(1))
        tok_ready = signal("tok_ready", range(1))
        tokp_ready = signal("tokp_ready", range(1))
        tokT_ready = signal("tokT_ready", range(1))
        proj_ready = signal("proj_ready", ["k0", "k1", "v0", "v1", "q0", "q1"])
        e_g1, e_act, e_hi, e_lo = (signal("ffn0_" + n_, range(HT0)) for n_ in ("g1", "act", "hi", "lo"))
        e_sums = signal("ffn0_sums", range(2))
        g1, acted, hid_hi, hid_lo = (signal("ffn1_" + n_, range(HTD)) for n_ in ("g1", "act", "hi", "lo"))
        g2 = signal("ffn1_g2", [n for n in range(HTD) if not ends_sums(n)])
        silu_half = signal("silu_half", range(HTS))
        prod = signal("swiglu_product", range(HTS))
        y_ready = signal("ffn1_sums", [(k, b) for k in range(1 + E) for b in range(2)])
        summed = signal("summed", [(k, b) for k in range(1 + E) for b in range(2)])

        def w(part, name, t, lo_, n, m=P):
            base, size = W_COLS[name]
            per = {"q_w": D, "k_w": D, "v_w": D, "W1": HT0 * P, "W2": D, "Wg": E, "router_w": E, "sw1": HTS * P,
                   "sw3": HTS * P, "sw2": D, "ew1": HTR * P, "ew2": D}[name]
            c = base + t * per + lo_
            return (WH, WL)[part][0:m, c:c + n]

        PARTS = ((0, 0), (0, 1), (1, 0))

        xg = a["x"].rearrange("(g s) t d -> g t s d", s=SEQS)
        og = out.rearrange("(g s) t d -> g t s d", s=SEQS)
        cg = a["ctx"].rearrange("(g s) t d -> g t s d", s=SEQS)
        m0g = a["mask0"].rearrange("(g s) o q k -> g q (s o) k", s=SEQS)
        m1g = a["mask1"].rearrange("(g s) k -> g s k", s=SEQS)
        mkg = a["mask1_keys"].rearrange("k (g s) -> g k s", s=SEQS)

        block = ctx.enter_context(nc.Block())

        @block.sync
        def _(sp):
            def load(i):
                sp.dma_start(ctx_in[:, :, :], cg[i]).then_inc(ctx_loaded.sem, 16)
                sp.dma_start(x_in[:, :, :], xg[i]).then_inc(x_loaded.sem, 16)
                sp.dma_start(m_in[0][:, :, :], m0g[i]).then_inc(m_loaded[0].sem, 16)
                sp.dma_start(m_in[1][:, :, :], m1g[i].partition_broadcast(P)).then_inc(m_loaded[1].sem, 16)
                sp.dma_start(mk_in[:, :], mkg[i]).then_inc(mk_loaded.sem, 16)

            smalls = [(ln_s[:, :, :], a["ln_s"].rearrange("(t p) e -> p t e", p=P)),
                      (ln_b[:, :, :], a["ln_b"].rearrange("(t p) e -> p t e", p=P)),
                      (b1[:, :], a["b1"]),
                      (rb[:, :], a["router_b"].partition_broadcast(P)),
                      (b2f[0:8, :], a["b2"]), (b2f[8:16, :], a["b2"])]
            smalls += [(gates4[:, 2 * j:2 * j + 2], a["g"][j].partition_broadcast(P)) for j in range(2)]
            for j, name in enumerate(("q_b", "k_b", "v_b")):
                src = a[name].rearrange("(o d) -> o d", o=1)
                smalls += [(bf[0:1, j, :], src), (bf[1:2, j, :], src)]
            sp.wait_ge(consts_made, 1)
            for dst, src in smalls:
                sp.dma_start(dst, src).then_inc(small_loaded, 16)
            for c, names in enumerate(CHUNKS):
                if c >= 2:
                    sp.wait_ge(w_high, c - 1)
                    sp.wait_ge(w_low, c - 1)
                at = 0
                for name in names:
                    n = W_COLS[name][1]
                    rows = a[name].shape[0] // P
                    src = a[name].rearrange("(t p) n -> p t n", p=P)
                    dst = stage[c % 2][:, at:at + n].rearrange("p (t n) -> p t n", t=rows)
                    sp.dma_start(dst, src).then_inc(w_loaded[c], 16)
                    at += n
                if c == 1:
                    load(0)

            def body(i):
                sp.wait_ge(lo["v0"].sem, lo["v0"].at(i, 0))
                sp.wait_ge(ct_ready.sem, ct_ready.at(i, KT - 1))
                sp.dma_start(ctx_in[:, :, :], cg[i + 1]).then_inc(ctx_loaded.sem, 16)
                sp.wait_ge(masks_made[0].sem, masks_made[0].at(i, 0))
                sp.dma_start(m_in[0][:, :, :], m0g[i + 1]).then_inc(m_loaded[0].sem, 16)
                sp.wait_ge(xn_ready["a"].sem, xn_ready["a"].at(i, SEQS - 1))
                sp.wait_ge(x_moved.sem, x_moved.at(i, 0))
                sp.dma_start(x_in[:, :, :], xg[i + 1]).then_inc(x_loaded.sem, 16)
                sp.wait_ge(masks_made[1].sem, masks_made[1].at(i, 0))
                sp.dma_start(m_in[1][:, :, :], m1g[i + 1].partition_broadcast(P)).then_inc(m_loaded[1].sem, 16)
                sp.dma_start(mk_in[:, :], mkg[i + 1]).then_inc(mk_loaded.sem, 16)

            def store(i):
                sp.wait_ge(summed.sem, summed.at(i, (E, 1)))
                sp.dma_start(og[i], x_out[:, :, :]).then_inc(out_stored.sem, 16)

            body(0)
            with sp.Fori(1, groups - 1) as i:
                body(i)
                store(i - 1)
            store(groups - 2)
            store(groups - 1)
            sp.wait_ge(out_stored.sem, out_stored.before(groups + 1))

        @block.gpsimd
        def _(pool):
            pool.memset(b2f[:, :], 0.0).then_inc(consts_made, 1)
            steps = 0
            zeroed = [(id32, 0.0), (id16, 0.0), (idb, 0.0), (pick, 0.0), (expert_of, 0.0)]
            for t, v in zeroed:
                pool.memset(t[tuple(slice(None) for _ in t.shape)], v).then_inc(const_step, 1)
                steps += 1
            for t, v in ((c_eps, LN_EPS), (c_1eps, 1.0 + LN_EPS), (c_eps2, LN_EPS * LN_EPS), (c_mhalf, -0.5), (ones_q, S_X), (ones_kv, S_W)):
                pool.memset(t[:, :], v).then_inc(consts_made, 1)
            pool.memset(mT[:, :, :], 0.0).then_inc(consts_made, 1)
            pool.memset(x_out[:, 0, 0:1], 0.0).then_inc(out_stored.sem, 16)
            pool.memset(tokens[:, :, :], 0.0).then_inc(consts_made, 1)
            for l in range(2):
                for h in range(2):
                    pool.memset(V[l][h][:, :, HD:VW], (S_W, 0.0)[h]).then_inc(consts_made, 1)
            pool.wait_ge(const_step, steps)
            for t in (id32, id16, idb):
                pool.affine_select(out=t[:, :], in_=t[:, :], compare_op=ALU.not_equal, fill=1.0, base=0,
                                   pattern=[[-1, P]], channel_multiplier=1).then_inc(consts_made, 1)
            pool.affine_select(out=pick[:, :, :], in_=pick[:, :, :], compare_op=ALU.not_equal, fill=1.0, base=0,
                               pattern=[[-1, 4], [0, P]], channel_multiplier=1).then_inc(consts_made, 1)
            pool.affine_select(out=expert_of[:, :, :], in_=expert_of[:, :, :], compare_op=ALU.not_equal,
                               fill=OFF_EXPERT, base=-16, pattern=[[-1, E], [0, 64]],
                               channel_multiplier=1).then_inc(consts_made, 1)
            pool.iota(iota8i[:, :], pattern=[[1, E]], base=0, channel_multiplier=0).then_inc(consts_made, 1)
            pool.iota(pi[:, 0:1], pattern=[[0, 1]], base=0, channel_multiplier=1).then_inc(consts_made, 1)

            chain = Chain(pool, pool_step, POOL_LINKS)
            prep = Chain(pool, pool_prep_step, POOL_PREP_LINKS)

            def inverse_std(i, ph):
                f = "abcd".index(ph)
                link = (prep if ph == "a" else chain).link
                var, r, q = mv[:, f, :, 1], rstd[:, f, :], ptmp[f]
                pool.wait_ge(stats_ready[ph].sem, stats_ready[ph].at(i, 0))
                if ph == "a":
                    link(pool.tensor_tensor(q[:, 0, :], var, c_eps[:, :], ALU.add))
                    link(pool.tensor_tensor(q[:, 1, :], q[:, 0, :], c_mhalf[:, :], ALU.pow))
                    pool.wait_ge(rows_made[0].sem, rows_made[0].at(i, 0))
                    pool.tensor_tensor(r, q[:, 1, :], some_on[:, 0, :], ALU.mult).then_inc(rstd_ready[ph].by(0), 1)
                elif ph == "b":
                    link(pool.tensor_tensor(q[:, 0, :], var, c_1eps[:, :], ALU.mult))
                    link(pool.tensor_tensor(q[:, 1, :], q[:, 0, :], c_eps2[:, :], ALU.add))
                    pool.tensor_tensor(r, q[:, 1, :], c_mhalf[:, :], ALU.pow).then_inc(rstd_ready[ph].by(0), 1)
                else:
                    link(pool.tensor_tensor(q[:, 0, :], var, c_eps[:, :], ALU.add))
                    pool.tensor_tensor(r, q[:, 0, :], c_mhalf[:, :], ALU.pow).then_inc(rstd_ready[ph].by(0), 1)

            def carry_wait(f):
                pool.tensor_tensor(ptmp[f][:, 2, :], c_eps[:, :], c_eps[:, :], ALU.add)

            def group(i, following, fill):
                chain.group(i)
                if following:
                    prep.group(i + 1)
                    inverse_std(i + 1, "a")
                inverse_std(i, "b")
                inverse_std(i, "c")
                inverse_std(i, "d")
                if fill:
                    pool.wait_ge(summed.sem, summed.at(i - 1, (0, 1)))
                    carry_wait(0)
                pool.tensor_copy(x_ffn[:, :, :], x[:, :, :]).then_inc(x_kept.by(0), 1)
                if following:
                    pool.wait_ge(xn_ready["d"].sem, xn_ready["d"].at(i, SEQS - 1))
                    carry_wait(2)
                    pool.wait_ge(x_kept.sem, x_kept.at(i, 0))
                    carry_wait(3)
                    pool.tensor_copy(x[:, :, :], x_in[:, :, :]).then_inc(x_moved.by(0), 1)

            pool.wait_ge(x_loaded.sem, 16)
            pool.tensor_copy(x[:, :, :], x_in[:, :, :]).then_inc(x_moved.by(0), 1)
            prep.group(0)
            inverse_std(0, "a")
            group(0, True, False)
            with pool.Fori(1, groups - 1) as i:
                group(i, True, True)
            group(groups - 1, False, True)

        N_CONSTS = 1 + 6 + 1 + 1 + 4 + 3 + 1 + 1 + 2

        @block.tensor
        def _(pe):
            pe.wait_ge(consts_made, N_CONSTS)
            pe.wait_ge(small_loaded, 16 * 14)
            pe.wait_ge(w_loaded[0], 16 * len(CHUNKS[0]))
            at = W_COLS["W1"][0]
            for t in range(HT0):
                for k in range(KT):
                    c = at + k * HT0 * P + t * P
                    mm = pe.matmul(ps[:, 0, t * E:(t + 1) * E], stage[0][:, c:c + P], ln_b[:, k, :],
                                   start=(t == 0 and k == 0), stop=(k == KT - 1), skip_group_check=True)
            mm.then_inc(b1_ready, 1)
            pe.wait_ge(setup_done, 1)

            def turn(i, f, first, xn=xn):
                for t in range(KT):
                    for s in range(SEQS):
                        if t == 0:
                            pe.wait_ge(xn_ready[f].sem, xn_ready[f].at(i, s))
                        mm = pe.transpose(ps[:, first + t, s * P:(s + 1) * P], xn[:, s, t * P:(t + 1) * P],
                                          id32[:, :])
                    mm.then_inc(xt_ready[f].by(t), 1)

            def scores(i, l, u):
                s, j = divmod(u, 4)
                tok = slice(s * P, (s + 1) * P)
                r = slice(32 * j, 32 * j + 32)
                if u:
                    pe.wait_ge(mt_ready.sem, mt_ready.at(i, (l, u - 1)))
                pe.matmul(ps[:, SQ, :].rearrange("p (n k) -> p n k", n=4), idb[:, :],
                          maskb[l][:, s:s + 1, :].to_broadcast([P, 4, P]), start=True, stop=False,
                          skip_group_check=True)
                for t in range(KT):
                    for e in range(2):
                        mm = pe.matmul(by_heads(SQ)[:, t, e, :], Q[l][0][r, t, e, tok],
                                       (CT, K1)[l][0][r, t, tok], start=False, stop=True, skip_group_check=True)
                mm.then_inc(s_ready.by((l, u)), 1)

            def turn_maxima(i, l, u):
                pe.wait_ge(max_done.sem, max_done.at(i, (l, u)))
                pe.transpose(maxT, negmax[:, u % 2, :], idb[:, :]).then_inc(t_ready.by((l, u)), 1)

            def attention(i, l, following, fill):
                kparts = CT if l == 0 else K1
                B = maskb[l]
                qh, ql = Q[l]
                for u in range(1 - l, UNITS + AV_LAG):
                    if u < UNITS:
                        scores(i, l, u)
                    if 1 <= u <= UNITS:
                        v = u - 1
                        s, j = divmod(v, 4)
                        tok = slice(s * P, (s + 1) * P)
                        r = slice(32 * j, 32 * j + 32)
                        bank = ST[v % 2]
                        pe.wait_ge(mt_ready.sem, mt_ready.at(i, (l, v)))
                        if v >= 2:
                            pe.wait_ge(exp_done.sem, exp_done.at(i, (l, v - 2, 1)))
                        if l == 0:
                            pe.matmul(ps[:, bank, :].rearrange("p (n q) -> p n q", n=4), B[:, s, :],
                                      idb[:, :].unsqueeze(1).to_broadcast([P, 4, P]), start=True, stop=False,
                                      skip_group_check=True)
                        for c in range(4):
                            pe.matmul(by_heads(bank)[:, c // 2, c % 2, :], pick[:, c, :], mT[:, v % 2, :],
                                      start=(l == 1 and c == 0), stop=False, skip_group_check=True)
                        for t in range(KT):
                            for n, (pk, pq) in enumerate(PARTS):
                                mm = pe.matmul(by_heads(bank)[:, t, :, :], kparts[pk][r, t, tok],
                                               (qh, ql)[pq][r, t, :, tok],
                                               start=False, stop=(n == 2), skip_group_check=True)
                        mm.then_inc(st_ready.by((l, v)), 1)
                    beside_maxima(i, l, u, following, fill)
                    if u < UNITS:
                        turn_maxima(i, l, u)
                    elif fill:
                        second_products(i, l, u)
                    j = step_at(l, u, 1)
                    if fill and j is not None:
                        step_first(i - 1, j, 1, 1)
                    if u >= AV_LAG:
                        v = u - AV_LAG
                        s, j = divmod(v, 4)
                        if l == 0 and v == 0:
                            pe.wait_ge(lo["v0"].sem, lo["v0"].at(i, 0))
                        pe.wait_ge(plo_done.sem, plo_done.at(i, (l, v)))
                        if j == 0 and s:
                            pe.wait_ge(o_read.sem, o_read.at(i, (l, s - 1)))
                        elif j == 0 and l == 0 and fill:
                            pe.wait_ge(o_read.sem, o_read.at(i - 1, (1, SEQS - 1)))
                        for t in range(KT):
                            for e in range(2):
                                c = t * 2 + e
                                h = 8 * t + 2 * j + e
                                for n, (pp, pv) in enumerate(PARTS):
                                    mm = pe.matmul(O[:, h, :], (PH, PL)[pp][:, v % 4, c * P:(c + 1) * P],
                                                   V[l][pv][:, s * HEADS + h, :],
                                                   start=(j == 0 and c == 0 and n == 0), stop=(n == 2),
                                                   skip_group_check=True)
                        mm.then_inc(av_done.by((l, v)), 1)
                    if fill and u < UNITS:
                        second_products(i, l, u)

            def keys(i, m, fill):
                if fill:
                    pe.wait_ge(acted.sem, acted.at(i - 1, slices(4)[m]))
                wide(6 + m, "k_w", m, CT, qkv_b[:, 1, m * P:(m + 1) * P], ones_kv[:, :])\
                    .then_inc(proj_ready.by(f"k{m}"), 1)

            def second_products(i, l, u):
                for half_ in range(2):
                    j = step_at(l, u, 5 + half_)
                    if j is not None and half_ < len(slices(j)):
                        step_second(i - 1, j, half_)

            def beside_maxima(i, l, u, following, fill):
                if l == 0 and u == UNITS + AV_LAG - 2:
                    keys(i, 0, fill)
                if fill:
                    if l == 0 and u == 1:
                        turn(i - 1, "d", G)
                    if l == 0 and u == 3:
                        pe.wait_ge(lo["xd"].sem, lo["xd"].at(i - 1, KT - 1))
                        logits(i - 1, "d", "router_w", XD, G + 1)
                    if following and l == 1 and u == 3:
                        pe.wait_ge(lo["ct"].sem, lo["ct"].at(i + 1, KT - 1))
                    if step_at(l, u, 0) is not None:
                        step_first(i - 1, step_at(l, u, 0), 0)
                    if step_at(l, u, 1) is not None:
                        step_first(i - 1, step_at(l, u, 1), 1, 0)
                if following and l == 1 and u < KT:
                    turn_context(i + 1, u)

            def wide(bank, name, m, src, bias=None, ones=None, stop=True, only=None):
                out_ = ps[:, bank, :]
                n = 0 if only is None else 3 * only
                for k in range(KT) if only is None else [only]:
                    for pw, px in PARTS:
                        mm = pe.matmul(out_, w(pw, name, k, m * P, P), src[px][:, k, :], start=(n == 0),
                                       stop=(stop and bias is None and n == 3 * KT - 1), skip_group_check=True)
                        n += 1
                if bias is not None:
                    mm = pe.matmul(out_, bias, ones, start=False, stop=True, skip_group_check=True)
                return mm

            def logits(i, ph, name, src, bank):
                for s in range(SEQS):
                    n = 0
                    for k in range(KT):
                        for px, pw in PARTS:
                            mm = pe.matmul(lgp(bank)[:, s * E:(s + 1) * E], src[px][:, k, s * P:(s + 1) * P],
                                           w(pw, name, k, 0, E), start=(s == 0 and n == 0),
                                           stop=(n == 3 * KT - 1), skip_group_check=True)
                            n += 1
                mm.then_inc(lg_ready[ph].by(0), 1)

            def turn_tokens(i, bank):
                pe.wait_ge(tok_ready.sem, tok_ready.at(i, 0))
                for s in range(SEQS):
                    mm = pe.transpose(token_bank(bank)[:, s * P:(s + 1) * P], tokens[:, s, :], id16[:, :])
                mm.then_inc(tokp_ready.by(0), 1)

            def second(parts, slot, sums, name, t, first, last, each=None, free=None):
                for s in range(SEQS):
                    tok = slice(s * P, (s + 1) * P)
                    if free and s % 2 == 0:
                        free(s // 2)
                    for m, (ph_, pw) in enumerate(PARTS):
                        mm = pe.matmul(y(s, sums), parts[ph_][:, slot, tok], w(pw, name, t, 0, D),
                                       start=(first and m == 0 and s % 2 == 0), stop=(last and m == 2),
                                       skip_group_check=True)
                    if each and s % 2:
                        mm.then_inc(each(s // 2), 1)
                return mm

            def step_first(g, j, half_, only=None):
                n = slices(j)[0] if j < HTS else slices(j)[half_]
                if only == 1:
                    pass
                elif j < HTS:
                    if j:
                        pe.wait_ge(prod.sem, prod.at(g, j - 1))
                    elif half_ == 1:
                        pe.wait_ge(lg_tanh.sem, lg_tanh.at(g, 0))
                else:
                    if n < HTS + 2:
                        pe.wait_ge(prod.sem, prod.at(g, HTS - 1))
                    else:
                        pe.wait_ge(acted.sem, acted.at(g, n - 2))
                if j < HTS:
                    mm = wide(G + half_, ("sw1", "sw3")[half_], n, XD, only=only)
                else:
                    mm = wide(G + n % 2, "ew1", n - HTS, XD, only=only)
                if only != 0 and (half_ == 1 or j >= HTS):
                    mm.then_inc(g1.by(n), 1)

            def step_second(g, j, half_):
                n = slices(j)[half_]
                pe.wait_ge(hid_lo.sem, hid_lo.at(g, n))
                name, t = ("sw2", n) if n < HTS else ("ew2", n - HTS)
                k = 0 if n < HTS else 1 + (n - HTS) // 2
                first = n == 0 or (n >= HTS and n % 2 == 0)
                last = n == HTS - 1 or (n >= HTS and n % 2 == 1)
                mm = second((HH, HL), n % 4, Y, name, t, first, last,
                            free=(lambda b: pe.wait_ge(summed.sem, summed.at(g, (k - 1, b)))) if first and k else None,
                            each=(lambda b: y_ready.by((k, b))) if last else None)
                if not last:
                    mm.then_inc(g2.by(n), 1)

            def turn_context(i, t):
                if t == 0:
                    pe.wait_ge(ctx_loaded.sem, ctx_loaded.at(i, "ctx"))
                for s in range(SEQS):
                    mm = pe.transpose(ps[:, G + t, s * P:(s + 1) * P], ctx_in[:, s, t * P:(t + 1) * P], id32[:, :])
                mm.then_inc(ct_ready.by(t), 1)

            def group(i, following, fill):
                attention(i, 0, following, fill)
                keys(i, 1, fill)
                if following:
                    turn(i + 1, "a", 0, xn_a)
                if fill:
                    step_second(i - 1, 4, 0)
                turn(i, "b", 2)
                if fill:
                    step_second(i - 1, 4, 1)
                pe.wait_ge(lo["xb"].sem, lo["xb"].at(i, KT - 1))
                logits(i, "b", "Wg", XT, 6)
                pe.wait_ge(lo["k"].sem, lo["k"].at(i, 1))
                wide(G0[0], "W1", 0, XT, stop=False)
                wide(G0[1], "W1", 1, XT, stop=False)
                turn_tokens(i, 6)
                wide(G0[2], "W1", 2, XT, stop=False)
                pe.wait_ge(tokT_ready.sem, tokT_ready.at(i, 0))

                def push_others(n):
                    pe.matmul(ps[:, G0[n], :], expert_of[:, 2 * n:2 * n + 2, :].rearrange("r e h -> r (e h)"),
                              tokT[:, :], start=False, stop=True, skip_group_check=True)\
                        .then_inc(e_g1.by(n), 1)

                for n in range(HT0 - 1):
                    push_others(n)
                wide(G0[3], "W1", 3, XT, stop=False)
                push_others(HT0 - 1)
                if following:
                    pe.wait_ge(lo["qa"].sem, lo["qa"].at(i + 1, KT - 1))
                for n in range(HT0):
                    if n == HT0 - 1:
                        for s in range(SEQS):
                            pe.matmul(y(s, 0), tokT[:, s * P:(s + 1) * P], b2[:, :], start=False, stop=False,
                                      skip_group_check=True)
                    pe.wait_ge(e_lo.sem, e_lo.at(i, n))
                    second((PH, PL), n, 0, "W2", n, n == 0, n == HT0 - 1,
                           each=e_sums.by if n == HT0 - 1 else None)
                if fill:
                    for half_ in range(2):
                        step_first(i - 1, IN_BETWEEN[0], half_)
                for s in range(SEQS):
                    n = 0
                    for k in range(KT):
                        for pc, pw in PARTS:
                            pe.matmul(y(s, 2), CT[pc][:, k, s * P:(s + 1) * P], w(pw, "v_w", k, 0, D),
                                      start=(n == 0 and s % 2 == 0), stop=False, skip_group_check=True)
                            n += 1
                    mm = pe.matmul(y(s, 2), ones_kv[:, 0:P], qkv_b[:, 2, :], start=False, stop=True,
                                   skip_group_check=True)
                    if s % 2:
                        mm.then_inc(proj_ready.by(f"v{s // 2}"), 1)
                turn(i, "c", 0)
                if fill:
                    for half_ in range(2):
                        step_first(i - 1, IN_BETWEEN[1], half_)
                pe.wait_ge(lo["xc"].sem, lo["xc"].at(i, KT - 1))
                pe.wait_ge(lo["v1"].sem, lo["v1"].at(i, 1))
                for m in range(2):
                    wide(2 + m, "q_w", m, XT, qkv_b[:, 0, m * P:(m + 1) * P], ones_q[:, :])\
                        .then_inc(proj_ready.by(f"q{m}"), 1)
                if fill:
                    for half_ in range(2):
                        step_second(i - 1, IN_BETWEEN[0], half_)
                    pe.wait_ge(acted.sem, acted.at(i - 1, slices(IN_BETWEEN[1])[-1]))
                pe.wait_ge(lo["qc"].sem, lo["qc"].at(i, KT - 1))
                attention(i, 1, following, fill)
                if following:
                    first_scores(i + 1)
                if fill:
                    step_second(i - 1, STEPS - 1, 0)
                if following:
                    turn_maxima(i + 1, 0, 0)
                if fill:
                    step_second(i - 1, STEPS - 1, 1)

            def first_scores(i):
                pe.wait_ge(lo["qa"].sem, lo["qa"].at(i, KT - 1))
                pe.wait_ge(lo["ct"].sem, lo["ct"].at(i, KT - 1))
                scores(i, 0, 0)

            for t in range(KT):
                turn_context(0, t)
            turn(0, "a", 0, xn_a)
            first_scores(0)
            turn_maxima(0, 0, 0)
            group(0, True, False)
            with pe.Fori(1, groups - 1) as i:
                group(i, True, True)
            group(groups - 1, False, True)
            turn(groups - 1, "d", G)
            pe.wait_ge(lo["xd"].sem, lo["xd"].at(groups - 1, KT - 1))
            logits(groups - 1, "d", "router_w", XD, G + 1)
            for j in range(STEPS + 1):
                if j < STEPS:
                    for half_ in range(2):
                        step_first(groups - 1, j, half_)
                if j:
                    for half_ in range(len(slices(j - 1))):
                        step_second(groups - 1, j - 1, half_)

        @block.scalar
        def _(act):
            act.wait_ge(small_loaded, 16 * 14)
            act.activation(tg[:, :], gates4[:, :], ACT.Tanh).then_inc(tg_ready, 1)
            for c, names in enumerate(CHUNKS):
                n = sum(W_COLS[x_][1] for x_ in names)
                base = W_COLS[names[0]][0]
                act.wait_ge(w_loaded[c], 16 * len(names))
                if c == 0:
                    act.wait_ge(w1_scaled, 1)
                act.activation(WH[:, base:base + n], stage[c % 2][:, 0:n], ACT.Copy, scale=S_W)\
                    .then_inc(w_high, 1)
            act.wait_ge(setup_done, 1)

            def high(name, t, o_, i_, scale):
                act.activation(o_, i_, ACT.Copy, scale=scale).then_inc(hi[name].by(t), 1)

            def query_high(name, l, t, bank):
                for e in range(2):
                    ins = act.activation(Q[l][0][:, t, e, :], ps[:, bank, :], ACT.Identity,
                                         scale=half[:, l, e:e + 1])
                ins.then_inc(hi[name].by(t), 1)

            def attention(i, l, following, fill):
                scale = 0.25 / (S_XW if l == 0 else S_WW)
                for v in range(UNITS + 2):
                    if v < UNITS:
                        src = ps[:, ST[v % 2], :]
                        bias = lnP[:, :] if l == 0 else key_bias[:, v // 4:v // 4 + 1]
                        act.wait_ge(st_ready.sem, st_ready.at(i, (l, v)))
                        if v >= 4:
                            act.wait_ge(av_done.sem, av_done.at(i, (l, v - 4)))
                        elif l == 0 and fill:
                            act.wait_ge(av_done.sem, av_done.at(i - 1, (1, v + UNITS - 4)))
                        act.activation(P32[:, v % 4, :], src, ACT.Exp, bias=bias, scale=scale)\
                            .then_inc(exp_done.by((l, v, 0)), 1)
                        act.activation(PH[:, v % 4, :], src, ACT.Exp, bias=bias, scale=scale)\
                            .then_inc(exp_done.by((l, v, 1)), 1)
                    if fill:
                        if l == 0 and v == 0:
                            turned(i - 1, "d", XD, G)
                        if l == 0 and v == 2:
                            router_tanh(i - 1)
                        j = step_at(l, v, 0)
                        if j is not None:
                            step_activation(i - 1, j)
                        j = step_at(l, v, 2)
                        if j is not None and j < HTS:
                            shared_high(i - 1, j)
                    if following and l == 1:
                        if v == 0:
                            context_high(i + 1)
                        if v == 2:
                            high("v0", 0, V[0][0][:, :, 0:HD],
                                 ctx_in[:, :, :].rearrange("p s (h d) -> p (s h) d", d=HD), S_W)

            def step_activation(g, j):
                for n in slices(j):
                    act.wait_ge(g1.sem, g1.at(g, n))
                    if n >= 2:
                        act.wait_ge(hid_lo.sem, hid_lo.at(g, n - 2))
                    func, scale = (ACT.Tanh, 0.5 / S_XW) if n < HTS else (ACT.Gelu, 1 / S_XW)
                    bank = G if n < HTS else G + n % 2
                    act.activation(h32[:, n % 2, :], ps[:, bank, :], func, scale=scale).then_inc(acted.by(n), 1)
                if j >= HTS:
                    for n in slices(j):
                        act.wait_ge(acted.sem, acted.at(g, n))
                        act.wait_ge(*multiplied(g, n - 4))
                        act.activation(HH[:, n % 4, :], h32[:, n % 2, :], ACT.Copy, scale=S_W)\
                            .then_inc(hid_hi.by(n), 1)

            def shared_high(g, j):
                act.wait_ge(prod.sem, prod.at(g, j))
                act.activation(HH[:, j % 4, :], v32[:, j % 2, :], ACT.Copy, scale=0.5 * S_W / (S_XW * S_XW))\
                    .then_inc(hid_hi.by(j), 1)

            def turned(i, f, dst, first):
                for t in range(KT):
                    act.wait_ge(xt_ready[f].sem, xt_ready[f].at(i, t))
                    high("x" + f, t, dst[0][:, t, :], ps[:, first + t, :], S_X)

            def router_tanh(i):
                act.wait_ge(lg_ready["d"].sem, lg_ready["d"].at(i, 0))
                act.activation(lg[:, :, :].rearrange("p s e -> p (s e)"), lgp(G + 1), ACT.Tanh, scale=0.5 / S_XW)\
                    .then_inc(lg_tanh.by(0), 1)

            def context_high(i):
                for t in range(KT):
                    act.wait_ge(ct_ready.sem, ct_ready.at(i, t))
                    high("ct", t, CT[0][:, t, :], ps[:, G + t, :], S_W)

            def prepare_queries(i):
                for t in range(KT):
                    act.wait_ge(xt_ready["a"].sem, xt_ready["a"].at(i, t))
                    query_high("qa", 0, t, t)

            def group(i, following, fill):
                attention(i, 0, following, fill)
                def key_high(m):
                    act.wait_ge(proj_ready.sem, proj_ready.at(i, f"k{m}"))
                    high("k", m, K1[0][:, m, :], ps[:, 6 + m, :], 1 / S_W)

                key_high(0)
                key_high(1)
                if following:
                    prepare_queries(i + 1)
                turned(i, "b", XT, 2)
                act.wait_ge(tokp_ready.sem, tokp_ready.at(i, 0))
                act.activation(tokT[:, :], token_bank(6), ACT.Copy).then_inc(tokT_ready.by(0), 1)

                def hidden(n):
                    act.wait_ge(e_g1.sem, e_g1.at(i, n))
                    act.activation(P32[:, n, :], ps[:, G0[n], :], ACT.Gelu, bias=b1e[:, n:n + 1],
                                   scale=1 / S_XW).then_inc(e_act.by(n), 1)

                def hidden_high(n):
                    act.wait_ge(e_act.sem, e_act.at(i, n))
                    act.activation(PH[:, n, :], P32[:, n, :], ACT.Copy, scale=S_W).then_inc(e_hi.by(n), 1)

                hidden(0)
                hidden_high(0)
                for n in range(1, HT0):
                    hidden(n)
                    if n > 1:
                        hidden_high(n - 1)
                hidden_high(HT0 - 1)
                if fill:
                    step_activation(i - 1, IN_BETWEEN[0])
                for m in range(2):
                    act.wait_ge(proj_ready.sem, proj_ready.at(i, f"v{m}"))
                    high("v1", m, V[1][0][:, 32 * m:32 * m + 32, 0:HD],
                         ps[:, 2 + m, :].rearrange("p (h d) -> p h d", d=HD), 1 / S_W)
                turned(i, "c", XT, 0)
                for m in range(2):
                    act.wait_ge(proj_ready.sem, proj_ready.at(i, f"q{m}"))
                    query_high("qc", 1, m, 2 + m)
                if fill:
                    step_activation(i - 1, IN_BETWEEN[1])
                attention(i, 1, following, fill)

            act.wait_ge(ctx_loaded.sem, ctx_loaded.at(0, "ctx"))
            high("v0", 0, V[0][0][:, :, 0:HD], ctx_in[:, :, :].rearrange("p s (h d) -> p (s h) d", d=HD), S_W)
            context_high(0)
            prepare_queries(0)
            group(0, True, False)
            with act.Fori(1, groups - 1) as i:
                group(i, True, True)
            group(groups - 1, False, True)
            turned(groups - 1, "d", XD, G)
            router_tanh(groups - 1)
            for j in range(STEPS):
                step_activation(groups - 1, j)
                if j < HTS:
                    shared_high(groups - 1, j)

        @block.vector
        def _(dve):
            chain = Chain(dve, dve_step, DVE_LINKS, DVE_SETUP)
            prep = Chain(dve, dve_prep_step, DVE_PREP_LINKS)
            router = Chain(dve, dve_router_step, DVE_ROUTER_LINKS)
            link = chain.link
            dve.memset(lnP[:, :], 5.545177444479562)
            dve.wait_ge(consts_made, N_CONSTS)
            link(dve.tensor_copy(iota8[:, :], iota8i[:, :]))
            for c, shift in ((1, 4), (2, 3), (3, 0)):
                link(dve.tensor_scalar(pi[:, c:c + 1], pi[:, 0:1], shift, 1, ALU.logical_shift_right,
                                       ALU.bitwise_and))
            link(dve.tensor_copy(pf[:, :], pi[:, :]))
            for l, sc in enumerate((S_X, 1 / S_X)):
                link(dve.tensor_scalar(half[:, l, 0:1], pf[:, 1:2], -sc, sc, ALU.mult, ALU.add))
                link(dve.tensor_scalar(half[:, l, 1:2], pf[:, 1:2], sc, None, ALU.mult))
            link(dve.tensor_scalar(pf[:, 2:4], pf[:, 2:4], -1.0, None, ALU.mult))
            dve.wait_ge(small_loaded, 16 * 14)
            for f_, h_, o_, col, rows in ((b2f[:, :], b2h[:, :], b2[:, :], 2, 32),
                                          (bf[:, :, :].rearrange("p a d -> p (a d)"),
                                           bh[:, :, :].rearrange("p a d -> p (a d)"),
                                           qkv_b[:, :, :].rearrange("p a d -> p (a d)"), 3, 2)):
                link(dve.tensor_scalar(f_, f_, S_W, None, ALU.mult))
                link(dve.tensor_copy(h_, f_))
                link(dve.scalar_tensor_tensor(out=o_, in0=h_, scalar=pf[0:rows, col:col + 1], in1=f_,
                                              op0=ALU.mult, op1=ALU.add))
            dve.wait_ge(tg_ready, 1)
            for c in (1, 3):
                link(dve.tensor_scalar(tg[:, c:c + 1], tg[:, c:c + 1], 1 / S_WW, None, ALU.mult))
            dve.wait_ge(b1_ready, 1)
            for t in range(HT0):
                for h_ in range(2):
                    r = slice(64 * h_, 64 * h_ + 64)
                    ins = dve.tensor_tensor(b1e[r, t:t + 1], ps[r, 0, t * E + 2 * t + h_:t * E + 2 * t + h_ + 1],
                                            b1[r, t:t + 1], ALU.add)
                    if h_ and t == HT0 - 1:
                        link(ins)
            at = W_COLS["W1"][0]
            w1v = stage[0][:, at:at + KT * HT0 * P].rearrange("p (t e h) -> p t e h", t=KT, e=E)
            for t in range(KT):
                ins = dve.tensor_tensor(w1v[:, t, :, :], w1v[:, t, :, :],
                                        ln_s[:, t, :].unsqueeze(2).to_broadcast([P, E, 64]), ALU.mult)
            ins.then_inc(w1_scaled, 1)
            dve.wait_ge(w1_scaled, 1)
            for c, names in enumerate(CHUNKS):
                n = sum(W_COLS[x_][1] for x_ in names)
                base = W_COLS[names[0]][0]
                dve.wait_ge(w_high, c + 1)
                ins = dve.scalar_tensor_tensor(out=WL[:, base:base + n], in0=stage[c % 2][:, 0:n], scalar=S_W,
                                               in1=WH[:, base:base + n], op0=ALU.mult, op1=ALU.subtract)
                ins.then_inc(w_low, 1)
            dve.wait_ge(w_low, len(CHUNKS))
            assert chain.done == DVE_SETUP, f"DVE_SETUP {chain.done}"
            dve.memset(idle[:, :], 0.0).then_inc(setup_done, 1)

            def low(i, name, t, o_, src, scale, h_):
                dve.wait_ge(hi[name].sem, hi[name].at(i, t))
                dve.scalar_tensor_tensor(out=o_, in0=src, scalar=scale, in1=h_, op0=ALU.mult,
                                         op1=ALU.subtract).then_inc(lo[name].by(t), 1)

            def query_low(i, name, l, t, bank):
                dve.wait_ge(hi[name].sem, hi[name].at(i, t))
                for e in range(2):
                    ins = dve.scalar_tensor_tensor(out=Q[l][1][:, t, e, :], in0=ps[:, bank, :],
                                                   scalar=half[:, l, e:e + 1], in1=Q[l][0][:, t, e, :],
                                                   op0=ALU.mult, op1=ALU.subtract)
                ins.then_inc(lo[name].by(t), 1)

            def carry_wait():
                dve.memset(idle[:, :], 0.0)

            def measure(i, f, seqs, src):
                for s in seqs:
                    ins = dve.bn_stats(stats[f % 2][:, s, :], src[:, s, :])
                (prep if f == 0 else chain).link(ins)

            def aggregate(i, f, seqs):
                for s in seqs:
                    ins = dve.bn_aggr(mv[:, f, s, :], stats[f % 2][:, s, :])
                    if s == SEQS - 1:
                        ins.then_inc(stats_ready["abcd"[f]].by(0), 1)

            def normalise(i, f, src, xn=xn):
                ph = "abcd"[f]
                dve.wait_ge(rstd_ready[ph].sem, rstd_ready[ph].at(i, 0))
                for s in range(SEQS):
                    dve.tensor_scalar(xn[:, s, :], src[:, s, :], mv[:, f, s, 0:1], rstd[:, f, s:s + 1],
                                      ALU.subtract, ALU.mult).then_inc(xn_ready[ph].by(s), 1)

            def masked_keys(i, l):
                link = (prep, chain)[l].link
                dve.wait_ge(m_loaded[l].sem, m_loaded[l].at(i, "m"))
                link(dve.tensor_scalar(off[l][:, :, :], m_in[l][:, :, :], 0.0, None,
                                       (ALU.is_equal, ALU.is_gt)[l]))
                link(dve.tensor_reduce(n_off[:, l, :], off[l][:, :, :], AX, ALU.add))
                dve.tensor_scalar(some_on[:, l, :], n_off[:, l, :], P - 0.5, None, ALU.is_lt)\
                    .then_inc(rows_made[l].by(0), 1)
                dve.wait_ge(rows_made[l].sem, rows_made[l].at(i, 0))

            def mask_bias(i, l):
                link = (prep, chain)[l].link
                link(dve.tensor_scalar(take_off[:, l, :], some_on[:, l, :],
                                       -MASKED * (S_XW, S_WW)[l], None, ALU.mult))
                ins = dve.tensor_tensor(maskb[l][:, :, :], off[l][:, :, :],
                                        take_off[:, l, :].unsqueeze(2).to_broadcast([P, SEQS, P]), ALU.mult)
                if l == 0:
                    ins.then_inc(masks_made[0].by(0), 1)
                else:
                    dve.wait_ge(mk_loaded.sem, mk_loaded.at(i, "m"))
                    link(dve.tensor_scalar(key_bias[:, :], mk_in[:, :], 0.0, -0.25 * MASKED, ALU.is_gt, ALU.mult))
                    link(dve.tensor_scalar(key_bias[:, :], key_bias[:, :], lnP[:, 0:1], None, ALU.add))
                    link(dve.reciprocal(nan_row[:, :], some_on[:, 1, :]))
                    dve.tensor_tensor(nan_row[:, :], nan_row[:, :], some_on[:, 1, :], ALU.mult)\
                        .then_inc(masks_made[1].by(0), 1)

            def divide(i, l, s):
                dve.wait_ge(av_done.sem, av_done.at(i, (l, 4 * s + 3)))
                link(dve.reciprocal(rden[:, :], O[:, :, HD]))
                if l == 1:
                    link(dve.tensor_scalar(rden[:, :], rden[:, :], nan_row[:, s:s + 1], None, ALU.mult))
                dve.tensor_tensor(att[:, :].rearrange("p (h d) -> p h d", d=HD), O[:, :, 0:HD],
                                  rden[:, :].unsqueeze(2).to_broadcast([P, HEADS, HD]), ALU.mult)\
                    .then_inc(o_read.by((l, s)), 1)

            def add_residual(i, l, s):
                ph = "ac"[l]
                if l == 0 and s == 0:
                    dve.wait_ge(x_moved.sem, x_moved.at(i, 0))
                dve.wait_ge(o_read.sem, o_read.at(i, (l, s)))
                dve.scalar_tensor_tensor(out=x[:, s, :], in0=att[:, :], scalar=tg[:, 2 * l:2 * l + 1],
                                         in1=x[:, s, :], op0=ALU.mult, op1=ALU.add)\
                    .then_inc(resid.by((ph, s)), 1)
                dve.wait_ge(resid.sem, resid.at(i, (ph, s)))
                measure(i, 2 * l + 1, [s], x)
                carry_wait()
                aggregate(i, 2 * l + 1, [s])

            def maxima(i, l, u):
                dve.wait_ge(s_ready.sem, s_ready.at(i, (l, u)))
                dve.tensor_reduce(negmax[:, u % 2, :], ps[:, SQ, :].rearrange("p (c k) -> p c k", c=4), AX,
                                  ALU.max, negate=True).then_inc(max_done.by((l, u)), 1)

            def copy_maxima(i, l, u):
                dve.wait_ge(t_ready.sem, t_ready.at(i, (l, u)))
                dve.tensor_copy(mT[0:4, u % 2, :], maxT).then_inc(mt_ready.by((l, u)), 1)

            def low_probabilities(i, l, v):
                dve.wait_ge(exp_done.sem, exp_done.at(i, (l, v, 1)))
                dve.tensor_tensor(PL[:, v % 4, :], P32[:, v % 4, :], PH[:, v % 4, :], ALU.subtract)\
                    .then_inc(plo_done.by((l, v)), 1)

            def attention(i, l, following, fill):
                for u in range(1 - l, UNITS + AV_LAG):
                    if u < UNITS:
                        maxima(i, l, u)
                    elif u < UNITS + PL_LAG:
                        low_probabilities(i, l, u - PL_LAG)
                    if fill:
                        beside_turning(i - 1, l, u)
                    divided, since = divmod(u - AV_LAG, 4)
                    adds = divided > 0 and since == 0 and u < UNITS + AV_LAG
                    early = step_at(l, u, 0) is not None or step_at(l, u, 1) is not None
                    if adds and early:
                        add_residual(i, l, divided - 1)
                    if u < UNITS:
                        copy_maxima(i, l, u)
                    if adds and not early:
                        add_residual(i, l, divided - 1)
                    if fill and l == 0 and u == 2:
                        turned_low(i - 1, "d", XD, G)
                    if following and l == 1 and u == 2:
                        context_low(i + 1)
                    j = step_at(l, u, 2)
                    if fill and j is not None and j < HTS:
                        swiglu_product(i - 1, j)
                    if PL_LAG <= u < UNITS:
                        low_probabilities(i, l, u - PL_LAG)
                    done, last = divmod(u + 1 - AV_LAG, 4)
                    if done and last == 0 and done < SEQS:
                        divide(i, l, done - 1)
                    if fill:
                        if l == 0 and u in GATES_AT:
                            gate_rows(i - 1, GATES_AT.index(u))
                        if l == 1 and u == 0:
                            step_low(i - 1, IN_BETWEEN[1])
                        if l == 1 and u == 1:
                            add_sums(i - 1, 1 + IN_BETWEEN[0] - HTS)
                    if l == 0 and following and u == 12:
                        dve.wait_ge(x_loaded.sem, x_loaded.at(i + 1, "x"))
                        measure(i + 1, 0, range(SEQS), x_in)
                        carry_wait()
                        aggregate(i + 1, 0, range(SEQS))
                    if l == 0 and following and u == 3:
                        masked_keys(i + 1, 0)
                    if l == 0 and following and u == 15:
                        normalise(i + 1, 0, x_in, xn_a)
                    if l == 1 and following and u == 5:
                        low(i + 1, "v0", 0, V[0][1][:, :, 0:HD],
                            ctx_in[:, :, :].rearrange("p s (h d) -> p (s h) d", d=HD), S_W, V[0][0][:, :, 0:HD])

            def beside_turning(g, l, u):
                j = step_at(l, u, 3)
                if j is not None and j >= HTS and u:
                    step_low(g, j)
                j = step_at(l, u, 4)
                if j is not None and j < HTS:
                    step_low(g, j)
                for b in range(2):
                    j = step_at(l, u, 7 if u >= UNITS else 7 + b)
                    if j is not None and j >= HTS:
                        add_sums(g, 1 + j - HTS, (b,))

            def swiglu_product(g, n):
                dve.wait_ge(acted.sem, acted.at(g, n))
                dve.scalar_tensor_tensor(out=v32[:, n % 2, :], in0=h32[:, n % 2, :], scalar=1.0,
                                         in1=ps[:, G, :], op0=ALU.add, op1=ALU.mult)\
                    .then_inc(silu_half.by(n), 1)
                dve.wait_ge(silu_half.sem, silu_half.at(g, n))
                dve.tensor_tensor(v32[:, n % 2, :], v32[:, n % 2, :], ps[:, G + 1, :], ALU.mult)\
                    .then_inc(prod.by(n), 1)

            def step_low(g, j):
                for n in slices(j):
                    dve.wait_ge(hid_hi.sem, hid_hi.at(g, n))
                    src_, scale = (v32, 0.5 * S_W / (S_XW * S_XW)) if n < HTS else (h32, S_W)
                    dve.scalar_tensor_tensor(out=HL[:, n % 4, :], in0=src_[:, n % 2, :], scalar=scale,
                                             in1=HH[:, n % 4, :], op0=ALU.mult, op1=ALU.subtract)\
                        .then_inc(hid_lo.by(n), 1)

            def add_sums(g, k, banks=(0, 1)):
                for b in banks:
                    dve.wait_ge(y_ready.sem, y_ready.at(g, (k, b)))
                    if k == 0 and b == 0:
                        dve.wait_ge(x_kept.sem, x_kept.at(g, 0))
                        dve.wait_ge(out_stored.sem, out_stored.before(g + 1))
                    elif k:
                        dve.wait_ge(summed.sem, summed.at(g, (k - 1, b)))
                        if k == 1 and b == 0:
                            dve.wait_ge(gates_ready.sem, gates_ready.at(g, 0))
                    for s in (2 * b, 2 * b + 1):
                        ins = dve.scalar_tensor_tensor(
                            out=x_out[:, s, :], in0=y(s, Y), scalar=gates[:, s, k - 1:k] if k else tg[:, 3:4],
                            in1=(x_out if k else x_ffn)[:, s, :], op0=ALU.mult, op1=ALU.add)
                    ins.then_inc(summed.by((k, b)), 1)

            def choose(values, link):
                carry_wait()
                for s in range(SEQS):
                    ins = dve.max(top8[:, s, :], values[:, s, :])
                link(ins)
                carry_wait()
                for s in range(SEQS):
                    ins = dve.max_index(topi[:, s, :], top8[:, s, :], values[:, s, :])
                link(ins)
                link(dve.tensor_copy(topf[:, :, :], topi[:, :, :]))

            def one_hot(dst, k):
                return dve.tensor_tensor(dst[:, :, :], iota8[:, :].unsqueeze(1).to_broadcast([P, SEQS, E]),
                                         topf[:, :, k:k + 1].to_broadcast([P, SEQS, E]), ALU.is_equal)

            def top1_rows(i):
                dve.wait_ge(lg_ready["b"].sem, lg_ready["b"].at(i, 0))
                link(dve.tensor_copy(lg[:, :, :].rearrange("p s e -> p (s e)"), lgp(6)))
                choose(lg, link)
                link(one_hot(oh, 0))
                dve.tensor_scalar(tokens[:, :, 0:8], oh[:, :, :], S_W, None, ALU.mult)
                dve.tensor_scalar(tokens[:, :, 8:16], oh[:, :, :], S_W, None, ALU.mult)
                dve.tensor_scalar(tokens[:, :, 16:24], oh[:, :, :], 1.0, OFF_EXPERT, ALU.subtract, ALU.mult)\
                    .then_inc(tok_ready.by(0), 1)

            def gate_rows(i, part):
                link = router.link
                if part == 0:
                    router.group(i)
                    dve.wait_ge(lg_tanh.sem, lg_tanh.at(i, 0))
                    link(dve.tensor_scalar(sig[:, :, :], lg[:, :, :], 0.5, 0.5, ALU.mult, ALU.add))
                    link(dve.tensor_tensor(oh2[:, :, :], sig[:, :, :],
                                           rb[:, :].unsqueeze(1).to_broadcast([P, SEQS, E]), ALU.add))
                    choose(oh2, link)
                elif part == 1:
                    link(one_hot(oh, 0))
                    link(one_hot(oh2, 1))
                    link(dve.tensor_tensor(oh[:, :, :], oh[:, :, :], oh2[:, :, :], ALU.add))
                    link(dve.tensor_tensor(sig[:, :, :], sig[:, :, :], oh[:, :, :], ALU.mult))
                    link(dve.tensor_reduce(den[:, 0, :], sig[:, :, :], AX, ALU.add))
                    link(dve.tensor_scalar(den[:, 1, :], den[:, 0, :], 1e-9, None, ALU.add))
                    link(dve.reciprocal(den[:, 2, :], den[:, 1, :]))
                else:
                    link(dve.tensor_scalar(den[:, 3, :], den[:, 0, :], 1e-9, None, ALU.is_gt))
                    link(dve.tensor_tensor(den[:, 2, :], den[:, 2, :], den[:, 3, :], ALU.mult))
                    link(dve.tensor_scalar(den[:, 4, :], den[:, 3, :], -0.5, 0.5, ALU.mult, ALU.add))
                    link(dve.tensor_tensor(sig[:, :, :], sig[:, :, :],
                                           den[:, 2, :].unsqueeze(2).to_broadcast([P, SEQS, E]), ALU.mult))
                    link(dve.tensor_tensor(oh[:, :, :], oh[:, :, :],
                                           den[:, 4, :].unsqueeze(2).to_broadcast([P, SEQS, E]), ALU.mult))
                    link(dve.tensor_tensor(sig[:, :, :], sig[:, :, :], oh[:, :, :], ALU.add))
                    dve.tensor_scalar(gates[:, :, :], sig[:, :, :], tg[:, 3:4], None, ALU.mult)\
                        .then_inc(gates_ready.by(0), 1)

            def turned_low(i, f, dst, first):
                for t in range(KT):
                    low(i, "x" + f, t, dst[1][:, t, :], ps[:, first + t, :], S_X, dst[0][:, t, :])

            def context_low(i):
                for t in range(KT):
                    low(i, "ct", t, CT[1][:, t, :], ps[:, G + t, :], S_W, CT[0][:, t, :])

            def group(i, following, fill):
                chain.group(i)
                if following:
                    prep.group(i + 1)
                attention(i, 0, following, fill)
                divide(i, 0, SEQS - 1)
                add_residual(i, 0, SEQS - 1)
                if fill:
                    add_sums(i - 1, 0)
                low(i, "k", 0, K1[1][:, 0, :], ps[:, 6, :], 1 / S_W, K1[0][:, 0, :])
                normalise(i, 1, x)
                low(i, "k", 1, K1[1][:, 1, :], ps[:, 7, :], 1 / S_W, K1[0][:, 1, :])
                turned_low(i, "b", XT, 2)
                if following:
                    query_low(i + 1, "qa", 0, 0, 0)
                top1_rows(i)
                if following:
                    query_low(i + 1, "qa", 0, 1, 1)
                    mask_bias(i + 1, 0)
                if fill:
                    gate_rows(i - 1, 2)
                for n in range(HT0):
                    dve.wait_ge(e_hi.sem, e_hi.at(i, n))
                    dve.scalar_tensor_tensor(out=PL[:, n, :], in0=P32[:, n, :], scalar=S_W, in1=PH[:, n, :],
                                             op0=ALU.mult, op1=ALU.subtract).then_inc(e_lo.by(n), 1)
                if fill:
                    add_sums(i - 1, 1)
                for m in range(2):
                    dve.wait_ge(e_sums.sem, e_sums.at(i, m))
                    both = range(2 * m, 2 * m + 2)
                    for s in both:
                        dve.scalar_tensor_tensor(out=x[:, s, :], in0=y(s, 0), scalar=tg[:, 1:2], in1=x[:, s, :],
                                                 op0=ALU.mult, op1=ALU.add).then_inc(resid.by(("b", s)), 1)
                    dve.wait_ge(resid.sem, resid.at(i, ("b", both[-1])))
                    measure(i, 2, both, x)
                carry_wait()
                aggregate(i, 2, range(SEQS))
                masked_keys(i, 1)
                normalise(i, 2, x)
                if fill:
                    step_low(i - 1, IN_BETWEEN[0])
                for m in range(2):
                    low(i, "v1", m, V[1][1][:, 32 * m:32 * m + 32, 0:HD],
                        ps[:, 2 + m, :].rearrange("p (h d) -> p h d", d=HD), 1 / S_W,
                        V[1][0][:, 32 * m:32 * m + 32, 0:HD])
                turned_low(i, "c", XT, 0)
                mask_bias(i, 1)
                for m in range(2):
                    query_low(i, "qc", 1, m, 2 + m)
                attention(i, 1, following, fill)
                divide(i, 1, SEQS - 1)
                if following:
                    maxima(i + 1, 0, 0)
                add_residual(i, 1, SEQS - 1)
                if following:
                    copy_maxima(i + 1, 0, 0)
                if fill:
                    add_sums(i - 1, E)
                if following:
                    normalise(i, 3, x)

            prep.group(0)
            dve.wait_ge(x_loaded.sem, x_loaded.at(0, "x"))
            measure(0, 0, range(SEQS), x_in)
            carry_wait()
            aggregate(0, 0, range(SEQS))
            masked_keys(0, 0)
            mask_bias(0, 0)
            low(0, "v0", 0, V[0][1][:, :, 0:HD], ctx_in[:, :, :].rearrange("p s (h d) -> p (s h) d", d=HD), S_W,
                V[0][0][:, :, 0:HD])
            normalise(0, 0, x_in, xn_a)
            context_low(0)
            for t in range(KT):
                query_low(0, "qa", 0, t, t)
            maxima(0, 0, 0)
            copy_maxima(0, 0, 0)
            group(0, True, False)
            with dve.Fori(1, groups - 1) as i:
                group(i, True, True)
            group(groups - 1, False, True)
            normalise(groups - 1, 3, x)
            turned_low(groups - 1, "d", XD, G)
            for part in range(3):
                gate_rows(groups - 1, part)
            for j in range(STEPS):
                if j < HTS:
                    swiglu_product(groups - 1, j)
                step_low(groups - 1, j)
                if j >= HTS - 1:
                    add_sums(groups - 1, j - HTS + 1)


def kernel(**inputs):
    import numpy as np
    import concourse.bacc as bacc
    from concourse.bass_utils import run_bass_kernel_spmd

    v = {k: np.asarray(t) for k, t in inputs.items()}
    arrays = {
        "x": v["x"], "ctx": v["ctx_1024"], "mask0": v["mask_Bx1xSxS2_ik1"], "mask1": v["mask_BxS2_ik0"],
        "mask1_keys": v["mask_BxS2_ik0"].T,
        "g": np.stack([np.stack([v["g_xattn"][l], v["g_ffn"][l]]) for l in range(2)]),
        "Wg": v["L0_ffn_Wg"].T, "ln_s": v["L0_ffn_ln_scale"].T, "ln_b": v["L0_ffn_ln_bias"].T,
        "W1": v["L0_ffn_W1"].transpose(1, 0, 2).reshape(D, HT0 * P),
        "b1": v["L0_ffn_b1"].reshape(HT0, P).T,
        "W2": v["L0_ffn_W2"].reshape(HT0 * P, D), "b2": v["L0_ffn_b2"],
        "q_w": v["L1_xattn_q_w"].T, "k_w": v["L1_xattn_k_w"].T, "v_w": v["L1_xattn_v_w"].T,
        "q_b": v["L1_xattn_q_b"], "k_b": v["L1_xattn_k_b"], "v_b": v["L1_xattn_v_b"],
        "router_w": v["L1_ffn_router_w"].T, "router_b": v["L1_ffn_router_bias"],
        "sw1": v["L1_ffn_sw1"], "sw3": v["L1_ffn_sw3"], "sw2": v["L1_ffn_sw2"],
        "ew1": v["L1_ffn_ew1"].transpose(1, 0, 2).reshape(D, HTR * P),
        "ew2": v["L1_ffn_ew2"].reshape(HTR * P, D),
    }
    nc = bacc.Bacc("TRN2", target_bir_lowering=False, num_devices=1)
    feeds, aps = {}, {}
    for name, t in arrays.items():
        t = np.ascontiguousarray(t)
        feeds[f"in_{name}"] = t
        aps[name] = nc.dram_tensor(f"in_{name}", t.shape, mybir.dt.from_np(t.dtype), kind="ExternalInput").ap()
    out = nc.dram_tensor("out", v["x"].shape, F32, kind="ExternalOutput").ap()
    build(nc, aps, out)
    r = run_bass_kernel_spmd(nc, [feeds], core_ids=[0])
    return r.results[0]["out"]
```
